# Optimizing a Trainium2 kernel written in Bass

```python
import numpy as np
import jax
import jax.numpy as jnp

def _softmax(x, axis=-1):
    return jax.nn.softmax(x, axis=axis)

def _gelu(x):
    return jax.nn.gelu(x, approximate=True)

def _silu(x):
    return jax.nn.silu(x)

def _sigmoid(x):
    return jax.nn.sigmoid(x)

def _layernorm(x, axis=-1, eps=1e-05):
    m = jnp.mean(x, axis=axis, keepdims=True)
    v = jnp.var(x, axis=axis, keepdims=True)
    return (x - m) / jnp.sqrt(v + eps)

def _scatter_add(tgt, idx, src, axis=0):
    return tgt.at[idx].add(src)

def _segment_sum(src, seg, n):
    return jax.ops.segment_sum(src, seg, n)
kernel_name = 'mk_xattn_ffn_d4_seqx_r8_f286a2'

def setup_inputs(seed: int=0):
    np.random.seed(seed)
    _w = jnp.asarray

    def _rec_inputs():
        import jax
        import jax.numpy as jnp
        _rk = jax.random.key(seed)
        x = -0.0009532 + 1.001 * jax.random.normal(jax.random.fold_in(_rk, 1), (8, 128, 512), jnp.float32)
        _lenS = 128 - jax.random.randint(jax.random.fold_in(_rk, 7), (8,), 0, max(1, 128 // 4) + 1, jnp.int32)
        _lenS2 = 128 - jax.random.randint(jax.random.fold_in(_rk, 8), (8,), 0, max(1, 128 // 4) + 1, jnp.int32)
        _ctx_4096P = jax.random.normal(jax.random.fold_in(_rk, 11), (8, 16, 512), jnp.float32)
        _ctx_4096c = jax.random.dirichlet(jax.random.fold_in(_rk, 511), 0.3 * jnp.ones((16,), jnp.float32), (8, 128))
        _ctx_4096t = jnp.einsum('bsk,bkd->bsd', _ctx_4096c, _ctx_4096P)
        _ctx_4096t = _ctx_4096t * jax.lax.rsqrt(jnp.mean(jnp.square(_ctx_4096t)) + 1e-12) * 0.953939
        ctx_4096 = -0.000394068 + 0.999852 * (_ctx_4096t + 0.3 * jax.random.normal(jax.random.fold_in(_rk, 611), (8, 128, 512), jnp.float32))
        pos_BxS2 = jnp.broadcast_to(jnp.arange(128, dtype=jnp.int32), (8, 128))
        _validS = jnp.arange(128)[None, :] < _lenS[:, None]
        _validS2 = jnp.arange(128)[None, :] < _lenS2[:, None]
        _causal = jnp.tril(jnp.ones((128, 128), dtype=bool))
        mask_BxSxS2_ik0 = jnp.where(jnp.broadcast_to(_validS2[:, None, :], (8, 128, 128)), 0, 1).astype(jnp.int32)
        return (x, ctx_4096, pos_BxS2, mask_BxSxS2_ik0)
    x, ctx_4096, pos_BxS2, mask_BxSxS2_ik0 = _rec_inputs()

    def _L0_xattn_setup():
        import jax, jax.numpy as jnp
        import numpy as np
        B, S, D = (2, 197, 512)
        HEADS = 16
        key = jax.random.key(seed)
        ks = jax.random.split(key, 9)
        inp = {'q': jax.random.normal(ks[0], (B, S, D), dtype=jnp.float32), 'v': jax.random.normal(ks[1], (B, S, D), dtype=jnp.float32), 'k': jax.random.normal(ks[2], (B, S, D), dtype=jnp.float32), 'Wq': jax.random.normal(ks[3], (D, D), dtype=jnp.float32) * 0.02, 'bq': jax.random.normal(ks[4], (D,), dtype=jnp.float32) * 0.02, 'Wk': jax.random.normal(ks[5], (D, D), dtype=jnp.float32) * 0.02, 'bk': jax.random.normal(ks[6], (D,), dtype=jnp.float32) * 0.02, 'Wv': jax.random.normal(ks[7], (D, D), dtype=jnp.float32) * 0.02, 'bv': jax.random.normal(ks[8], (D,), dtype=jnp.float32) * 0.02, 'head_num': HEADS}
        return inp
    _L0_xattn_all = _L0_xattn_setup()
    _L0_xattn_in = {k: v for k, v in _L0_xattn_all.items() if k in ('Wq', 'bq', 'Wk', 'bk', 'Wv', 'bv')}
    del _L0_xattn_all

    def _L0_ffn_setup():
        import jax, jax.numpy as jnp
        import numpy as np
        RANKS = (8, 16, 32, 64)
        TOPK = 1
        SCALING = 1.0 / 4
        key = jax.random.key(seed)
        ks = jax.random.split(key, 7)
        D_IN, D_OUT, MAX_R, N_RANKS = (512, 512, 64, len(RANKS))
        B_, S_ = (4, 256)
        return {'hidden_states': jax.random.normal(ks[0], (B_, S_, D_IN), jnp.float32), 'W': jax.random.normal(ks[1], (D_OUT, D_IN), jnp.float32) * 0.02, 'b': jax.random.normal(ks[2], (D_OUT,), jnp.float32) * 0.02, 'A': jax.random.normal(ks[3], (MAX_R, D_IN), jnp.float32) * 0.02, 'B': jnp.zeros((D_OUT, MAX_R), jnp.float32) + jax.random.normal(ks[4], (D_OUT, MAX_R), jnp.float32) * 0.02, 'gate_w': jax.random.normal(ks[5], (N_RANKS, D_IN), jnp.float32) * 0.02, 'gate_b': jax.random.normal(ks[6], (N_RANKS,), jnp.float32) * 0.02}
    _L0_ffn_all = _L0_ffn_setup()
    _L0_ffn_in = {k: v for k, v in _L0_ffn_all.items() if k in ('W', 'b', 'A', 'B', 'gate_w', 'gate_b')}
    del _L0_ffn_all

    def _L1_xattn_setup():
        import jax, jax.numpy as jnp
        import numpy as np
        B, S, E = (2, 256, 512)
        H, KVH, D = (32, 8, 128)
        GROUPS = H // KVH
        MAX_POS = 512
        ROPE_THETA = 10000.0

        def _rope_tables(max_pos, dim, theta):
            inv_freq = 1.0 / theta ** (jnp.arange(0, dim, 2, dtype=jnp.float32) / dim)
            t = jnp.arange(max_pos, dtype=jnp.float32)
            freqs = jnp.einsum('i,j->ij', t, inv_freq)
            emb = jnp.concatenate([freqs, freqs], axis=-1)
            return (jnp.cos(emb), jnp.sin(emb))

        def _rotate_half(x):
            x1, x2 = (x[..., :x.shape[-1] // 2], x[..., x.shape[-1] // 2:])
            return jnp.concatenate([-x2, x1], axis=-1)
        key = jax.random.key(seed)
        ks = jax.random.split(key, 8)
        scale_w = 1.0 / np.sqrt(E)
        query = jax.random.normal(ks[0], (B, S, E), dtype=jnp.float32)
        k_in = jax.random.normal(ks[1], (B, S, E), dtype=jnp.float32)
        v_in = jax.random.normal(ks[2], (B, S, E), dtype=jnp.float32)
        position_ids = jnp.broadcast_to(jnp.arange(S, dtype=jnp.int64), (B, S))
        src_mask = jnp.tril(jnp.ones((S, S), dtype=jnp.int32))
        src_mask = jnp.broadcast_to(src_mask, (B, S, S))
        Wq = jax.random.normal(ks[3], (E, H * D), dtype=jnp.float32) * scale_w
        Wk = jax.random.normal(ks[4], (E, KVH * D), dtype=jnp.float32) * scale_w
        Wv = jax.random.normal(ks[5], (E, KVH * D), dtype=jnp.float32) * scale_w
        Wo = jax.random.normal(ks[6], (H * D, E), dtype=jnp.float32) * scale_w
        return {'query': query, 'key': k_in, 'value': v_in, 'position_ids': position_ids, 'src_mask': src_mask, 'Wq': Wq, 'Wk': Wk, 'Wv': Wv, 'Wo': Wo}
    _L1_xattn_all = _L1_xattn_setup()
    _L1_xattn_in = {k: v for k, v in _L1_xattn_all.items() if k in ('Wq', 'Wk', 'Wv', 'Wo')}
    del _L1_xattn_all

    def _L1_ffn_setup():
        import jax, jax.numpy as jnp
        import numpy as np
        B, S, D = (4, 256, 512)
        NUM_EXPERTS, TOP_K = (3, 2)

        def _expert_outputs(h, w1, b1, w2, b2):
            pre = jnp.einsum('bsd,edf->ebsf', h, w1) + b1[:, None, None, :]
            act = jnp.stack([jnp.tanh(pre[0]), jax.nn.gelu(pre[1], approximate=False), jax.nn.silu(pre[2])])
            return jnp.einsum('ebsf,efd->ebsd', act, w2) + b2[:, None, None, :]
        key = jax.random.key(seed)
        ks = jax.random.split(key, 8)
        scale_in = 1.0 / np.sqrt(D)
        scale_gate = 1.0 / np.sqrt(D + 1)
        return {'h': jax.random.normal(ks[0], (B, S, D), dtype=jnp.float32), 'gate_w': jax.random.uniform(ks[1], (D + 1, NUM_EXPERTS), minval=-scale_gate, maxval=scale_gate, dtype=jnp.float32), 'gate_b': jnp.zeros((NUM_EXPERTS,), dtype=jnp.float32), 'w1': jax.random.uniform(ks[2], (NUM_EXPERTS, D, D), minval=-scale_in, maxval=scale_in, dtype=jnp.float32), 'b1': jnp.zeros((NUM_EXPERTS, D), dtype=jnp.float32), 'w2': jax.random.uniform(ks[3], (NUM_EXPERTS, D, D), minval=-scale_in, maxval=scale_in, dtype=jnp.float32), 'b2': jnp.zeros((NUM_EXPERTS, D), dtype=jnp.float32)}
    _L1_ffn_all = _L1_ffn_setup()
    _L1_ffn_in = {k: v for k, v in _L1_ffn_all.items() if k in ('gate_w', 'gate_b', 'w1', 'b1', 'w2', 'b2')}
    del _L1_ffn_all

    def _L2_xattn_setup():
        import jax, jax.numpy as jnp
        import numpy as np
        H = 8
        C = 2

        def _autocorrelation(Q, K, V):
            B, L, D = Q.shape
            d = D // H
            q = Q.reshape(B, L, H, d).transpose(0, 2, 1, 3)
            k = K.reshape(B, L, H, d).transpose(0, 2, 1, 3)
            v = V.reshape(B, L, H, d).transpose(0, 2, 1, 3)
            qf = jnp.fft.fft(q, axis=2)
            kf = jnp.fft.fft(k, axis=2)
            corr = jnp.fft.ifft(qf * jnp.conj(kf), axis=2).real
            topk = int(C * np.log(L))
            w, idx = jax.lax.top_k(corr.transpose(0, 1, 3, 2), topk)
            w = jax.nn.softmax(w, axis=-1)
            pos = jnp.arange(L)[:, None]
            out = jnp.zeros_like(v)
            for i in range(topk):
                g = jnp.minimum(idx[:, :, None, :, i] + pos, L - 1)
                out = out + w[:, :, None, :, i] * jnp.take_along_axis(v, g, axis=2)
            return out.transpose(0, 2, 1, 3).reshape(B, L, D)
        key = jax.random.key(seed)
        k1, k2, k3 = jax.random.split(key, 3)
        B, L, D = (16, 64, 512)
        Q = jax.random.normal(k1, (B, L, D), dtype=jnp.float32)
        K = jax.random.normal(k2, (B, L, D), dtype=jnp.float32)
        V = jax.random.normal(k3, (B, L, D), dtype=jnp.float32)
        return {'Q': Q, 'K': K, 'V': V}
    _L2_xattn_all = _L2_xattn_setup()
    _L2_xattn_in = {k: v for k, v in _L2_xattn_all.items() if k in ()}
    del _L2_xattn_all

    def _L2_ffn_setup():
        import jax, jax.numpy as jnp
        import numpy as np
        BLOCK = 128

        def _dequant(weight, scale_inv):
            O, I = weight.shape
            w = weight.reshape(O // BLOCK, BLOCK, I // BLOCK, BLOCK)
            w = w * scale_inv[:, None, :, None]
            return w.reshape(O, I)
        key = jax.random.key(seed)
        k_x, k_w, k_s, k_b = jax.random.split(key, 4)
        B, S, IN, OUT = (2, 256, 512, 512)
        x = jax.random.normal(k_x, (B, S, IN), dtype=jnp.float32)
        w = jax.random.normal(k_w, (OUT, IN), dtype=jnp.float32) * 0.02
        weight = w.astype(jnp.float8_e4m3fn).astype(jnp.float32)
        weight_scale_inv = jax.random.uniform(k_s, (OUT // BLOCK, IN // BLOCK), dtype=jnp.float32, minval=0.5, maxval=1.5)
        bias = jax.random.normal(k_b, (OUT,), dtype=jnp.float32) * 0.01
        return {'x': x, 'weight': weight, 'weight_scale_inv': weight_scale_inv, 'bias': bias}
    _L2_ffn_all = _L2_ffn_setup()
    _L2_ffn_in = {k: v for k, v in _L2_ffn_all.items() if k in ('weight', 'weight_scale_inv', 'bias')}
    del _L2_ffn_all

    def _L3_xattn_setup():
        import jax, jax.numpy as jnp
        import numpy as np
        B, D, N, H, K = (4, 128, 512, 16, 32)
        HD = D // H

        def _conv1x1(x, W, b):
            return jnp.einsum('od,bdn->bon', W, x) + b[None, :, None]
        key = jax.random.key(seed)
        ks = jax.random.split(key, 12)
        std_w = 1.0 / np.sqrt(D)
        std_p = 1.0 / np.sqrt(K)
        u = lambda k, shape, s: jax.random.uniform(k, shape, jnp.float32, -s, s)
        return {'query': jax.random.normal(ks[0], (B, D, N), jnp.float32), 'key': jax.random.normal(ks[1], (B, D, N), jnp.float32), 'value': jax.random.normal(ks[2], (B, D, N), jnp.float32), 'Wq': u(ks[3], (D, D), std_w), 'bq': u(ks[4], (D,), std_w), 'Wk': u(ks[5], (D, D), std_w), 'bk': u(ks[6], (D,), std_w), 'Wv': u(ks[7], (D, D), std_w), 'bv': u(ks[8], (D,), std_w), 'proj_k': u(ks[9], (N, K), std_p), 'proj_v': u(ks[10], (N, K), std_p), 'Wm': u(ks[11], (D, D), std_w), 'bm': u(jax.random.fold_in(key, 99), (D,), std_w)}
    _L3_xattn_all = _L3_xattn_setup()
    _L3_xattn_in = {k: v for k, v in _L3_xattn_all.items() if k in ('Wq', 'bq', 'Wk', 'bk', 'Wv', 'bv', 'proj_k', 'proj_v', 'Wm', 'bm')}
    del _L3_xattn_all

    def _L3_ffn_setup():
        import jax, jax.numpy as jnp
        import numpy as np
        GROUP_SIZE = 128

        def dequantize(qweight, qzeros, scales):
            shifts = jnp.arange(8, dtype=jnp.int32) * 4
            out_features = qweight.shape[1]
            q = qweight[:, None, :] >> shifts[None, :, None] & 15
            q = q.reshape(-1, out_features)
            z = qzeros[:, :, None] >> shifts[None, None, :] & 15
            z = z.reshape(qzeros.shape[0], -1)
            G = scales.shape[0]
            W = (q.reshape(G, GROUP_SIZE, out_features).astype(jnp.float16) - z[:, None, :].astype(jnp.float16)) * scales[:, None, :]
            return W.reshape(-1, out_features)
        key = jax.random.key(seed)
        k1, k2, k3, k4, k5 = jax.random.split(key, 5)
        B, S, IN, OUT, G = (4, 256, 512, 512, 512 // GROUP_SIZE)
        x = jax.random.normal(k1, (B, S, IN), dtype=jnp.float16)
        qweight = jax.random.randint(k2, (IN // 8, OUT), 0, 2147483647, dtype=jnp.int32)
        qzeros = jax.random.randint(k3, (G, OUT // 8), 0, 2147483647, dtype=jnp.int32)
        scales = (jax.random.uniform(k4, (G, OUT), dtype=jnp.float32) * 0.01 + 0.001).astype(jnp.float16)
        bias = (jax.random.normal(k5, (OUT,), dtype=jnp.float32) * 0.02).astype(jnp.float16)
        return {'x': x, 'qweight': qweight, 'qzeros': qzeros, 'scales': scales, 'bias': bias}
    _L3_ffn_all = _L3_ffn_setup()
    _L3_ffn_in = {k: v for k, v in _L3_ffn_all.items() if k in ('qweight', 'qzeros', 'scales', 'bias')}
    del _L3_ffn_all
    return {'x': x, 'ctx_4096': ctx_4096, 'pos_BxS2': pos_BxS2, 'mask_BxSxS2_ik0': mask_BxSxS2_ik0, 'L0_xattn_Wq': _L0_xattn_in['Wq'], 'L0_xattn_bq': _L0_xattn_in['bq'], 'L0_xattn_Wk': _L0_xattn_in['Wk'], 'L0_xattn_bk': _L0_xattn_in['bk'], 'L0_xattn_Wv': _L0_xattn_in['Wv'], 'L0_xattn_bv': _L0_xattn_in['bv'], 'L0_ffn_W': _L0_ffn_in['W'], 'L0_ffn_b': _L0_ffn_in['b'], 'L0_ffn_A': _L0_ffn_in['A'], 'L0_ffn_B': _L0_ffn_in['B'], 'L0_ffn_gate_w': _L0_ffn_in['gate_w'], 'L0_ffn_gate_b': _L0_ffn_in['gate_b'], 'L1_xattn_Wq': _L1_xattn_in['Wq'], 'L1_xattn_Wk': _L1_xattn_in['Wk'], 'L1_xattn_Wv': _L1_xattn_in['Wv'], 'L1_xattn_Wo': _L1_xattn_in['Wo'], 'L1_ffn_gate_w': _L1_ffn_in['gate_w'], 'L1_ffn_gate_b': _L1_ffn_in['gate_b'], 'L1_ffn_w1': _L1_ffn_in['w1'], 'L1_ffn_b1': _L1_ffn_in['b1'], 'L1_ffn_w2': _L1_ffn_in['w2'], 'L1_ffn_b2': _L1_ffn_in['b2'], 'L2_ffn_weight': _L2_ffn_in['weight'], 'L2_ffn_weight_scale_inv': _L2_ffn_in['weight_scale_inv'], 'L2_ffn_bias': _L2_ffn_in['bias'], 'L3_xattn_Wq': _L3_xattn_in['Wq'], 'L3_xattn_bq': _L3_xattn_in['bq'], 'L3_xattn_Wk': _L3_xattn_in['Wk'], 'L3_xattn_bk': _L3_xattn_in['bk'], 'L3_xattn_Wv': _L3_xattn_in['Wv'], 'L3_xattn_bv': _L3_xattn_in['bv'], 'L3_xattn_proj_k': _L3_xattn_in['proj_k'], 'L3_xattn_proj_v': _L3_xattn_in['proj_v'], 'L3_xattn_Wm': _L3_xattn_in['Wm'], 'L3_xattn_bm': _L3_xattn_in['bm'], 'L3_ffn_qweight': _L3_ffn_in['qweight'], 'L3_ffn_qzeros': _L3_ffn_in['qzeros'], 'L3_ffn_scales': _L3_ffn_in['scales'], 'L3_ffn_bias': _L3_ffn_in['bias']}

def reference(x, ctx_4096, pos_BxS2, mask_BxSxS2_ik0, L0_xattn_Wq, L0_xattn_bq, L0_xattn_Wk, L0_xattn_bk, L0_xattn_Wv, L0_xattn_bv, L0_ffn_W, L0_ffn_b, L0_ffn_A, L0_ffn_B, L0_ffn_gate_w, L0_ffn_gate_b, L1_xattn_Wq, L1_xattn_Wk, L1_xattn_Wv, L1_xattn_Wo, L1_ffn_gate_w, L1_ffn_gate_b, L1_ffn_w1, L1_ffn_b1, L1_ffn_w2, L1_ffn_b2, L2_ffn_weight, L2_ffn_weight_scale_inv, L2_ffn_bias, L3_xattn_Wq, L3_xattn_bq, L3_xattn_Wk, L3_xattn_bk, L3_xattn_Wv, L3_xattn_bv, L3_xattn_proj_k, L3_xattn_proj_v, L3_xattn_Wm, L3_xattn_bm, L3_ffn_qweight, L3_ffn_qzeros, L3_ffn_scales, L3_ffn_bias):
    import jax
    import jax.numpy as jnp

    def _L0_xattn_ref(q, v, k, Wq, bq, Wk, bk, Wv, bv, head_num):
        import jax, jax.numpy as jnp
        import numpy as np
        B, S, D = (2, 197, 512)
        HEADS = 16
        b, s, _ = q.shape
        hide = Wq.shape[0]
        hd = hide // head_num

        def proj(x, W, bias):
            y = x @ W.T + bias
            return y.reshape(b, s, head_num, hd).transpose(0, 2, 1, 3).reshape(b * head_num, s, hd)
        Q = proj(q, Wq, bq)
        K = proj(k, Wk, bk)
        V = proj(v, Wv, bv)
        scores = jnp.einsum('bqd,bkd->bqk', Q, K) / jnp.sqrt(jnp.asarray(hd, jnp.float32))
        attn = jax.nn.softmax(scores, axis=0)
        res = jnp.einsum('bqk,bkd->bqd', attn, V)
        out = res.reshape(b, head_num, s, hd).transpose(0, 2, 3, 1).reshape(b, s, hd * head_num)
        return out

    def _L0_ffn_ref(hidden_states, W, b, A, B, gate_w, gate_b):
        import jax, jax.numpy as jnp
        import numpy as np
        RANKS = (8, 16, 32, 64)
        TOPK = 1
        SCALING = 1.0 / 4
        bsz, seq, d_in = hidden_states.shape
        out = jnp.einsum('bsd,od->bso', hidden_states, W) + b
        x = hidden_states.reshape(-1, d_in)
        scores = x @ gate_w.T + gate_b
        probs = jax.nn.softmax(scores, axis=-1)
        routing_weights, selected = jax.lax.top_k(probs, TOPK)
        routing_weights = routing_weights / jnp.sum(routing_weights, axis=-1, keepdims=True)
        lora_outputs = jnp.stack([x @ A[:r, :].T @ B[:, :r].T for r in RANKS], axis=1)
        sel = jnp.take_along_axis(lora_outputs, selected[:, :, None], axis=1)
        final = jnp.sum(sel * routing_weights[:, :, None], axis=1)
        return out + final.reshape(bsz, seq, -1)

    def _L1_xattn_ref(query, key, value, position_ids, src_mask, Wq, Wk, Wv, Wo):
        import jax, jax.numpy as jnp
        import numpy as np
        B, S, E = (2, 256, 512)
        H, KVH, D = (32, 8, 128)
        GROUPS = H // KVH
        MAX_POS = 512
        ROPE_THETA = 10000.0

        def _rope_tables(max_pos, dim, theta):
            inv_freq = 1.0 / theta ** (jnp.arange(0, dim, 2, dtype=jnp.float32) / dim)
            t = jnp.arange(max_pos, dtype=jnp.float32)
            freqs = jnp.einsum('i,j->ij', t, inv_freq)
            emb = jnp.concatenate([freqs, freqs], axis=-1)
            return (jnp.cos(emb), jnp.sin(emb))

        def _rotate_half(x):
            x1, x2 = (x[..., :x.shape[-1] // 2], x[..., x.shape[-1] // 2:])
            return jnp.concatenate([-x2, x1], axis=-1)
        nb, q_len, _ = query.shape
        q = (query @ Wq).reshape(nb, q_len, H, D).transpose(0, 2, 1, 3)
        k = (key @ Wk).reshape(nb, q_len, KVH, D).transpose(0, 2, 1, 3)
        v = (value @ Wv).reshape(nb, q_len, KVH, D).transpose(0, 2, 1, 3)
        cos_t, sin_t = _rope_tables(MAX_POS, D, ROPE_THETA)
        cos = cos_t[position_ids][:, None]
        sin = sin_t[position_ids][:, None]
        q = q * cos + _rotate_half(q) * sin
        k = k * cos + _rotate_half(k) * sin
        k = jnp.repeat(k, GROUPS, axis=1)
        v = jnp.repeat(v, GROUPS, axis=1)
        scores = jnp.einsum('bhqd,bhkd->bhqk', q, k) / jnp.sqrt(jnp.float32(D))
        mask = src_mask[:, None]
        scores = jnp.where(mask == 0, jnp.float32(-1000000000.0), scores)
        attn = jax.nn.softmax(scores, axis=-1)
        x = jnp.einsum('bhqk,bhkd->bhqd', attn, v)
        x = x.transpose(0, 2, 1, 3).reshape(nb, q_len, H * D)
        return x @ Wo

    def _L1_ffn_ref(h, gate_w, gate_b, w1, b1, w2, b2):
        import jax, jax.numpy as jnp
        import numpy as np
        B, S, D = (4, 256, 512)
        NUM_EXPERTS, TOP_K = (3, 2)

        def _expert_outputs(h, w1, b1, w2, b2):
            pre = jnp.einsum('bsd,edf->ebsf', h, w1) + b1[:, None, None, :]
            act = jnp.stack([jnp.tanh(pre[0]), jax.nn.gelu(pre[1], approximate=False), jax.nn.silu(pre[2])])
            return jnp.einsum('ebsf,efd->ebsd', act, w2) + b2[:, None, None, :]
        b, s, d = h.shape
        vision_len = int(s * 0.3)
        text_strength = jnp.mean(jnp.abs(h[:, vision_len:, :]), axis=(1, 2), keepdims=True)
        vision_strength = jnp.mean(jnp.abs(h[:, :vision_len, :]), axis=(1, 2), keepdims=True)
        modality_ratio = text_strength / (vision_strength + 1e-08)
        modality_ratio = jnp.broadcast_to(modality_ratio, (b, s, 1))
        router_input = jnp.concatenate([h, modality_ratio], axis=-1)
        gate_logits = router_input @ gate_w + gate_b
        gate_scores = jax.nn.softmax(gate_logits, axis=-1)
        top_val, top_idx = jax.lax.top_k(gate_scores, TOP_K)
        top_val = top_val / (jnp.sum(top_val, axis=-1, keepdims=True) + 1e-08)
        expert_out = _expert_outputs(h, w1, b1, w2, b2)
        moe_out = jnp.zeros_like(h)
        batch_idx = jnp.arange(b)
        for i in range(TOP_K):
            j = top_idx[:, 0, i]
            out_i = expert_out[j, batch_idx]
            moe_out = moe_out + top_val[..., i:i + 1] * out_i
        return moe_out

    def _L2_xattn_ref(Q, K, V):
        import jax, jax.numpy as jnp
        import numpy as np
        H = 8
        C = 2

        def _autocorrelation(Q, K, V):
            B, L, D = Q.shape
            d = D // H
            q = Q.reshape(B, L, H, d).transpose(0, 2, 1, 3)
            k = K.reshape(B, L, H, d).transpose(0, 2, 1, 3)
            v = V.reshape(B, L, H, d).transpose(0, 2, 1, 3)
            qf = jnp.fft.fft(q, axis=2)
            kf = jnp.fft.fft(k, axis=2)
            corr = jnp.fft.ifft(qf * jnp.conj(kf), axis=2).real
            topk = int(C * np.log(L))
            w, idx = jax.lax.top_k(corr.transpose(0, 1, 3, 2), topk)
            w = jax.nn.softmax(w, axis=-1)
            pos = jnp.arange(L)[:, None]
            out = jnp.zeros_like(v)
            for i in range(topk):
                g = jnp.minimum(idx[:, :, None, :, i] + pos, L - 1)
                out = out + w[:, :, None, :, i] * jnp.take_along_axis(v, g, axis=2)
            return out.transpose(0, 2, 1, 3).reshape(B, L, D)
        return _autocorrelation(Q, K, V)

    def _L2_ffn_ref(x, weight, weight_scale_inv, bias):
        import jax, jax.numpy as jnp
        import numpy as np
        BLOCK = 128

        def _dequant(weight, scale_inv):
            O, I = weight.shape
            w = weight.reshape(O // BLOCK, BLOCK, I // BLOCK, BLOCK)
            w = w * scale_inv[:, None, :, None]
            return w.reshape(O, I)
        w_deq = _dequant(weight, weight_scale_inv)
        out = jnp.einsum('bsi,oi->bso', x, w_deq)
        return out + bias

    def _L3_xattn_ref(query, key, value, Wq, bq, Wk, bk, Wv, bv, proj_k, proj_v, Wm, bm):
        import jax, jax.numpy as jnp
        import numpy as np
        B, D, N, H, K = (4, 128, 512, 16, 32)
        HD = D // H

        def _conv1x1(x, W, b):
            return jnp.einsum('od,bdn->bon', W, x) + b[None, :, None]
        b = query.shape[0]
        q = _conv1x1(query, Wq, bq)
        k = _conv1x1(key, Wk, bk)
        v = _conv1x1(value, Wv, bv)
        k = jnp.einsum('bdn,nk->bdk', k, proj_k)
        v = jnp.einsum('bdn,nk->bdk', v, proj_v)
        q = q.reshape(b, HD, H, -1)
        k = k.reshape(b, HD, H, -1)
        v = v.reshape(b, HD, H, -1)
        scores = jnp.einsum('bdhn,bdhk->bhnk', q, k) / HD ** 0.5
        prob = jax.nn.softmax(scores, axis=-1)
        x = jnp.einsum('bhnk,bdhk->bdhn', prob, v)
        return _conv1x1(x.reshape(b, HD * H, -1), Wm, bm)

    def _L3_ffn_ref(x, qweight, qzeros, scales, bias):
        import jax, jax.numpy as jnp
        import numpy as np
        GROUP_SIZE = 128

        def dequantize(qweight, qzeros, scales):
            shifts = jnp.arange(8, dtype=jnp.int32) * 4
            out_features = qweight.shape[1]
            q = qweight[:, None, :] >> shifts[None, :, None] & 15
            q = q.reshape(-1, out_features)
            z = qzeros[:, :, None] >> shifts[None, None, :] & 15
            z = z.reshape(qzeros.shape[0], -1)
            G = scales.shape[0]
            W = (q.reshape(G, GROUP_SIZE, out_features).astype(jnp.float16) - z[:, None, :].astype(jnp.float16)) * scales[:, None, :]
            return W.reshape(-1, out_features)
        W = dequantize(qweight, qzeros, scales)
        out = jnp.einsum('bsi,io->bso', x.astype(jnp.float16), W)
        return out + bias
    x = x + _L0_xattn_ref(_layernorm(x, axis=-1), ctx_4096, ctx_4096, L0_xattn_Wq, L0_xattn_bq, L0_xattn_Wk, L0_xattn_bk, L0_xattn_Wv, L0_xattn_bv, 16)
    x = x + _L0_ffn_ref(_layernorm(x, axis=-1), L0_ffn_W, L0_ffn_b, L0_ffn_A, L0_ffn_B, L0_ffn_gate_w, L0_ffn_gate_b)
    x = x + _L1_xattn_ref(_layernorm(x, axis=-1), ctx_4096, ctx_4096, pos_BxS2, mask_BxSxS2_ik0, L1_xattn_Wq, L1_xattn_Wk, L1_xattn_Wv, L1_xattn_Wo)
    x = x + _L1_ffn_ref(_layernorm(x, axis=-1), L1_ffn_gate_w, L1_ffn_gate_b, L1_ffn_w1, L1_ffn_b1, L1_ffn_w2, L1_ffn_b2)
    x = x + _L2_xattn_ref(_layernorm(x, axis=-1), ctx_4096, ctx_4096)
    x = x + _L2_ffn_ref(_layernorm(x, axis=-1), L2_ffn_weight, L2_ffn_weight_scale_inv, L2_ffn_bias)
    x = x + _L3_xattn_ref(_layernorm(x, axis=-1), ctx_4096, ctx_4096, L3_xattn_Wq, L3_xattn_bq, L3_xattn_Wk, L3_xattn_bk, L3_xattn_Wv, L3_xattn_bv, L3_xattn_proj_k, L3_xattn_proj_v, L3_xattn_Wm, L3_xattn_bm)
    x = x + _L3_ffn_ref(_layernorm(x, axis=-1), L3_ffn_qweight, L3_ffn_qzeros, L3_ffn_scales, L3_ffn_bias)
    return x

_drawn_inputs = setup_inputs


def setup_inputs(seed=0):
    import zlib

    import numpy as np

    out = dict(_drawn_inputs(seed))
    spreads = {'L1_ffn_gate_b': (0.0, 0.8), 'L1_ffn_b1': (0.0, 0.663), 'L1_ffn_b2': (0.0, 0.1)}
    factors = {'L0_xattn_bq': 51.159,
     'L0_xattn_bk': 28.682,
     'L0_xattn_bv': 4.459,
     'L0_ffn_b': 4.979,
     'L0_ffn_gate_b': 36.091,
     'L2_ffn_bias': 8.0,
     'L3_xattn_bq': 8.0,
     'L3_xattn_bk': 8.0,
     'L3_xattn_bv': 8.0,
     'L3_xattn_bm': 2.966,
     'L3_ffn_bias': 7.479}
    for name, (base, spread) in spreads.items():
        noise = np.random.default_rng([zlib.crc32(name.encode()), seed]).standard_normal(out[name].shape)
        drawn = base * np.exp(spread * noise) if base else spread * noise
        out[name] = jnp.asarray(drawn.astype(out[name].dtype))
    for name, factor in factors.items():
        out[name] = (out[name] * factor).astype(out[name].dtype)
    return out
```

```python
import numpy as np

import concourse.bass as bass
from concourse import mybir
from contextlib import ExitStack

F32 = mybir.dt.float32
F16 = mybir.dt.float16
I32 = mybir.dt.int32
ALU = mybir.AluOpType
ACT = mybir.ActivationFunctionType
AX = mybir.AxisListType

P = 128
NB = 8
D = 512
C = D // P
TOK = NB * P
EPS = 1e-5
LOWEST = -3.0e38


class Link:

    def __init__(self, eng, sem, n=0):
        self.eng, self.sem, self.n = eng, sem, n

    def __call__(self, ins):
        self.n += 1
        ins.then_inc(self.sem, 1)
        self.eng.wait_ge(self.sem, self.n)


class Core:

    def __init__(self, nc, ctx, dram):
        self.nc, self.ctx, self.dram = nc, ctx, dram
        self.x = self.sb(ctx, "x", [P, NB, D])
        self.ctxT = self.sb(ctx, "ctxT", [P, C, TOK])
        self.ident = self.sb(ctx, "ident", [P, P])
        self.xn = self.sb(ctx, "xn", [P, 2, D])
        self.stats = self.sb(ctx, "stats", [P, NB, 6])
        self.meanvar = self.sb(ctx, "meanvar", [P, NB, 2])
        self.varpe = self.sb(ctx, "varpe", [P, NB])
        self.rstd = self.sb(ctx, "rstd", [P, NB])
        self.mhalf = self.sb(ctx, "mhalf", [P, 1])
        self.ps = ctx.enter_context(nc.psum_tensor("ps", [P, 8, 512], F32))
        self.var_ready = self.sem("var_ready")
        self.rstd_ready = self.sem("rstd_ready")
        self.dve_own = self.sem("dve_own")
        self.pool_own = self.sem("pool_own")
        self.loaded = {}
        self.dve_count = 0
        self.pool_count = 0

    def sb(self, ctx, name, shape, dt=F32):
        return ctx.enter_context(self.nc.sbuf_tensor(name, shape, dt))

    def sem(self, name):
        return self.ctx.enter_context(self.nc.semaphore(name))

    def load(self, eng, name, dst, src):
        if name not in self.loaded:
            self.loaded[name] = [self.sem(f"{name}_loaded"), 0]
        sem, _ = self.loaded[name]
        eng.dma_start(dst, src).then_inc(sem, 16)
        self.loaded[name][1] += 16

    def arrived(self, eng, name):
        eng.wait_ge(*self.loaded[name])

    def row_stats(self, dve, link, b):
        link(self.nc.vector.bn_stats(self.stats[:, b, :], self.x[:, b, :]))
        self.nc.vector.bn_aggr(self.meanvar[:, b, :], self.stats[:, b, :]).then_inc(self.var_ready, 1)

    def row_rstd(self, pool, link, layer, b):
        pool.wait_ge(self.var_ready, NB * layer + b + 1)
        link(self.nc.gpsimd.tensor_scalar(self.varpe[:, b:b + 1], self.meanvar[:, b, 1:2], EPS, None, ALU.add))
        self.nc.gpsimd.tensor_tensor(self.rstd[:, b:b + 1], self.varpe[:, b:b + 1], self.mhalf[:, :],
                                     ALU.pow).then_inc(self.rstd_ready, 1)

    def normed(self, dve, layer, b, out, row=None):
        dve.wait_ge(self.rstd_ready, NB * layer + b + 1)
        return self.nc.vector.tensor_scalar(out, self.x[:, b, :] if row is None else row, self.meanvar[:, b, 0:1],
                                            self.rstd[:, b:b + 1], ALU.subtract, ALU.mult)

    def transpose4(self, bank, src):
        for c in range(C):
            last = self.nc.tensor.transpose(self.ps[:, bank, c * P:(c + 1) * P], src[:, c * P:(c + 1) * P],
                                            self.ident[:, :])
        return last


def row_block(ap):
    return ap.rearrange("(c p) n -> p c n", p=P)


def cross_attention_over_heads(k, x_dram, ctxT_dram, w, out=None):
    nc = k.nc
    H, HD = 16, 32
    R = P // HD
    scale = 1.0 / float(np.sqrt(HD))
    with ExitStack() as ctx:
        wq = k.sb(ctx, "a0_wq", [P, C, D])
        wk = k.sb(ctx, "a0_wk", [P, C, D])
        wv = k.sb(ctx, "a0_wv", [P, C, D])
        bqk = k.sb(ctx, "a0_bqk", [P, 2, C])
        bv = k.sb(ctx, "a0_bv", [P, D])
        xT = k.sb(ctx, "a0_xT", [P, C, TOK])
        qT = k.sb(ctx, "a0_qT", [P, C, TOK])
        kT = k.sb(ctx, "a0_kT", [P, C, TOK])
        v = k.sb(ctx, "a0_v", [P, NB, D])
        E = k.sb(ctx, "a0_E", [P, NB, R, C, P])
        rowmax = k.sb(ctx, "a0_rowmax", [P, NB, P])
        allmax = k.sb(ctx, "a0_allmax", [P, P])
        total = k.sb(ctx, "a0_total", [P, P])
        inv = k.sb(ctx, "a0_inv", [P, P])
        S = {n: k.sem("a0_" + n) for n in (
            "xn_ready", "xt_ready", "xt_copied", "kq_ready", "kq_copied", "v_ready",
            "v_copied", "scores_ready", "scores_copied", "shifted", "exp_ready", "sum_ready", "probs_ready",
            "out_ready", "added")}
        block = ctx.enter_context(nc.Block())
        ps = k.ps

        @block.sync
        def _(sp):
            k.load(sp, "a0_k", k.ident[:, :], k.dram["ident"])
            for b in range(NB):
                k.load(sp, f"x{b}", k.x[:, b, :], x_dram[b])
                if b == 1:
                    k.load(sp, "a0_k", wk[:, :, :], w["Wk"])
                    k.load(sp, "a0_k", bqk[:, :, :], w["bqk"])
                    for half in range(2):
                        k.load(sp, f"ctxT{half}", k.ctxT[:, :, half * 512:(half + 1) * 512], ctxT_dram[half])
            k.load(sp, "a0_v", wv[:, :, :], w["Wv"])
            k.load(sp, "a0_v", bv[:, :], w["bv"].partition_broadcast(P))
            k.load(sp, "a0_wq", wq[:, :, :], w["Wq"])

        @block.gpsimd
        def _(pool):
            link = Link(pool, k.pool_own)
            link(nc.gpsimd.memset(k.mhalf[:, :], -0.5))
            for b in range(NB):
                k.row_rstd(pool, link, 0, b)
            for b in range(NB):
                k.row_rstd(pool, link, 1, b)
            k.pool_count = link.n

        @block.tensor
        def _(pe):
            def project(u, bank, weight, acts, o, half):
                if u >= 2:
                    pe.wait_ge(S["kq_copied"], u - 1)
                for c in range(C):
                    last = nc.tensor.matmul(ps[:, bank, :], weight[:, c, o * P:(o + 1) * P],
                                            acts[:, c, half * 512:(half + 1) * 512], start=c == 0, stop=c == C - 1)
                last.then_inc(S["kq_ready"], 1)

            k.arrived(pe, "a0_k")
            u = 0
            for half in range(2):
                k.arrived(pe, f"ctxT{half}")
                for o in range(C):
                    project(u, u % 2, wk, k.ctxT, o, half)
                    u += 1
            k.arrived(pe, "a0_k")
            for b in range(NB):
                pe.wait_ge(S["xn_ready"], b + 1)
                if b >= 2:
                    pe.wait_ge(S["xt_copied"], b - 1)
                k.transpose4(4 + b % 2, k.xn[:, b % 2, :]).then_inc(S["xt_ready"], 1)
            k.arrived(pe, "a0_v")
            for b in range(NB):
                if b >= 2:
                    pe.wait_ge(S["v_copied"], b - 1)
                for c in range(C):
                    last = nc.tensor.matmul(ps[:, 2 + b % 2, :], k.ctxT[:, c, b * P:(b + 1) * P], wv[:, c, :],
                                            start=c == 0, stop=c == C - 1)
                last.then_inc(S["v_ready"], 1)
            k.arrived(pe, "a0_wq")
            for half in range(2):
                pe.wait_ge(S["xt_copied"], 4 * half + 4)
                for o in range(C):
                    project(u, u % 2, wq, xT, o, half)
                    u += 1
            pe.wait_ge(S["kq_copied"], 16)
            pe.wait_ge(S["v_copied"], NB)
            for b in range(NB):
                if b >= 2:
                    pe.wait_ge(S["scores_copied"], b - 1)
                for c in range(C):
                    for r in range(R):
                        last = nc.tensor.matmul(ps[:, 4 * (b % 2) + r, c * P:(c + 1) * P],
                                                kT[HD * r:HD * (r + 1), c, b * P:(b + 1) * P],
                                                qT[HD * r:HD * (r + 1), c, b * P:(b + 1) * P],
                                                start=True, stop=True)
                last.then_inc(S["scores_ready"], 1)
            pe.wait_ge(S["scores_copied"], NB)
            for b in range(NB):
                pe.wait_ge(S["exp_ready"], b + 1)
                for r in range(R):
                    last = nc.tensor.matmul(ps[:, 0, :], k.ident[:, :], E[:, b, r, :, :].rearrange("p c q -> p (c q)"),
                                            start=b == 0 and r == 0, stop=b == NB - 1 and r == R - 1)
            last.then_inc(S["sum_ready"], 1)
            for b in range(NB):
                pe.wait_ge(S["probs_ready"], b + 1)
                if b >= 2:
                    pe.wait_ge(S["added"], b - 1)
                o = ps[:, 2 + b % 2, :].rearrange("p (d h) -> p h d", h=H)
                for c in range(C):
                    for r in range(R):
                        h = R * c + r
                        last = nc.tensor.matmul(o[:, h, :], E[:, b, r, c, :], v[:, b, h * HD:(h + 1) * HD],
                                                start=True, stop=True)
                last.then_inc(S["out_ready"], 1)

        @block.scalar
        def _(act):
            def copy_kq(u, dst, which, o, half):
                act.wait_ge(S["kq_ready"], u + 1)
                nc.scalar.activation(dst[:, o, half * 512:(half + 1) * 512], ps[:, u % 2, :], ACT.Identity,
                                     bias=bqk[:, which, o:o + 1]).then_inc(S["kq_copied"], 1)

            k.arrived(act, "a0_k")
            for u in range(8):
                copy_kq(u, kT, 1, u % C, u // C)
            for b in range(NB):
                act.wait_ge(S["xt_ready"], b + 1)
                nc.scalar.copy(xT[:, :, b * P:(b + 1) * P],
                               ps[:, 4 + b % 2, :].rearrange("p (c t) -> p c t", c=C)).then_inc(S["xt_copied"], 1)
            for u in range(8):
                copy_kq(8 + u, qT, 0, u % C, u // C)
            for b in range(NB):
                act.wait_ge(S["scores_ready"], b + 1)
                nc.scalar.copy(E[:, b, :, :, :].rearrange("p r c q -> p (r c q)"),
                               ps[:, 4 * (b % 2):4 * (b % 2) + 4, :].rearrange("p r n -> p (r n)"))\
                  .then_inc(S["scores_copied"], 1)
            for b in range(NB):
                act.wait_ge(S["shifted"], b + 1)
                e = E[:, b, :, :, :].rearrange("p r c q -> p (r c q)")
                nc.scalar.activation(e, e, ACT.Exp, scale=scale).then_inc(S["exp_ready"], 1)

        @block.vector
        def _(dve):
            link = Link(dve, k.dve_own)
            for b in range(NB):
                k.arrived(dve, f"x{b}")
                k.row_stats(dve, link, b)
                if b >= 1:
                    if b >= 3:
                        dve.wait_ge(S["xt_ready"], b - 2)
                    k.normed(dve, 0, b - 1, k.xn[:, (b - 1) % 2, :]).then_inc(S["xn_ready"], 1)
            dve.wait_ge(S["xt_ready"], NB - 2)
            k.normed(dve, 0, NB - 1, k.xn[:, (NB - 1) % 2, :]).then_inc(S["xn_ready"], 1)
            k.arrived(dve, "a0_v")
            for b in range(NB):
                dve.wait_ge(S["v_ready"], b + 1)
                nc.vector.tensor_tensor(v[:, b, :], ps[:, 2 + b % 2, :], bv[:, :], ALU.add).then_inc(S["v_copied"], 1)
            for b in range(NB):
                dve.wait_ge(S["scores_copied"], b + 1)
                nc.vector.tensor_reduce(rowmax[:, b, :], E[:, b, :, :, :].rearrange("p r c q -> p q (r c)"),
                                        AX.X, ALU.max).then_inc(k.dve_own, 1)
                link.n += 1
            dve.wait_ge(k.dve_own, link.n)
            link(nc.vector.tensor_reduce(allmax[:, :], rowmax[:, :, :].rearrange("p b q -> p q b"), AX.X, ALU.max))
            heads = [P, R * C, P]
            for b in range(NB):
                e = E[:, b, :, :, :].rearrange("p r c q -> p (r c) q")
                nc.vector.tensor_tensor(e, e, allmax[:, :].unsqueeze(1).to_broadcast(heads), ALU.subtract)\
                  .then_inc(S["shifted"], 1)
            dve.wait_ge(S["sum_ready"], 1)
            link(nc.vector.tensor_reduce(total[:, :], ps[:, 0, :].rearrange("p (c q) -> p q c", c=C), AX.X, ALU.add))
            link(nc.vector.reciprocal(inv[:, :], total[:, :]))

            def divide(b):
                e = E[:, b, :, :, :].rearrange("p r c q -> p (r c) q")
                nc.vector.tensor_tensor(e, e, inv[:, :].unsqueeze(1).to_broadcast(heads), ALU.mult)\
                  .then_inc(S["probs_ready"], 1)

            divide(0)
            for b in range(NB):
                if b + 1 < NB:
                    divide(b + 1)
                dve.wait_ge(S["out_ready"], b + 1)
                nc.vector.tensor_tensor(k.x[:, b, :], k.x[:, b, :], ps[:, 2 + b % 2, :], ALU.add)\
                  .then_inc(S["added"], 1)
                dve.wait_ge(S["added"], b + 1)
                k.row_stats(dve, link, b)
            k.dve_count = link.n


def ranked_lora(k, w):
    nc, ps = k.nc, k.ps
    RANKS = (8, 16, 32, 64)
    NR, MAXR = len(RANKS), RANKS[-1]
    with ExitStack() as ctx:
        wt = k.sb(ctx, "f0_w", [P, C, D])
        ag = k.sb(ctx, "f0_ag", [P, C, MAXR + NR])
        bt = k.sb(ctx, "f0_bt", [MAXR, D])
        bias = k.sb(ctx, "f0_bias", [P, D])
        gate_b = k.sb(ctx, "f0_gate_b", [P, NR])
        xT = k.sb(ctx, "f0_xT", [P, NB, C, P])
        low = k.sb(ctx, "f0_low", [P, NB, MAXR + NR])
        gated = k.sb(ctx, "f0_gated", [P, NB, MAXR])
        scores = k.sb(ctx, "f0_scores", [P, NB, NR])
        before = k.sb(ctx, "f0_before", [P, NB, NR])
        after = k.sb(ctx, "f0_after", [P, NB, NR])
        keep = k.sb(ctx, "f0_keep", [P, NB, NR])
        gatedT = k.sb(ctx, "f0_gatedT", [MAXR, 2, P])
        S = {n: k.sem("f0_" + n) for n in (
            "xn_ready", "xt_ready", "xt_copied", "low_ready", "low_copied", "biased", "gated", "gt_ready",
            "gt_copied", "out_ready", "added")}
        block = ctx.enter_context(nc.Block())

        @block.sync
        def _(sp):
            k.load(sp, "f0_low", ag[:, :, :], w["AG"])
            k.load(sp, "f0_low", gate_b[:, :], w["gate_b"].partition_broadcast(P))
            k.load(sp, "f0_w", wt[:, :, :], w["W"])
            k.load(sp, "f0_out", bt[:, :], w["B"])
            k.load(sp, "f0_out", bias[:, :], w["b"].partition_broadcast(P))

        @block.gpsimd
        def _(pool):
            link = Link(pool, k.pool_own, k.pool_count)
            k.arrived(pool, "f0_out")
            for b in range(NB):
                pool.wait_ge(S["xn_ready"], b + 1)
                nc.gpsimd.tensor_tensor(k.x[:, b, :], k.x[:, b, :], bias[:, :], ALU.add).then_inc(S["biased"], 1)
            for b in range(NB):
                k.row_rstd(pool, link, 2, b)
            k.pool_count = link.n

        @block.tensor
        def _(pe):
            def low_rank(b):
                pe.wait_ge(S["xt_copied"], b + 1)
                if b >= 2:
                    pe.wait_ge(S["low_copied"], b - 1)
                for c in range(C):
                    last = nc.tensor.matmul(ps[:, b % 2, 0:MAXR + NR], xT[:, b, c, :], ag[:, c, :],
                                            start=c == 0, stop=c == C - 1)
                last.then_inc(S["low_ready"], 1)

            for b in range(NB):
                pe.wait_ge(S["xn_ready"], b + 1)
                if b >= 2:
                    pe.wait_ge(S["xt_copied"], b - 1)
                k.transpose4(6 + b % 2, k.xn[:, b % 2, :]).then_inc(S["xt_ready"], 1)
                if b == 0:
                    k.arrived(pe, "f0_low")
                else:
                    low_rank(b - 1)
            low_rank(NB - 1)
            k.arrived(pe, "f0_w")
            for i in range(NB + 2):
                if i < NB:
                    if i >= 4:
                        pe.wait_ge(S["added"], i - 3)
                    for c in range(C):
                        nc.tensor.matmul(ps[:, 2 + i % 4, :], xT[:, i, c, :], wt[:, c, :], start=c == 0, stop=False)
                if 1 <= i <= NB:
                    b = i - 1
                    if b == 0:
                        pe.wait_ge(S["gated"], NR)
                    if b >= 2:
                        pe.wait_ge(S["gt_copied"], b - 1)
                    nc.tensor.transpose(ps[0:MAXR, 6 + b % 2, 0:P], gated[:, b, :], k.ident[:, :])\
                      .then_inc(S["gt_ready"], 1)
                if i >= 2:
                    b = i - 2
                    if b == 0:
                        k.arrived(pe, "f0_out")
                    pe.wait_ge(S["gt_copied"], b + 1)
                    nc.tensor.matmul(ps[:, 2 + b % 4, :], gatedT[:, b % 2, :], bt[:, :], start=False, stop=True)\
                      .then_inc(S["out_ready"], 1)

        @block.scalar
        def _(act):
            for b in range(NB):
                act.wait_ge(S["xt_ready"], b + 1)
                nc.scalar.copy(xT[:, b, :, :].rearrange("p c t -> p (c t)"), ps[:, 6 + b % 2, :])\
                  .then_inc(S["xt_copied"], 1)
                if b >= 1:
                    act.wait_ge(S["low_ready"], b)
                    nc.scalar.copy(low[:, b - 1, :], ps[:, (b - 1) % 2, 0:MAXR + NR]).then_inc(S["low_copied"], 1)
            act.wait_ge(S["low_ready"], NB)
            nc.scalar.copy(low[:, NB - 1, :], ps[:, (NB - 1) % 2, 0:MAXR + NR]).then_inc(S["low_copied"], 1)
            for b in range(NB):
                act.wait_ge(S["gt_ready"], b + 1)
                if b >= 2:
                    act.wait_ge(S["out_ready"], b - 1)
                nc.scalar.copy(gatedT[:, b % 2, :], ps[0:MAXR, 6 + b % 2, 0:P]).then_inc(S["gt_copied"], 1)

        @block.vector
        def _(dve):
            link = Link(dve, k.dve_own, k.dve_count)
            for b in range(NB):
                if b >= 2:
                    dve.wait_ge(S["xt_ready"], b - 1)
                k.normed(dve, 1, b, k.xn[:, b % 2, :]).then_inc(S["xn_ready"], 1)
            k.arrived(dve, "f0_low")
            dve.wait_ge(S["low_copied"], NB)
            link(nc.vector.tensor_tensor(scores[:, :, :], low[:, :, MAXR:MAXR + NR],
                                         gate_b[:, :].unsqueeze(1).to_broadcast([P, NB, NR]), ALU.add))
            link(nc.vector.tensor_copy(before[:, :, 1:2], scores[:, :, 0:1]))
            link(nc.vector.tensor_copy(after[:, :, NR - 1:NR], scores[:, :, NR - 1:NR]))
            for t in range(2, NR):
                link(nc.vector.tensor_tensor(before[:, :, t:t + 1], before[:, :, t - 1:t], scores[:, :, t - 1:t],
                                             ALU.max))
            for t in range(NR - 2, 0, -1):
                link(nc.vector.tensor_tensor(after[:, :, t:t + 1], after[:, :, t + 1:t + 2], scores[:, :, t:t + 1],
                                             ALU.max))
            link(nc.vector.tensor_tensor(keep[:, :, 1:NR], before[:, :, 1:NR], after[:, :, 1:NR], ALU.is_lt))
            nc.vector.tensor_copy(gated[:, :, 0:RANKS[0]], low[:, :, 0:RANKS[0]]).then_inc(S["gated"], 1)
            for t in range(1, NR):
                lo, hi = RANKS[t - 1], RANKS[t]
                nc.vector.tensor_tensor(gated[:, :, lo:hi], low[:, :, lo:hi],
                                        keep[:, :, t:t + 1].to_broadcast([P, NB, hi - lo]), ALU.mult)\
                  .then_inc(S["gated"], 1)
            for b in range(NB):
                dve.wait_ge(S["out_ready"], b + 1)
                dve.wait_ge(S["biased"], b + 1)
                nc.vector.tensor_tensor(k.x[:, b, :], k.x[:, b, :], ps[:, 2 + b % 4, :], ALU.add)\
                  .then_inc(S["added"], 1)
                dve.wait_ge(S["added"], b + 1)
                k.row_stats(dve, link, b)
            k.dve_count = link.n


def after_first(eng, sem, value):
    if isinstance(value, int) and value <= 0:
        return
    eng.wait_ge(sem, value)


def grouped_attention(k, dram):
    nc, ps = k.nc, k.ps
    G, R, HD = 8, 4, P
    HALF = TOK // 2
    scale = 1.0 / float(np.sqrt(HD))
    MAXPOS = dram["a1_rope"].shape[1] * P
    QK_BANK, V_BANK, S_BANK, PT_BANK, OT_BANK, Y_BANK = 0, 2, 3, 4, 5, 6
    with ExitStack() as ctx:
        pos_i = k.sb(ctx, "a1_pos_i", [P, TOK], I32)
        pos = k.sb(ctx, "a1_pos", [P, TOK])
        wrap = k.sb(ctx, "a1_wrap", [P, TOK])
        onehot = k.sb(ctx, "a1_onehot", [P, MAXPOS // P, TOK])
        iota = k.sb(ctx, "a1_iota", [P, MAXPOS // P])
        rope = k.sb(ctx, "a1_rope", [P, MAXPOS // P, 2 * P])
        cos = k.sb(ctx, "a1_cos", [P, TOK])
        sin = k.sb(ctx, "a1_sin", [P, TOK])
        mask = k.sb(ctx, "a1_mask", [P, NB, P], I32)
        hidden = k.sb(ctx, "a1_hidden", [P, NB, P], I32)
        fill = k.sb(ctx, "a1_fill", [P, P])
        gate = k.sb(ctx, "a1_gate", [P, 1])
        wq = k.sb(ctx, "a1_wq", [P, R, C, HD])
        wk = k.sb(ctx, "a1_wk", [P, C, HD])
        wv = k.sb(ctx, "a1_wv", [P, G, C, HD])
        wo = k.sb(ctx, "a1_wo", [P, 2, R, D])
        xT = k.sb(ctx, "a1_xT", [P, C, TOK])
        qT = k.sb(ctx, "a1_qT", [P, R, TOK])
        kT = k.sb(ctx, "a1_kT", [P, TOK])
        v = k.sb(ctx, "a1_v", [P, NB, HD])
        turned = k.sb(ctx, "a1_turned", [P, 2, 2, HALF])
        negmax = k.sb(ctx, "a1_negmax", [P, 2, R])
        bias = k.sb(ctx, "a1_bias", [P, 2, R])
        total = k.sb(ctx, "a1_total", [P, 2, R])
        inv = k.sb(ctx, "a1_inv", [P, 2, R])
        prob = k.sb(ctx, "a1_prob", [P, 2, R, P])
        probT = k.sb(ctx, "a1_probT", [P, 2, R * P])
        oT = k.sb(ctx, "a1_oT", [P, 2, R * P])
        S = {n: k.sem("a1_" + n) for n in (
            "onehot_ready", "table_ready", "table_copied", "xn_ready", "xt_ready", "xt_copied", "qk_ready",
            "turned", "rotated", "v_ready", "v_copied", "s_ready", "bias_ready", "exp_ready", "prob_ready",
            "pt_ready", "pt_copied", "ot_ready", "ot_copied", "y_ready", "y_added", "wk_loaded", "wo_loaded")}
        wq_loaded = [k.sem(f"a1_wq{h}_loaded") for h in range(R)]
        block = ctx.enter_context(nc.Block())

        def rotation(half, h):
            return 5 * half + 1 + h

        @block.sync
        def _(sp):
            k.load(sp, "a1_tables", pos_i[:, :], dram["pos"].partition_broadcast(P))
            k.load(sp, "a1_tables", iota[:, :], dram["a1_iota"])
            k.load(sp, "a1_tables", rope[:, :, :], dram["a1_rope"])
            k.load(sp, "a1_mask", mask[:, :, :], dram["mask"])

            def load_wk(g):
                sp.dma_start(wk[:, :, :], dram["a1_wk"][g]).then_inc(S["wk_loaded"], 16)

            def load_wq(g, h):
                sp.dma_start(wq[:, h, :, :], dram["a1_wq"][g, h]).then_inc(wq_loaded[h], 16)

            def load_wo(g, slot):
                sp.dma_start(wo[:, slot, :, :], dram["a1_wo"][g]).then_inc(S["wo_loaded"], 16)

            load_wk(0)
            for h in range(R):
                load_wq(0, h)
            k.load(sp, "a1_wv", wv[:, :, :, :], dram["a1_wv"])
            load_wo(0, 0)

            def loads_in(g):
                after_first(sp, S["y_ready"], 8 * g)
                sp.wait_ge(S["wo_loaded"], 16 * (g + 1))
                load_wo(g + 1, (g + 1) % 2)
                sp.wait_ge(S["qk_ready"], 10 * g + rotation(1, -1) + 1)
                load_wk(g + 1)
                for h in range(R):
                    sp.wait_ge(S["qk_ready"], 10 * g + rotation(1, h) + 1)
                    load_wq(g + 1, h)

            loads_in(0)
            with sp.Fori(1, G - 1) as g:
                loads_in(g)

        @block.gpsimd
        def _(pool):
            link = Link(pool, k.pool_own, k.pool_count)

            def rotate(g, half, h):
                r = 10 * g + rotation(half, h)
                slot = rotation(half, h) % 2
                pool.wait_ge(S["turned"], r + 1)
                after_first(pool, S["s_ready"], 8 * g - 8 + 4 * half + 4)
                dst = kT[:, half * HALF:(half + 1) * HALF] if h < 0 else qT[:, h, half * HALF:(half + 1) * HALF]
                nc.gpsimd.tensor_tensor(dst, turned[:, slot, 0, :], turned[:, slot, 1, :], ALU.add)\
                  .then_inc(S["rotated"], 1)

            def units(g, half):
                for h in range(-1, R):
                    rotate(g, half, h)

            units(0, 0)
            units(0, 1)
            with pool.Fori(1, G) as g:
                units(g, 0)
                units(g, 1)
            for b in range(NB):
                k.row_rstd(pool, link, 3, b)
            k.pool_count = link.n

        @block.tensor
        def _(pe):
            def unit(g, half, h):
                heads = [-1, 0] if h == 0 else [h]
                for j in heads:
                    r = 10 * g + rotation(half, j)
                    bank = QK_BANK + rotation(half, j) % 2
                    if half == 0:
                        pe.wait_ge(S["wk_loaded"] if j < 0 else wq_loaded[j], 16 * (g + 1))
                    after_first(pe, S["turned"], r - 1)
                    for c in range(C):
                        src = wk[:, c, :] if j < 0 else wq[:, j, c, :]
                        acts = k.ctxT if j < 0 else xT
                        last = nc.tensor.matmul(ps[:, bank, :], src, acts[:, c, half * HALF:(half + 1) * HALF],
                                                start=c == 0, stop=c == C - 1)
                    last.then_inc(S["qk_ready"], 1)
                b = 4 * half + h
                after_first(pe, S["v_copied"], 8 * g + b)
                for c in range(C):
                    last = nc.tensor.matmul(ps[:, V_BANK, 0:HD], k.ctxT[:, c, b * P:(b + 1) * P], wv[:, g, c, :],
                                            start=c == 0, stop=c == C - 1)
                last.then_inc(S["v_ready"], 1)

            def output(g, b):
                t = 8 * g + b
                if b == 0:
                    pe.wait_ge(S["wo_loaded"], 16 * (g + 1))
                pe.wait_ge(S["ot_copied"], t + 1)
                after_first(pe, S["y_added"], t - 1)
                for h in range(R):
                    last = nc.tensor.matmul(ps[:, Y_BANK + b % 2, :], oT[:, b % 2, h * P:(h + 1) * P],
                                            wo[:, g % 2, h, :], start=h == 0, stop=h == R - 1)
                last.then_inc(S["y_ready"], 1)

            def step(g, b, project):
                t = 8 * g + b
                if b % 4 == 0:
                    pe.wait_ge(S["rotated"], 10 * g + 5 * (b // 4 + 1))
                after_first(pe, S["exp_ready"], R * t)
                for h in range(R):
                    last = nc.tensor.matmul(ps[:, S_BANK, h * P:(h + 1) * P], qT[:, h, b * P:(b + 1) * P],
                                            kT[:, b * P:(b + 1) * P], start=True, stop=True)
                last.then_inc(S["s_ready"], 1)
                if b < 4:
                    unit(g, 1, b)
                elif project:
                    unit(g + 1, 0, b - 4)
                pe.wait_ge(S["prob_ready"], t + 1)
                after_first(pe, S["pt_copied"], t)
                k.transpose4(PT_BANK, prob[:, b % 2, :, :].rearrange("p h k -> p (h k)")).then_inc(S["pt_ready"], 1)
                if b >= 1:
                    output(g, b - 1)
                pe.wait_ge(S["pt_copied"], t + 1)
                pe.wait_ge(S["v_copied"], t + 1)
                after_first(pe, S["ot_copied"], t)
                nc.tensor.matmul(ps[:, OT_BANK, :], v[:, b, :], probT[:, b % 2, :], start=True, stop=True)\
                  .then_inc(S["ot_ready"], 1)
                if b == NB - 1:
                    output(g, b)

            k.arrived(pe, "a1_tables")
            pe.wait_ge(S["onehot_ready"], MAXPOS // P)
            for part in range(2):
                for half in range(2):
                    for c in range(MAXPOS // P):
                        last = nc.tensor.matmul(ps[:, 2 * part + half, :], rope[:, c, part * P:(part + 1) * P],
                                                onehot[:, c, half * HALF:(half + 1) * HALF],
                                                start=c == 0, stop=c == MAXPOS // P - 1)
                    last.then_inc(S["table_ready"], 1)
            for b in range(NB):
                pe.wait_ge(S["xn_ready"], b + 1)
                after_first(pe, S["xt_copied"], b - 1)
                k.transpose4(4 + b % 2, k.xn[:, b % 2, :]).then_inc(S["xt_ready"], 1)
            pe.wait_ge(S["table_copied"], 4)
            k.arrived(pe, "a1_wv")
            pe.wait_ge(S["xt_copied"], NB)
            for h in range(R):
                unit(0, 0, h)

            def group(g, last=False):
                for b in range(NB):
                    step(g, b, not last)

            group(0)
            with pe.Fori(1, G - 1) as g:
                group(g)
            group(G - 1, last=True)

        @block.scalar
        def _(act):
            def copy_v(g, b):
                act.wait_ge(S["v_ready"], 8 * g + b + 1)
                after_first(act, S["ot_ready"], 8 * g - 8 + b + 1)
                nc.scalar.copy(v[:, b, :], ps[:, V_BANK, 0:HD]).then_inc(S["v_copied"], 1)

            def step(g, b, project):
                t = 8 * g + b
                slot = b % 2
                act.wait_ge(S["bias_ready"], t + 1)
                after_first(act, S["pt_ready"], t - 1)
                for h in range(R):
                    nc.scalar.activation(prob[:, slot, h, :], ps[:, S_BANK, h * P:(h + 1) * P], ACT.Exp,
                                         bias=bias[:, slot, h:h + 1], scale=scale,
                                         accum_out=total[:, slot, h:h + 1]).then_inc(S["exp_ready"], 1)
                if b < 4:
                    copy_v(g, b + 4)
                elif project:
                    copy_v(g + 1, b - 4)
                act.wait_ge(S["pt_ready"], t + 1)
                after_first(act, S["ot_ready"], t - 1)
                nc.scalar.copy(probT[:, slot, :], ps[:, PT_BANK, :]).then_inc(S["pt_copied"], 1)
                act.wait_ge(S["ot_ready"], t + 1)
                after_first(act, S["y_ready"], t - 1)
                nc.scalar.copy(oT[:, slot, :], ps[:, OT_BANK, :]).then_inc(S["ot_copied"], 1)

            for part, table in enumerate((cos, sin)):
                for half in range(2):
                    n = 2 * part + half
                    act.wait_ge(S["table_ready"], n + 1)
                    nc.scalar.copy(table[:, half * HALF:(half + 1) * HALF], ps[:, n, :])\
                      .then_inc(S["table_copied"], 1)
            for b in range(NB):
                act.wait_ge(S["xt_ready"], b + 1)
                nc.scalar.copy(xT[:, :, b * P:(b + 1) * P],
                               ps[:, 4 + b % 2, :].rearrange("p (c t) -> p c t", c=C)).then_inc(S["xt_copied"], 1)
            for b in range(4):
                copy_v(0, b)

            def group(g, last=False):
                for b in range(NB):
                    step(g, b, not last)

            group(0)
            with act.Fori(1, G - 1) as g:
                group(g)
            group(G - 1, last=True)

        @block.vector
        def _(dve):
            link = Link(dve, k.dve_own, k.dve_count)
            hot, top = HD // 2, MAXPOS - 1

            k.arrived(dve, "a1_tables")
            link(nc.vector.tensor_copy(pos[:, :], pos_i[:, :]))
            link(nc.vector.tensor_scalar(wrap[:, :], pos[:, :], 0.0, float(MAXPOS), ALU.is_lt, ALU.mult))
            link(nc.vector.tensor_tensor(pos[:, :], pos[:, :], wrap[:, :], ALU.add))
            link(nc.vector.tensor_scalar(pos[:, :], pos[:, :], 0.0, float(top), ALU.max, ALU.min))
            k.arrived(dve, "a1_tables")
            for c in range(MAXPOS // P):
                nc.vector.tensor_scalar(onehot[:, c, :], pos[:, :], iota[:, c:c + 1], None, ALU.is_equal)\
                  .then_inc(S["onehot_ready"], 1)
            for b in range(NB):
                after_first(dve, S["xt_ready"], b - 1)
                k.normed(dve, 2, b, k.xn[:, b % 2, :]).then_inc(S["xn_ready"], 1)
            k.arrived(dve, "a1_mask")
            link(nc.vector.memset(fill[:, :], -1e9 / scale))
            link(nc.vector.tensor_scalar(hidden[:, :, :], mask[:, :, :], 0.0, None, ALU.is_equal))
            dve.wait_ge(S["table_copied"], 4)

            own0 = link.n
            OWN = 3

            def turn(g, half, h):
                r = 10 * g + rotation(half, h)
                slot = rotation(half, h) % 2
                bank = ps[:, QK_BANK + slot, :]
                tok = slice(half * HALF, (half + 1) * HALF)
                dve.wait_ge(S["qk_ready"], r + 1)
                after_first(dve, S["rotated"], r - 1)
                nc.vector.tensor_tensor(turned[:, slot, 0, :], bank, cos[:, tok], ALU.mult)
                nc.vector.tensor_tensor(turned[0:hot, slot, 1, :], bank[hot:P, :], sin[hot:P, tok], ALU.mult)
                nc.vector.tensor_tensor(turned[hot:P, slot, 1, :], bank[0:hot, :], sin[0:hot, tok], ALU.mult)\
                  .then_inc(S["turned"], 1)

            def add(g, b, last):
                t = 8 * g + b
                dve.wait_ge(S["y_ready"], t + 1)
                after_first(dve, S["y_added"], t - 7)
                nc.vector.tensor_tensor(k.x[:, b, :], k.x[:, b, :], ps[:, Y_BANK + b % 2, :], ALU.add)\
                  .then_inc(S["y_added"], 1)
                if last:
                    dve.wait_ge(S["y_added"], t + 1)
                    k.row_stats(dve, last, b)

            def step(g, b, project, last):
                t = 8 * g + b
                own = own0 + OWN * t
                slot = b % 2
                scores = ps[:, S_BANK, :].rearrange("p (h k) -> p h k", h=R)
                dve.wait_ge(S["s_ready"], t + 1)
                nc.vector.memset(gate[:, :], 0.0)
                nc.vector.copy_predicated(scores, hidden[:, b, :].unsqueeze(1).to_broadcast([P, R, P]),
                                          fill[:, :].unsqueeze(1).to_broadcast([P, R, P])).then_inc(k.dve_own, 1)
                dve.wait_ge(k.dve_own, own + 1)
                nc.vector.tensor_reduce(negmax[:, slot, :], scores, AX.X, ALU.max, negate=True)\
                  .then_inc(k.dve_own, 1)
                dve.wait_ge(k.dve_own, own + 2)
                after_first(dve, S["exp_ready"], R * (t - 1))
                nc.vector.tensor_scalar(bias[:, slot, :], negmax[:, slot, :], scale, None, ALU.mult)\
                  .then_inc(S["bias_ready"], 1)
                next_g, half, h = (g, 1, b) if b < 4 else (g + 1, 0, b - 4)
                if h == 0 and (project or b < 4):
                    turn(next_g, half, -1)
                dve.wait_ge(S["exp_ready"], R * (t + 1))
                nc.vector.reciprocal(inv[:, slot, :], total[:, slot, :]).then_inc(k.dve_own, 1)
                dve.wait_ge(k.dve_own, own + 3)
                nc.vector.tensor_tensor(prob[:, slot, :, :], prob[:, slot, :, :],
                                        inv[:, slot, :].unsqueeze(2).to_broadcast([P, R, P]), ALU.mult)\
                  .then_inc(S["prob_ready"], 1)
                if project or b < 4:
                    turn(next_g, half, h)
                if b >= 1:
                    add(g, b - 1, last)
                if b == NB - 1:
                    add(g, b, last)

            for h in range(-1, R):
                turn(0, 0, h)

            def group(g, last=None):
                for b in range(NB):
                    step(g, b, last is None, last)

            group(0)
            with dve.Fori(1, G - 1) as g:
                group(g)
            group(G - 1, last=Link(dve, k.sem("a1_stats")))
            k.dve_count = own0 + OWN * NB * G


def mixture_of_experts(k, dram):
    nc, ps = k.nc, k.ps
    NE = 3
    HALF = TOK // 2
    VISION = int(P * 0.3)
    FUNCS = (ACT.Tanh, ACT.Gelu, ACT.Silu)
    GATE, NORMS, PICKED = slice(0, NB * NE), slice(64, 64 + 2 * NB), slice(128, 128 + NB * 2 * NE)
    PRE_BANK, OUT_BANK, OUT_BANKS, GATE_BANK, T_BANK = 0, 2, 3, 5, 6
    with ExitStack() as ctx:
        w1 = k.sb(ctx, "f1_w1", [P, NE, C, D])
        w2 = k.sb(ctx, "f1_w2", [P, NE, C, D])
        b1 = k.sb(ctx, "f1_b1", [P, NE, C])
        b2 = k.sb(ctx, "f1_b2", [P, NE, D])
        gw = k.sb(ctx, "f1_gw", [P, C, NE])
        gw_ratio = k.sb(ctx, "f1_gw_ratio", [P, NE])
        gb = k.sb(ctx, "f1_gb", [P, NE])
        ones = k.sb(ctx, "f1_ones", [P, P])
        row0 = k.sb(ctx, "f1_row0", [P, P])
        share = k.sb(ctx, "f1_share", [P, 2])
        xT = k.sb(ctx, "f1_xT", [P, C, TOK])
        act_T = k.sb(ctx, "f1_act", [P, 2, C, HALF])
        junk = k.sb(ctx, "f1_junk", [P, 2, D])
        norms = k.sb(ctx, "f1_norms", [P, NB])
        parts = k.sb(ctx, "f1_parts", [P, NB, 2])
        prob = k.sb(ctx, "f1_prob", [P, NB, NE])
        tmp = k.sb(ctx, "f1_tmp", [P, NB, NE])
        ratio = k.sb(ctx, "f1_ratio", [P, NB])
        one = k.sb(ctx, "f1_one", [P, 12, NB])
        first = k.sb(ctx, "f1_first", [P, NB, NE])
        lowest = k.sb(ctx, "f1_lowest", [P, NB, NE])
        picks = k.sb(ctx, "f1_picks", [P, NB, 2, NE])
        weight = k.sb(ctx, "f1_weight", [P, NB, NE])
        S = {n: k.sem("f1_" + n) for n in (
            "xn_ready", "norm_ready", "xt_ready", "xt_copied", "gate_ready", "asked", "answered",
            "pre_ready", "act_ready", "out_ready", "added")}
        MEANS, EXP, PICKS = 1, 2, 3
        block = ctx.enter_context(nc.Block())

        @block.sync
        def _(sp):
            for name, dst in (("gw", gw[:, :, :]), ("ones", ones[:, :]), ("share", share[:, :]), ("b1", b1[:, :, :]),
                              ("row0", row0[:, :])):
                k.load(sp, "f1_small", dst, dram["f1_" + name])
            k.load(sp, "f1_small", gw_ratio[:, :], dram["f1_gw_ratio"].partition_broadcast(P))
            k.load(sp, "f1_small", gb[:, :], dram["f1_gb"].partition_broadcast(P))
            for e in range(NE):
                k.load(sp, f"f1_w1_{e}", w1[:, e, :, :], dram["f1_w1"][e])
                k.load(sp, f"f1_w2_{e}", w2[:, e, :, :], dram["f1_w2"][e])
                k.load(sp, f"f1_w2_{e}", b2[:, e, :], dram["f1_b2"][e].partition_broadcast(P))

        @block.gpsimd
        def _(pool):
            link = Link(pool, k.pool_own, k.pool_count)
            for b in range(NB):
                k.row_rstd(pool, link, 4, b)
            k.pool_count = link.n

        @block.tensor
        def _(pe):
            def gate(b):
                pe.wait_ge(S["xt_copied"], b + 1)
                for c in range(C):
                    last = nc.tensor.matmul(ps[:, GATE_BANK, GATE][:, NE * b:NE * (b + 1)],
                                            xT[:, c, b * P:(b + 1) * P], gw[:, c, :], start=c == 0, stop=c == C - 1)
                last.then_inc(S["gate_ready"], 1)

            for b in range(NB):
                pe.wait_ge(S["xn_ready"], b + 1)
                after_first(pe, S["xt_copied"], b - 1)
                k.transpose4(T_BANK + b % 2, k.xn[:, b % 2, :]).then_inc(S["xt_ready"], 1)
                if b == 0:
                    k.arrived(pe, "f1_small")
                else:
                    gate(b - 1)
            gate(NB - 1)
            k.arrived(pe, "f1_small")
            pe.wait_ge(S["asked"], MEANS)
            nc.tensor.matmul(ps[:, GATE_BANK, NORMS], ones[:, :], parts[:, :, :].rearrange("p b n -> p (b n)"),
                             start=True, stop=True).then_inc(S["answered"], 1)

            def first_product(n):
                e, half = n // 2, n % 2
                k.arrived(pe, f"f1_w1_{e}")
                for f in range(C):
                    u = C * n + f
                    after_first(pe, S["act_ready"], u - 1)
                    for c in range(C):
                        last = nc.tensor.matmul(ps[:, PRE_BANK + u % 2, :], w1[:, e, c, f * P:(f + 1) * P],
                                                xT[:, c, half * HALF:(half + 1) * HALF], start=c == 0, stop=c == C - 1)
                    last.then_inc(S["pre_ready"], 1)

            def second_product(n):
                e, half = n // 2, n % 2
                k.arrived(pe, f"f1_w2_{e}")
                pe.wait_ge(S["act_ready"], C * (n + 1))
                for j in range(4):
                    o = 4 * n + j
                    after_first(pe, S["added"], o - OUT_BANKS + 1)
                    for f in range(C):
                        last = nc.tensor.matmul(ps[:, OUT_BANK + o % OUT_BANKS, :],
                                                act_T[:, n % 2, f, j * P:(j + 1) * P], w2[:, e, f, :],
                                                start=f == 0, stop=f == C - 1)
                    last.then_inc(S["out_ready"], 1)

            for n in range(2 * NE + 1):
                if n < 2 * NE:
                    first_product(n)
                if n == 0:
                    k.arrived(pe, "f1_small")
                    pe.wait_ge(S["asked"], PICKS)
                    nc.tensor.matmul(ps[:, GATE_BANK, PICKED], row0[:, :],
                                     picks[:, :, :, :].rearrange("p b i e -> p (b i e)"), start=True, stop=True)\
                      .then_inc(S["answered"], 1)
                else:
                    second_product(n - 1)

        @block.scalar
        def _(act):
            for b in range(NB):
                act.wait_ge(S["xn_ready"], b + 1)
                after_first(act, S["norm_ready"], b - 1)
                nc.scalar.activation(junk[:, b % 2, :], k.xn[:, b % 2, :], ACT.Abs, accum_out=norms[:, b:b + 1])\
                  .then_inc(S["norm_ready"], 1)
                act.wait_ge(S["xt_ready"], b + 1)
                nc.scalar.copy(xT[:, :, b * P:(b + 1) * P],
                               ps[:, T_BANK + b % 2, :].rearrange("p (c t) -> p c t", c=C)).then_inc(S["xt_copied"], 1)
            act.wait_ge(S["asked"], EXP)
            nc.scalar.activation(prob[:, :, :], prob[:, :, :], ACT.Exp).then_inc(S["answered"], 1)
            k.arrived(act, "f1_small")
            for n in range(2 * NE):
                e = n // 2
                after_first(act, S["out_ready"], 4 * (n - 1))
                for f in range(C):
                    u = C * n + f
                    act.wait_ge(S["pre_ready"], u + 1)
                    nc.scalar.activation(act_T[:, n % 2, f, :], ps[:, PRE_BANK + u % 2, :], FUNCS[e],
                                         bias=b1[:, e, f:f + 1]).then_inc(S["act_ready"], 1)

        @block.vector
        def _(dve):
            link = Link(dve, k.dve_own, k.dve_count)
            tt, ts = nc.vector.tensor_tensor, nc.vector.tensor_scalar
            for b in range(NB):
                after_first(dve, S["xt_ready"], b - 1)
                after_first(dve, S["norm_ready"], b - 1)
                k.normed(dve, 3, b, k.xn[:, b % 2, :]).then_inc(S["xn_ready"], 1)
            k.arrived(dve, "f1_small")
            dve.wait_ge(S["norm_ready"], NB)
            link(ts(parts[:, :, 0], norms[:, :], share[:, 0:1], None, ALU.mult))
            ts(parts[:, :, 1], norms[:, :], share[:, 1:2], None, ALU.mult).then_inc(S["asked"], 1)
            dve.wait_ge(S["gate_ready"], NB)
            dve.wait_ge(S["answered"], MEANS)
            means = ps[:, GATE_BANK, NORMS].rearrange("p (b n) -> p b n", n=2)
            link(ts(ratio[:, :], means[:, :, 1], 1e-8, None, ALU.add))
            link(nc.vector.reciprocal(one[:, 0, :], ratio[:, :]))
            link(tt(ratio[:, :], means[:, :, 0], one[:, 0, :], ALU.mult))
            each = [P, NB, NE]
            k.arrived(dve, "f1_small")
            k.arrived(dve, "f1_small")
            link(tt(tmp[:, :, :], ratio[:, :].unsqueeze(2).to_broadcast(each),
                    gw_ratio[:, :].unsqueeze(1).to_broadcast(each), ALU.mult))
            link(tt(tmp[:, :, :], ps[:, GATE_BANK, GATE].rearrange("p (b e) -> p b e", e=NE), tmp[:, :, :], ALU.add))
            link(tt(tmp[:, :, :], tmp[:, :, :], gb[:, :].unsqueeze(1).to_broadcast(each), ALU.add))
            link(nc.vector.tensor_reduce(one[:, 1, :], tmp[:, :, :], AX.X, ALU.max))
            tt(prob[:, :, :], tmp[:, :, :], one[:, 1, :].unsqueeze(2).to_broadcast(each), ALU.subtract)\
              .then_inc(S["asked"], 1)
            dve.wait_ge(S["answered"], EXP)
            link(nc.vector.tensor_reduce(one[:, 2, :], prob[:, :, :], AX.X, ALU.add))
            link(nc.vector.reciprocal(one[:, 3, :], one[:, 2, :]))
            link(tt(prob[:, :, :], prob[:, :, :], one[:, 3, :].unsqueeze(2).to_broadcast(each), ALU.mult))
            p0, p1, p2 = (prob[:, :, e] for e in range(NE))
            top, second, least, larger, lesser, other, either = (one[:, n, :] for n in range(4, 11))
            link(tt(larger, p0, p1, ALU.max))
            link(tt(lesser, p0, p1, ALU.min))
            link(tt(top, larger, p2, ALU.max))
            link(tt(least, lesser, p2, ALU.min))
            link(tt(other, larger, p2, ALU.min))
            link(tt(second, lesser, other, ALU.max))
            link(tt(first[:, :, :], prob[:, :, :], top.unsqueeze(2).to_broadcast(each), ALU.is_ge))
            link(tt(lowest[:, :, :], prob[:, :, :], least.unsqueeze(2).to_broadcast(each), ALU.is_le))
            link(tt(either, first[:, :, 0], first[:, :, 1], ALU.max))
            link(tt(first[:, :, 2], first[:, :, 2], either, ALU.is_gt))
            link(tt(first[:, :, 1], first[:, :, 1], first[:, :, 0], ALU.is_gt))
            link(tt(either, lowest[:, :, 2], lowest[:, :, 1], ALU.max))
            link(tt(lowest[:, :, 0], lowest[:, :, 0], either, ALU.is_gt))
            link(tt(lowest[:, :, 1], lowest[:, :, 1], lowest[:, :, 2], ALU.is_gt))
            link(nc.vector.tensor_copy(picks[:, :, 0, :], first[:, :, :]))
            link(tt(tmp[:, :, :], first[:, :, :], lowest[:, :, :], ALU.add))
            ts(picks[:, :, 1, :], tmp[:, :, :], -1.0, 1.0, ALU.mult, ALU.add).then_inc(S["asked"], 1)
            link(tt(one[:, 0, :], top, second, ALU.add))
            link(ts(one[:, 1, :], one[:, 0, :], 1e-8, None, ALU.add))
            link(nc.vector.reciprocal(one[:, 2, :], one[:, 1, :]))
            link(tt(top, top, one[:, 2, :], ALU.mult))
            link(tt(second, second, one[:, 2, :], ALU.mult))
            dve.wait_ge(S["asked"], PICKS)
            dve.wait_ge(S["answered"], PICKS)
            picked = ps[:, GATE_BANK, PICKED].rearrange("p (b i e) -> p b i e", b=NB, i=2)
            link(tt(weight[:, :, :], picked[:, :, 0, :], top.unsqueeze(2).to_broadcast(each), ALU.mult))
            link(tt(tmp[:, :, :], picked[:, :, 1, :], second.unsqueeze(2).to_broadcast(each), ALU.mult))
            link(tt(weight[:, :, :], weight[:, :, :], tmp[:, :, :], ALU.add))

            def add(n):
                e, half = n // 2, n % 2
                k.arrived(dve, f"f1_w2_{e}")
                for j in range(4):
                    b = 4 * half + j
                    link(nc.vector.scalar_tensor_tensor(k.x[:, b, :], b2[:, e, :], weight[:, b, e:e + 1],
                                                        k.x[:, b, :], ALU.mult, ALU.add))
                    dve.wait_ge(S["out_ready"], 4 * n + j + 1)
                    nc.vector.scalar_tensor_tensor(k.x[:, b, :], ps[:, OUT_BANK + (4 * n + j) % OUT_BANKS, :],
                                                   weight[:, b, e:e + 1], k.x[:, b, :], ALU.mult, ALU.add)\
                      .then_inc(S["added"], 1)
                    dve.wait_ge(S["added"], 4 * n + j + 1)
                    if e == NE - 1:
                        k.row_stats(dve, link, b)

            for n in range(2 * NE):
                add(n)
            k.dve_count = link.n


def autocorrelation(k, dram):
    nc, ps = k.nc, k.ps
    CTX_BANK, Q_BANK, C_BANK, WT_BANK, W_BANK, OUT_BANK = 0, 2, 3, 4, 5, 7
    K1, K2, VC, VS = range(4)
    TOP = 9
    with ExitStack() as ctx:
        table = k.sb(ctx, "a2_table", [P, 12, P])
        T_Q, T_K2, T_VC, T_VS, T_C1, T_C2, T_WC, T_WS, T_OC, T_OSN, T_OS, T_LAST = (
            table[:, n, :] for n in range(12))
        value = k.sb(ctx, "a2_ctx", [P, NB, D])
        freq = k.sb(ctx, "a2_freq", [P, 2, 4, D])
        prod = k.sb(ctx, "a2_prod", [P, 2, D])
        corr = k.sb(ctx, "a2_corr", [P, 2, C, P])
        less8 = k.sb(ctx, "a2_less8", [P, C, P])
        less9 = k.sb(ctx, "a2_less9", [P, C, P])
        top8 = k.sb(ctx, "a2_top8", [P, C, 8])
        ninth = k.sb(ctx, "a2_ninth", [P, C, 8])
        negmax = k.sb(ctx, "a2_negmax", [P, 2, C])
        expo = k.sb(ctx, "a2_exp", [P, C, P])
        picked = k.sb(ctx, "a2_picked", [P, C, P])
        total = k.sb(ctx, "a2_total", [P, C])
        inv = k.sb(ctx, "a2_inv", [P, C])
        weight = k.sb(ctx, "a2_weight", [P, C, P])
        weightT = k.sb(ctx, "a2_weightT", [P, D])
        shift = k.sb(ctx, "a2_shift", [P, 4, D])
        S = {n: k.sem("a2_" + n) for n in (
            "xn_ready", "freq_ready", "freq_copied", "q_ready", "prod_ready", "corr_ready", "corr_copied",
            "max_ready", "exp_ready", "weight_ready", "wt_ready", "wt_copied", "w_ready", "shift_ready",
            "out_ready", "added")}
        block = ctx.enter_context(nc.Block())

        @block.sync
        def _(sp):
            k.load(sp, "a2_table", table[:, :, :], dram["a2_table"])
            for b in range(NB):
                k.load(sp, f"a2_ctx{b // 4}", value[:, b, :], dram["ctx"][b])

        @block.gpsimd
        def _(pool):
            link = Link(pool, k.pool_own, k.pool_count)
            for b in range(NB):
                k.row_rstd(pool, link, 5, b)
            k.pool_count = link.n

        @block.tensor
        def _(pe):
            mm = nc.tensor.matmul

            def context(b):
                k.arrived(pe, f"a2_ctx{b // 4}")
                for n, t in enumerate((T_Q, T_K2, T_VC, T_VS)):
                    u = 4 * b + n
                    after_first(pe, S["freq_copied"], u - 1)
                    mm(ps[:, CTX_BANK + u % 2, :], t, value[:, b, :], start=True, stop=True)\
                        .then_inc(S["freq_ready"], 1)

            def query(b):
                pe.wait_ge(S["xn_ready"], b + 1)
                after_first(pe, S["prod_ready"], b)
                mm(ps[:, Q_BANK, :], T_Q, k.xn[:, b % 2, :], start=True, stop=True).then_inc(S["q_ready"], 1)

            def correlate(b):
                pe.wait_ge(S["prod_ready"], b + 1)
                after_first(pe, S["corr_copied"], b)
                for c in range(C):
                    o = ps[:, C_BANK, c * P:(c + 1) * P]
                    mm(o, prod[:, 0, c * P:(c + 1) * P], T_C1, start=True, stop=False)
                    last = mm(o, prod[:, 1, c * P:(c + 1) * P], T_C2, start=False, stop=True)
                last.then_inc(S["corr_ready"], 1)

            def weights(b):
                pe.wait_ge(S["weight_ready"], b + 1)
                after_first(pe, S["wt_copied"], b)
                k.transpose4(WT_BANK, weight[:, :, :].rearrange("p c t -> p (c t)")).then_inc(S["wt_ready"], 1)

            def weights_transform(b):
                pe.wait_ge(S["wt_copied"], b + 1)
                after_first(pe, S["shift_ready"], b)
                mm(ps[:, W_BANK, :], T_WC, weightT[:, :], start=True, stop=True)
                mm(ps[:, W_BANK + 1, :], T_WS, weightT[:, :], start=True, stop=True).then_inc(S["w_ready"], 1)

            def output(b):
                after_first(pe, S["added"], b)
                mm(ps[:, OUT_BANK, :], T_LAST, value[:, b, :], start=True, stop=False)
                pe.wait_ge(S["shift_ready"], b + 1)
                for n, t in enumerate((T_OC, T_OC, T_OSN, T_OS)):
                    last = mm(ps[:, OUT_BANK, :], t, shift[:, n, :], start=False, stop=n == 3)
                last.then_inc(S["out_ready"], 1)

            k.arrived(pe, "a2_table")
            for i in range(NB + 1):
                if i < NB:
                    context(i)
                    query(i)
                if i >= 1:
                    weights(i - 1)
                if i < NB:
                    correlate(i)
                if i >= 1:
                    weights_transform(i - 1)
                    output(i - 1)

        @block.scalar
        def _(act):
            def context(b):
                for n in range(4):
                    u = 4 * b + n
                    act.wait_ge(S["freq_ready"], u + 1)
                    after_first(act, S["prod_ready"], b - 1)
                    after_first(act, S["shift_ready"], b - 1)
                    nc.scalar.copy(freq[:, b % 2, n, :], ps[:, CTX_BANK + u % 2, :]).then_inc(S["freq_copied"], 1)

            for i in range(NB + 1):
                if i < NB:
                    context(i)
                if i >= 1:
                    act.wait_ge(S["wt_ready"], i)
                    after_first(act, S["w_ready"], i - 1)
                    nc.scalar.copy(weightT[:, :], ps[:, WT_BANK, :]).then_inc(S["wt_copied"], 1)
                if i < NB:
                    act.wait_ge(S["corr_ready"], i + 1)
                    after_first(act, S["weight_ready"], i - 1)
                    nc.scalar.copy(corr[:, i % 2, :, :].rearrange("p c t -> p (c t)"), ps[:, C_BANK, :])\
                      .then_inc(S["corr_copied"], 1)
                    act.wait_ge(S["max_ready"], i + 1)
                    act.wait_ge(S["corr_copied"], i + 1)
                    after_first(act, S["weight_ready"], i)
                    for c in range(C):
                        nc.scalar.activation(expo[:, c, :], corr[:, i % 2, c, :], ACT.Exp,
                                             bias=negmax[:, i % 2, c:c + 1]).then_inc(S["exp_ready"], 1)

        @block.vector
        def _(dve):
            link = Link(dve, k.dve_own, k.dve_count)
            tt = nc.vector.tensor_tensor

            def normalise(b):
                after_first(dve, S["q_ready"], b - 1)
                k.normed(dve, 4, b, k.xn[:, b % 2, :]).then_inc(S["xn_ready"], 1)

            def multiply(b):
                dve.wait_ge(S["q_ready"], b + 1)
                dve.wait_ge(S["freq_copied"], 4 * b + 2)
                after_first(dve, S["corr_ready"], b)
                tt(prod[:, 0, :], ps[:, Q_BANK, :], freq[:, b % 2, K1, :], ALU.mult)
                tt(prod[:, 1, :], ps[:, Q_BANK, :], freq[:, b % 2, K2, :], ALU.mult).then_inc(S["prod_ready"], 1)

            def multiply_shift(b):
                dve.wait_ge(S["w_ready"], b + 1)
                dve.wait_ge(S["freq_copied"], 4 * b + 4)
                after_first(dve, S["out_ready"], b)
                wc, ws = ps[:, W_BANK, :], ps[:, W_BANK + 1, :]
                vc, vs = freq[:, b % 2, VC, :], freq[:, b % 2, VS, :]
                tt(shift[:, 0, :], wc, vc, ALU.mult)
                tt(shift[:, 1, :], ws, vs, ALU.mult)
                tt(shift[:, 2, :], ws, vc, ALU.mult)
                tt(shift[:, 3, :], wc, vs, ALU.mult).then_inc(S["shift_ready"], 1)

            def pick(b):
                dve.wait_ge(S["corr_copied"], b + 1)
                for c in range(C):
                    nc.vector.max(top8[:, c, :], corr[:, b % 2, c, :]).then_inc(k.dve_own, 1)
                link.n += C
                dve.wait_ge(k.dve_own, link.n)
                after_first(dve, S["exp_ready"], C * (b - 1))
                nc.vector.tensor_scalar(negmax[:, b % 2, :], top8[:, :, 0], -1.0, None, ALU.mult)\
                  .then_inc(S["max_ready"], 1)
                for c in range(C):
                    nc.vector.match_replace(less8[:, c, :], top8[:, c, :], corr[:, b % 2, c, :], LOWEST)\
                      .then_inc(k.dve_own, 1)
                link.n += C
                dve.wait_ge(k.dve_own, link.n)
                link(nc.vector.tensor_reduce(ninth[:, :, 0], less8[:, :, :], AX.X, ALU.max))
                for c in range(C):
                    nc.vector.match_replace(less9[:, c, :], ninth[:, c, :], less8[:, c, :], LOWEST)\
                      .then_inc(k.dve_own, 1)
                link.n += C
                dve.wait_ge(k.dve_own, link.n)
                dve.wait_ge(S["exp_ready"], C * (b + 1))
                link(nc.vector.scalar_tensor_tensor(picked[:, :, :], less9[:, :, :], LOWEST, expo[:, :, :],
                                                    ALU.is_equal, ALU.mult))
                link(nc.vector.tensor_reduce(total[:, :], picked[:, :, :], AX.X, ALU.add))
                link(nc.vector.reciprocal(inv[:, :], total[:, :]))
                after_first(dve, S["wt_ready"], b)
                tt(weight[:, :, :], picked[:, :, :], inv[:, :].unsqueeze(2).to_broadcast([P, C, P]), ALU.mult)\
                    .then_inc(S["weight_ready"], 1)
                dve.wait_ge(S["weight_ready"], b + 1)

            def add(b):
                dve.wait_ge(S["out_ready"], b + 1)
                tt(k.x[:, b, :], k.x[:, b, :], ps[:, OUT_BANK, :], ALU.add).then_inc(S["added"], 1)
                dve.wait_ge(S["added"], b + 1)
                k.row_stats(dve, link, b)

            link(nc.vector.memset(ninth[:, :, :], LOWEST))
            normalise(0)
            normalise(1)
            for i in range(NB + 1):
                if i < NB:
                    multiply(i)
                    if i + 2 < NB:
                        normalise(i + 2)
                if i >= 1:
                    multiply_shift(i - 1)
                if i < NB:
                    pick(i)
                if i >= 1:
                    add(i - 1)
            k.dve_count = link.n


def scaled_linear(k, dram):
    nc, ps = k.nc, k.ps
    OUT_BANK, OUT_BANKS, T_BANK = 0, 4, 6
    with ExitStack() as ctx:
        wt = k.sb(ctx, "f2_w", [P, C, D])
        scale = k.sb(ctx, "f2_scale", [P, C, C])
        bias = k.sb(ctx, "f2_bias", [P, D])
        xT = k.sb(ctx, "f2_xT", [P, 2, C, P])
        S = {n: k.sem("f2_" + n) for n in (
            "w_ready", "xn_ready", "biased", "xt_ready", "xt_copied", "out_ready", "added")}
        block = ctx.enter_context(nc.Block())

        @block.sync
        def _(sp):
            k.load(sp, "f2_w", scale[:, :, :].rearrange("p i o -> p (i o)"),
                   dram["f2_scale"].partition_broadcast(P))
            k.load(sp, "f2_w", wt[:, :, :], dram["f2_w"])
            k.load(sp, "f2_bias", bias[:, :], dram["f2_bias"].partition_broadcast(P))

        @block.gpsimd
        def _(pool):
            link = Link(pool, k.pool_own, k.pool_count)
            k.arrived(pool, "f2_bias")
            for b in range(NB):
                pool.wait_ge(S["xn_ready"], b + 1)
                nc.gpsimd.tensor_tensor(k.x[:, b, :], k.x[:, b, :], bias[:, :], ALU.add).then_inc(S["biased"], 1)
                if b >= 2:
                    k.row_rstd(pool, link, 6, b - 2)
            k.row_rstd(pool, link, 6, NB - 2)
            k.row_rstd(pool, link, 6, NB - 1)
            k.pool_count = link.n

        @block.tensor
        def _(pe):
            for i in range(NB + 1):
                if i < NB:
                    pe.wait_ge(S["xn_ready"], i + 1)
                    after_first(pe, S["xt_copied"], i - 1)
                    k.transpose4(T_BANK + i % 2, k.xn[:, i % 2, :]).then_inc(S["xt_ready"], 1)
                if i >= 1:
                    b = i - 1
                    if b == 0:
                        pe.wait_ge(S["w_ready"], C)
                    pe.wait_ge(S["xt_copied"], b + 1)
                    after_first(pe, S["added"], b - OUT_BANKS + 1)
                    for c in range(C):
                        last = nc.tensor.matmul(ps[:, OUT_BANK + b % OUT_BANKS, :], xT[:, b % 2, c, :], wt[:, c, :],
                                                start=c == 0, stop=c == C - 1)
                    last.then_inc(S["out_ready"], 1)

        @block.scalar
        def _(act):
            for b in range(NB):
                act.wait_ge(S["xt_ready"], b + 1)
                after_first(act, S["out_ready"], b - 1)
                nc.scalar.copy(xT[:, b % 2, :, :].rearrange("p c t -> p (c t)"), ps[:, T_BANK + b % 2, :])\
                  .then_inc(S["xt_copied"], 1)

        @block.vector
        def _(dve):
            link = Link(dve, k.dve_own, k.dve_count)

            def normalise(b):
                after_first(dve, S["xt_ready"], b - 1)
                k.normed(dve, 5, b, k.xn[:, b % 2, :]).then_inc(S["xn_ready"], 1)

            normalise(0)
            k.arrived(dve, "f2_w")
            k.arrived(dve, "f2_w")
            for c in range(C):
                w = wt[:, c, :].rearrange("p (o n) -> p o n", o=C)
                nc.vector.tensor_tensor(w, w, scale[:, c, :].unsqueeze(2).to_broadcast([P, C, P]), ALU.mult)\
                  .then_inc(S["w_ready"], 1)
            normalise(1)
            for b in range(NB):
                if b + 2 < NB:
                    normalise(b + 2)
                dve.wait_ge(S["out_ready"], b + 1)
                dve.wait_ge(S["biased"], b + 1)
                nc.vector.tensor_tensor(k.x[:, b, :], k.x[:, b, :], ps[:, OUT_BANK + b % OUT_BANKS, :], ALU.add)\
                  .then_inc(S["added"], 1)
                dve.wait_ge(S["added"], b + 1)
                k.row_stats(dve, link, b)
            k.dve_count = link.n


def token_attention(k, dram):
    nc, ps = k.nc, k.ps
    H, NK = 16, 32
    HJ = P // NK
    J = H // HJ
    T = D // P
    scale = 1.0 / float((P // H) ** 0.5)
    PROJ = NK + P
    Q_BANK, S_BANK, T_BANK, PV_BANK, OUT_BANK = 0, 1, 3, 5, 6
    with ExitStack() as ctx:
        w = k.sb(ctx, "a3_w", [P, 4, P])
        proj = k.sb(ctx, "a3_proj", [P, C, PROJ])
        bcol = k.sb(ctx, "a3_bcol", [P, 2])
        brow = k.sb(ctx, "a3_brow", [1, 2, P])
        ones = k.sb(ctx, "a3_ones", [P, 1])
        of_head = k.sb(ctx, "a3_of_head", [P, H])
        of_pair = k.sb(ctx, "a3_of_pair", [P, J, P])
        sums = k.sb(ctx, "a3_sums", [1, PROJ])
        sums_k = k.sb(ctx, "a3_sums_k", [1, NB, NK])
        ck = k.sb(ctx, "a3_ck", [P, NB, NK])
        cv = k.sb(ctx, "a3_cv", [P, NB, P])
        keys = k.sb(ctx, "a3_keys", [P, NB, NK])
        values = k.sb(ctx, "a3_values", [P, NB, P])
        spread_k = k.sb(ctx, "a3_spread_k", [P, 2, H, NK])
        spread_v = k.sb(ctx, "a3_spread_v", [P, 2, J, P])
        q = k.sb(ctx, "a3_q", [P, 2, D])
        top = k.sb(ctx, "a3_top", [P, 2, H])
        prob = k.sb(ctx, "a3_prob", [P, 3, H, NK])
        total = k.sb(ctx, "a3_total", [P, 2, H])
        inv = k.sb(ctx, "a3_inv", [P, 2, H])
        probT = k.sb(ctx, "a3_probT", [P, 2, J, D])
        o = k.sb(ctx, "a3_o", [P, 2, D])
        S = {n: k.sem("a3_" + n) for n in (
            "made", "made_copied", "k_spread", "v_spread", "xn_ready", "q_ready", "q_copied", "s_ready", "shifted",
            "exp_ready", "inv_ready", "prob_ready", "pt_ready", "pt_copied", "o_ready", "o_copied", "out_ready",
            "added")}
        block = ctx.enter_context(nc.Block())
        TILES = NB * T
        SUMS, PROJECTED, KEYS, VALUES = 1, 2, NB + 2, NB + 3

        @block.sync
        def _(sp):
            for name, dst in (("proj", proj[:, :, :]), ("ones", ones[:, :]), ("w", w[:, :, :]), ("brow", brow[:, :, :]),
                              ("bcol", bcol[:, :]), ("of_head", of_head[:, :]), ("of_pair", of_pair[:, :, :])):
                k.load(sp, "a3_consts", dst, dram["a3_" + name])

        @block.gpsimd
        def _(pool):
            link = Link(pool, k.pool_own, k.pool_count)

            def spread(b):
                if b == 0:
                    pool.wait_ge(S["made_copied"], KEYS)
                    k.arrived(pool, "a3_consts")
                after_first(pool, S["s_ready"], T * (b - 1))
                nc.gpsimd.tensor_tensor(spread_k[:, b % 2, :, :], keys[:, b, :].unsqueeze(1).to_broadcast([P, H, NK]),
                                        of_head[:, :].unsqueeze(2).to_broadcast([P, H, NK]), ALU.mult)\
                  .then_inc(S["k_spread"], 1)
                if b == 0:
                    pool.wait_ge(S["made_copied"], VALUES + 1)
                    k.arrived(pool, "a3_consts")
                after_first(pool, S["o_ready"], b - 1)
                nc.gpsimd.tensor_tensor(spread_v[:, b % 2, :, :], values[:, b, :].unsqueeze(1).to_broadcast([P, J, P]),
                                        of_pair[:, :, :], ALU.mult).then_inc(S["v_spread"], 1)

            spread(0)
            for u in range(TILES):
                b, t = u // T, u % T
                pool.wait_ge(S["inv_ready"], u + 1)
                nc.gpsimd.tensor_tensor(prob[:, u % 3, :, :], prob[:, u % 3, :, :],
                                        inv[:, u % 2, :].unsqueeze(2).to_broadcast([P, H, NK]), ALU.mult)\
                    .then_inc(S["prob_ready"], 1)
                if t == 1 and b + 1 < NB:
                    spread(b + 1)
                if t == 2 and b >= 2:
                    k.row_rstd(pool, link, 7, b - 2)
            k.row_rstd(pool, link, 7, NB - 2)
            k.row_rstd(pool, link, 7, NB - 1)
            k.pool_count = link.n

        @block.tensor
        def _(pe):
            mm = nc.tensor.matmul
            k.arrived(pe, "a3_consts")
            k.arrived(pe, "a3_consts")
            for c in range(C):
                last = mm(ps[0:1, OUT_BANK, 0:PROJ], ones[:, :], proj[:, c, :], start=c == 0, stop=c == C - 1)
            last.then_inc(S["made"], 1)
            for b in range(NB):
                if b >= 2:
                    pe.wait_ge(S["made_copied"], PROJECTED + b - 2)
                for c in range(C):
                    last = mm(ps[:, T_BANK + b % 2, 0:PROJ], k.ctxT[:, c, b * P:(b + 1) * P], proj[:, c, :],
                              start=c == 0, stop=c == C - 1)
                last.then_inc(S["made"], 1)

            def query(b):
                if b == 0:
                    k.arrived(pe, "a3_consts")
                pe.wait_ge(S["xn_ready"], b + 1)
                after_first(pe, S["q_copied"], b)
                mm(ps[:, Q_BANK, :], w[:, 0, :], k.xn[:, b % 2, :], start=True, stop=True).then_inc(S["q_ready"], 1)

            query(0)
            pe.wait_ge(S["made_copied"], SUMS)
            k.arrived(pe, "a3_consts")
            pe.wait_ge(S["made_copied"], PROJECTED + NB - 1)
            mm(ps[:, PV_BANK, 0:NB * NK], w[:, 1, :], ck[:, :, :].rearrange("p b k -> p (b k)"), start=True, stop=False)
            mm(ps[:, PV_BANK, 0:NB * NK], brow[:, 0, :], sums_k[:, :, :].rearrange("p b k -> p (b k)"),
               start=False, stop=True).then_inc(S["made"], 1)
            for half in range(2):
                for b in range(4 * half, 4 * half + 4):
                    out = ps[:, OUT_BANK + half, (b % 4) * P:(b % 4 + 1) * P]
                    mm(out, cv[:, b, :], w[:, 2, :], start=True, stop=False)
                    last = mm(out, sums[:, NK:PROJ], brow[:, 1, :], start=False, stop=True)
                last.then_inc(S["made"], 1)
            pe.wait_ge(S["made_copied"], KEYS)
            pe.wait_ge(S["made_copied"], VALUES + 1)

            def scores(u):
                b, t = u // T, u % T
                if t == 0:
                    pe.wait_ge(S["q_copied"], b + 1)
                    pe.wait_ge(S["k_spread"], b + 1)
                after_first(pe, S["shifted"], u - 1)
                mm(ps[:, S_BANK + u % 2, :], q[:, b % 2, t * P:(t + 1) * P],
                   spread_k[:, b % 2, :, :].rearrange("p h k -> p (h k)"), start=True, stop=True)\
                    .then_inc(S["s_ready"], 1)

            def transposes(u):
                pe.wait_ge(S["prob_ready"], u + 1)
                after_first(pe, S["pt_copied"], u - 1)
                k.transpose4(T_BANK + u % 2, prob[:, u % 3, :, :].rearrange("p h k -> p (h k)"))\
                    .then_inc(S["pt_ready"], 1)

            def attend(b):
                pe.wait_ge(S["pt_copied"], T * (b + 1))
                pe.wait_ge(S["v_spread"], b + 1)
                after_first(pe, S["o_copied"], b)
                for j in range(J):
                    last = mm(ps[:, PV_BANK, :], spread_v[:, b % 2, j, :], probT[:, b % 2, j, :],
                              start=j == 0, stop=j == J - 1)
                last.then_inc(S["o_ready"], 1)

            def output(b):
                pe.wait_ge(S["o_copied"], b + 1)
                after_first(pe, S["added"], b - 1)
                mm(ps[:, OUT_BANK + b % 2, :], w[:, 3, :], o[:, b % 2, :], start=True, stop=True)\
                    .then_inc(S["out_ready"], 1)

            for u in range(TILES + 2 * T):
                b, t = u // T, u % T
                if u < TILES:
                    scores(u)
                if 2 <= u < TILES + 2:
                    transposes(u - 2)
                if t == 1 and b + 1 < NB:
                    query(b + 1)
                if t == 2 and 1 <= b <= NB:
                    attend(b - 1)
                if t == 3 and 1 <= b <= NB:
                    output(b - 1)

        @block.scalar
        def _(act):
            act.wait_ge(S["made"], SUMS)
            nc.scalar.copy(sums[:, :], ps[0:1, OUT_BANK, 0:PROJ])
            nc.scalar.copy(sums_k[:, :, :], ps[0:1, OUT_BANK, 0:NK].unsqueeze(1).to_broadcast([1, NB, NK]))\
              .then_inc(S["made_copied"], 1)
            for b in range(NB):
                act.wait_ge(S["made"], PROJECTED + b)
                nc.scalar.copy(ck[:, b, :], ps[:, T_BANK + b % 2, 0:NK])
                nc.scalar.copy(cv[:, b, :], ps[:, T_BANK + b % 2, NK:PROJ]).then_inc(S["made_copied"], 1)

            def query(b):
                act.wait_ge(S["q_ready"], b + 1)
                after_first(act, S["s_ready"], T * (b - 1))
                nc.scalar.activation(q[:, b % 2, :], ps[:, Q_BANK, :], ACT.Identity, bias=bcol[:, 0:1])\
                  .then_inc(S["q_copied"], 1)

            k.arrived(act, "a3_consts")
            query(0)
            act.wait_ge(S["made"], KEYS)
            nc.scalar.copy(keys[:, :, :].rearrange("p b k -> p (b k)"), ps[:, PV_BANK, 0:NB * NK])\
              .then_inc(S["made_copied"], 1)
            for half in range(2):
                act.wait_ge(S["made"], VALUES + half)
                nc.scalar.copy(values[:, 4 * half:4 * half + 4, :].rearrange("p b d -> p (b d)"),
                               ps[:, OUT_BANK + half, :]).then_inc(S["made_copied"], 1)
            for u in range(TILES + 2 * T):
                b, t = u // T, u % T
                if u < TILES:
                    act.wait_ge(S["shifted"], u + 1)
                    nc.scalar.activation(prob[:, u % 3, :, :], prob[:, u % 3, :, :], ACT.Exp, scale=scale)\
                      .then_inc(S["exp_ready"], 1)
                if 2 <= u < TILES + 2:
                    n = u - 2
                    act.wait_ge(S["pt_ready"], n + 1)
                    after_first(act, S["o_ready"], n // T - 1)
                    nc.scalar.copy(probT[:, (n // T) % 2, :, (n % T) * P:(n % T + 1) * P],
                                   ps[:, T_BANK + n % 2, :].rearrange("p (j n) -> p j n", j=J))\
                      .then_inc(S["pt_copied"], 1)
                if t == 1 and b + 1 < NB:
                    query(b + 1)
                if t == 2 and 1 <= b <= NB:
                    act.wait_ge(S["o_ready"], b)
                    after_first(act, S["out_ready"], b - 2)
                    nc.scalar.copy(o[:, (b - 1) % 2, :], ps[:, PV_BANK, :]).then_inc(S["o_copied"], 1)

        @block.vector
        def _(dve):
            link = Link(dve, k.dve_own, k.dve_count)

            def normalise(b):
                after_first(dve, S["q_ready"], b - 1)
                k.normed(dve, 6, b, k.xn[:, b % 2, :]).then_inc(S["xn_ready"], 1)

            def shift(u):
                s = ps[:, S_BANK + u % 2, :].rearrange("p (h k) -> p h k", h=H)
                dve.wait_ge(S["s_ready"], u + 1)
                link(nc.vector.tensor_reduce(top[:, u % 2, :], s, AX.X, ALU.max))
                after_first(dve, S["pt_ready"], u - 2)
                nc.vector.tensor_tensor(prob[:, u % 3, :, :], s,
                                        top[:, u % 2, :].unsqueeze(2).to_broadcast([P, H, NK]), ALU.subtract)\
                  .then_inc(S["shifted"], 1)

            def invert(u):
                dve.wait_ge(S["exp_ready"], u + 1)
                link(nc.vector.tensor_reduce(total[:, u % 2, :], prob[:, u % 3, :, :], AX.X, ALU.add))
                after_first(dve, S["prob_ready"], u - 1)
                nc.vector.reciprocal(inv[:, u % 2, :], total[:, u % 2, :]).then_inc(S["inv_ready"], 1)

            normalise(0)
            normalise(1)
            for u in range(TILES + 2 * T + 1):
                b, t = u // T, u % T
                if u < TILES:
                    shift(u)
                if 1 <= u < TILES + 1:
                    invert(u - 1)
                if t == 2 and b + 2 < NB:
                    normalise(b + 2)
                if t == 0 and 2 <= b <= NB + 1:
                    b -= 2
                    dve.wait_ge(S["out_ready"], b + 1)
                    nc.vector.scalar_tensor_tensor(k.x[:, b, :], ps[:, OUT_BANK + b % 2, :], bcol[:, 1:2],
                                                   k.x[:, b, :], ALU.add, ALU.add).then_inc(S["added"], 1)
                    dve.wait_ge(S["added"], b + 1)
                    k.row_stats(dve, link, b)
            k.dve_count = link.n


def packed_linear(k, dram, out):
    nc, ps = k.nc, k.ps
    NIB, BITS = 8, 4
    WORDS = D // NIB
    OUT_BANK, OUT_BANKS, T_BANK = 0, 4, 6
    with ExitStack() as ctx:
        words = k.sb(ctx, "f3_words", [P, D], I32)
        zwords = k.sb(ctx, "f3_zwords", [P, WORDS], I32)
        scale = k.sb(ctx, "f3_scale", [P, D], F16)
        bias = k.sb(ctx, "f3_bias", [P, D], F16)
        q = k.sb(ctx, "f3_q", [P, C, D], I32)
        z = k.sb(ctx, "f3_z", [P, WORDS, NIB], I32)
        wt = k.sb(ctx, "f3_w", [P, C, D], F16)
        xT = k.sb(ctx, "f3_xT", [P, 2, C, P], F16)
        y = k.sb(ctx, "f3_y", [P, 2, D], F16)
        yb = k.sb(ctx, "f3_yb", [P, 2, D], F16)
        S = {n: k.sem("f3_" + n) for n in (
            "w_ready", "xn_ready", "xt_ready", "xt_copied", "out_ready", "out_copied",
            "added", "stored")}
        block = ctx.enter_context(nc.Block())

        @block.sync
        def _(sp):
            for name, dst in (("words", words[:, :]), ("zwords", zwords[:, :]), ("scale", scale[:, :])):
                k.load(sp, "f3_consts", dst, dram["f3_" + name])
            k.load(sp, "f3_consts", bias[:, :], dram["f3_bias"].partition_broadcast(P))
            for b in range(NB):
                sp.wait_ge(S["added"], b + 1)
                sp.dma_start(out[b], k.x[:, b, :]).then_inc(S["stored"], 16)
            sp.wait_ge(S["stored"], 16 * NB)

        @block.tensor
        def _(pe):
            for i in range(NB + 1):
                if i < NB:
                    pe.wait_ge(S["xn_ready"], i + 1)
                    after_first(pe, S["xt_copied"], i - 1)
                    k.transpose4(T_BANK + i % 2, k.xn[:, i % 2, :]).then_inc(S["xt_ready"], 1)
                if i >= 1:
                    b = i - 1
                    if b == 0:
                        pe.wait_ge(S["w_ready"], C)
                    pe.wait_ge(S["xt_copied"], b + 1)
                    after_first(pe, S["out_copied"], b - OUT_BANKS + 1)
                    for j in range(C):
                        last = nc.tensor.matmul(ps[:, OUT_BANK + b % OUT_BANKS, :], xT[:, b % 2, j, :], wt[:, j, :],
                                                start=j == 0, stop=j == C - 1)
                    last.then_inc(S["out_ready"], 1)

        @block.scalar
        def _(act):
            for i in range(NB + 1):
                if i < NB:
                    act.wait_ge(S["xt_ready"], i + 1)
                    after_first(act, S["out_ready"], i - 1)
                    nc.scalar.copy(xT[:, i % 2, :, :].rearrange("p c t -> p (c t)"), ps[:, T_BANK + i % 2, :])\
                      .then_inc(S["xt_copied"], 1)
                if i >= 1:
                    b = i - 1
                    act.wait_ge(S["out_ready"], b + 1)
                    after_first(act, S["added"], b - 1)
                    nc.scalar.copy(y[:, b % 2, :], ps[:, OUT_BANK + b % OUT_BANKS, :]).then_inc(S["out_copied"], 1)

        @block.vector
        def _(dve):
            link = Link(dve, k.dve_own, k.dve_count)

            def normalise(b):
                after_first(dve, S["xt_ready"], b - 1)
                k.normed(dve, 7, b, k.xn[:, b % 2, :].rearrange("p (s r) -> p r s", s=NIB),
                         k.x[:, b, :].rearrange("p (r s) -> p r s", s=NIB)).then_inc(S["xn_ready"], 1)

            def unpack(dst, src, s):
                nc.vector.tensor_scalar(dst, src, BITS * s, 15, ALU.logical_shift_right, ALU.bitwise_and)\
                  .then_inc(k.dve_own, 1)
                link.n += 1

            normalise(0)
            normalise(1)
            k.arrived(dve, "f3_consts")
            for j in range(C):
                for h in range(2):
                    rows = slice(h * WORDS, (h + 1) * WORDS)
                    unpack(q[rows, j, :], words[rows, :], 2 * j + h)
            k.arrived(dve, "f3_consts")
            for s in range(NIB):
                unpack(z[:, :, s], zwords[:, :], s)
            dve.wait_ge(k.dve_own, link.n)
            for j in range(C):
                nc.vector.tensor_tensor(wt[:, j, :], q[:, j, :], z[:, :, :].rearrange("p w s -> p (w s)"),
                                        ALU.subtract).then_inc(k.dve_own, 1)
            link.n += C
            k.arrived(dve, "f3_consts")
            for j in range(C):
                dve.wait_ge(k.dve_own, link.n - C + j + 1)
                nc.vector.tensor_tensor(wt[:, j, :], wt[:, j, :], scale[:, :], ALU.mult).then_inc(S["w_ready"], 1)
            k.arrived(dve, "f3_consts")
            for b in range(NB):
                if b + 2 < NB:
                    normalise(b + 2)
                dve.wait_ge(S["out_copied"], b + 1)
                after_first(dve, S["added"], b - 1)
                link(nc.vector.tensor_tensor(yb[:, b % 2, :], y[:, b % 2, :], bias[:, :], ALU.add))
                nc.vector.tensor_tensor(k.x[:, b, :], k.x[:, b, :], yb[:, b % 2, :], ALU.add)\
                  .then_inc(S["added"], 1)




def program(nc, dram, out):
    with ExitStack() as ctx:
        k = Core(nc, ctx, dram)
        cross_attention_over_heads(k, dram["x"], dram["ctxT"], {
            "Wq": dram["a0_wq"], "Wk": dram["a0_wk"], "Wv": dram["a0_wv"], "bqk": dram["a0_bqk"],
            "bv": dram["a0_bv"]})
        ranked_lora(k, {"AG": dram["f0_ag"], "gate_b": dram["f0_gate_b"], "W": dram["f0_w"], "B": dram["f0_bt"],
                        "b": dram["f0_b"]})
        grouped_attention(k, dram)
        mixture_of_experts(k, dram)
        autocorrelation(k, dram)
        scaled_linear(k, dram)
        token_attention(k, dram)
        packed_linear(k, dram, out)


def rows128(a):
    return np.ascontiguousarray(a.reshape(-1, P, a.shape[-1]).transpose(1, 0, 2))


def columns(a):
    return np.ascontiguousarray(a.reshape(-1, P).T)


def rope_table(positions, dim, theta):
    freq = (1.0 / np.float32(theta) ** (np.arange(0, dim, 2, dtype=np.float32) / np.float32(dim))).astype(np.float32)
    angle = np.arange(positions, dtype=np.float32)[:, None] * freq
    c, s = np.cos(angle), np.sin(angle)
    return rows128(np.concatenate([c, c, s, -s], axis=1).astype(np.float32))


def shares(vision):
    text = np.arange(P) >= vision
    return np.stack([text / ((P - vision) * D), ~text / (vision * D)], axis=1).astype(np.float32)


def transform_tables():
    t, f = np.arange(P)[:, None], np.arange(P // 2)[None, :]
    angle = 2 * np.pi * t * f / P
    cos, sin, flip = np.cos(angle), np.sin(angle), np.cos(np.pi * t)
    to_q = np.concatenate([cos, flip, sin[:, 1:]], axis=1)
    to_k2 = np.concatenate([sin, 0 * flip, -cos[:, 1:]], axis=1)
    from_1 = np.concatenate([0.5 * cos[:, :1], cos[:, 1:], 0.5 * flip, cos[:, 1:]], axis=1).T * (2 / P)
    from_2 = np.concatenate([0 * flip, -sin[:, 1:], 0 * flip, -sin[:, 1:]], axis=1).T * (2 / P)
    odd = 2 * np.pi * t * (np.arange(P)[None, :] + 0.5) / (2 * P)
    wc, ws = np.cos(odd), np.sin(odd)
    vc, vs = wc.copy(), ws.copy()
    vc[-1], vs[-1] = -wc[:-1].sum(axis=0), -ws[:-1].sum(axis=0)
    last = np.zeros((P, P))
    last[-1] = 1.0
    tables = [to_q, to_k2, vc, vs, from_1, from_2, wc, ws, wc.T / P, -ws.T / P, ws.T / P, last]
    return np.stack(tables, axis=1).astype(np.float32)


def layouts(i):
    ctx = i["ctx_4096"].reshape(TOK, D)
    ctxT = rows128(ctx.T)
    channel = np.arange(P)
    row0 = np.zeros((P, P), np.float32)
    row0[0] = 1.0
    return {
        "ident": np.eye(P, dtype=np.float32),
        "x": i["x"],
        "ctxT": np.stack([ctxT[:, :, :512], ctxT[:, :, 512:]]),
        "a0_wq": rows128(i["L0_xattn_Wq"].T), "a0_wk": rows128(i["L0_xattn_Wk"].T),
        "a0_wv": rows128(i["L0_xattn_Wv"].T),
        "a0_bqk": np.stack([columns(i["L0_xattn_bq"]), columns(i["L0_xattn_bk"])], axis=1),
        "a0_bv": i["L0_xattn_bv"],
        "f0_w": rows128(i["L0_ffn_W"].T), "f0_b": i["L0_ffn_b"],
        "f0_ag": rows128(np.concatenate([i["L0_ffn_A"], i["L0_ffn_gate_w"]]).T),
        "f0_gate_b": i["L0_ffn_gate_b"], "f0_bt": i["L0_ffn_B"].T,
        "pos": i["pos_BxS2"].reshape(TOK), "mask": i["mask_BxSxS2_ik0"].transpose(1, 0, 2),
        "a1_iota": columns(np.arange(512, dtype=np.float32)), "a1_rope": rope_table(512, P, 10000.0),
        "a1_wq": i["L1_xattn_Wq"].reshape(C, P, 8, 4, P).transpose(2, 3, 1, 0, 4),
        "a1_wk": i["L1_xattn_Wk"].reshape(C, P, 8, P).transpose(2, 1, 0, 3),
        "a1_wv": i["L1_xattn_Wv"].reshape(C, P, 8, P).transpose(1, 2, 0, 3),
        "f1_gw": rows128(i["L1_ffn_gate_w"][:D]), "f1_gw_ratio": i["L1_ffn_gate_w"][D], "f1_gb": i["L1_ffn_gate_b"],
        "f1_ones": np.ones((P, P), np.float32), "f1_row0": row0, "f1_share": shares(int(P * 0.3)),
        "f1_b1": i["L1_ffn_b1"].reshape(3, C, P).transpose(2, 0, 1), "f1_b2": i["L1_ffn_b2"],
        "f1_w1": i["L1_ffn_w1"].reshape(3, C, P, D).transpose(0, 2, 1, 3),
        "f1_w2": i["L1_ffn_w2"].reshape(3, C, P, D).transpose(0, 2, 1, 3),
        "ctx": i["ctx_4096"], "a2_table": transform_tables(),
        "f2_w": rows128(i["L2_ffn_weight"].T), "f2_scale": i["L2_ffn_weight_scale_inv"].T.reshape(C * C),
        "f2_bias": i["L2_ffn_bias"],
        "a3_w": np.stack([i[f"L3_xattn_W{n}"].T for n in "qkvm"], axis=1),
        "a3_proj": rows128(np.concatenate([i["L3_xattn_proj_k"]] + [i["L3_xattn_proj_v"]] * 4, axis=1)),
        "a3_bcol": np.stack([i["L3_xattn_bq"], i["L3_xattn_bm"]], axis=1),
        "a3_brow": np.stack([i["L3_xattn_bk"], i["L3_xattn_bv"]])[None],
        "a3_ones": np.ones((P, 1), np.float32),
        "a3_of_head": (channel[:, None] % 16 == np.arange(16)).astype(np.float32),
        "a3_of_pair": (4 * np.arange(4)[None, :, None] + channel[:, None, None] // 32
                       == channel[None, None, :] % 16).astype(np.float32),
        "f3_words": np.tile(i["L3_ffn_qweight"], (2, 1)),
        "f3_zwords": np.tile(np.repeat(i["L3_ffn_qzeros"], 16, axis=0), (2, 1)),
        "f3_scale": np.tile(np.repeat(i["L3_ffn_scales"], 16, axis=0), (2, 1)), "f3_bias": i["L3_ffn_bias"],
        "a1_wo": i["L1_xattn_Wo"].reshape(8, 4, P, D).transpose(0, 2, 1, 3),
    }


def kernel(**inputs):
    import concourse.bacc as bacc
    from concourse.bass_utils import run_bass_kernel_spmd

    nc = bacc.Bacc("TRN2", target_bir_lowering=False, num_devices=1)
    arrays, dram = {}, {}
    for name, a in layouts({n: np.asarray(a) for n, a in inputs.items()}).items():
        a = np.ascontiguousarray(a)
        arrays[f"in_{name}"] = a
        dram[name] = nc.dram_tensor(f"in_{name}", a.shape, mybir.dt.from_np(a.dtype), kind="ExternalInput").ap()
    out = nc.dram_tensor("out_x", (NB, P, D), F32, kind="ExternalOutput").ap()
    program(nc, dram, out)
    r = run_bass_kernel_spmd(nc, [arrays], core_ids=[0])
    return r.results[0]["out_x"]
```

```python
import numpy as np

import concourse.bass as bass
from concourse import mybir
from contextlib import ExitStack

F32 = mybir.dt.float32
F16 = mybir.dt.float16
I32 = mybir.dt.int32
F32R = mybir.dt.float32r
ALU = mybir.AluOpType
ACT = mybir.ActivationFunctionType
AX = mybir.AxisListType

P = 128
NB = 8
D = 512
C = D // P
TOK = NB * P
EPS = 1e-5
LOWEST = -3.0e38


HI, LO = 0, 1


def after_first(eng, sem, value):
    if isinstance(value, int) and value <= 0:
        return
    eng.wait_ge(sem, value)


def split_product(nc, out, weights, moving, first=True, last=True):
    nc.tensor.matmul(out, weights[HI], moving[HI], start=first, stop=False)
    nc.tensor.matmul(out, weights[HI], moving[LO], start=False, stop=False)
    return nc.tensor.matmul(out, weights[LO], moving[HI], start=False, stop=last)


def parts(tile, *at):
    return [tile[(slice(None), part, *at)] for part in (HI, LO)]


def low_part(engine, out, whole, high):
    return engine.tensor_tensor(out, whole, high.bitcast(F32), ALU.subtract)


class Link:

    def __init__(self, eng, sem, n=0):
        self.eng, self.sem, self.n = eng, sem, n

    def __call__(self, ins):
        self.n += 1
        ins.then_inc(self.sem, 1)
        self.eng.wait_ge(self.sem, self.n)


class Core:

    def __init__(self, nc, ctx, dram):
        self.nc, self.ctx, self.dram = nc, ctx, dram
        self.x = self.sb(ctx, "x", [P, NB, D])
        self.ctxT = self.sb(ctx, "ctxT", [P, C, TOK])
        self.ident = self.sb(ctx, "ident", [P, P])
        self.xn = self.sb(ctx, "xn", [P, 2, D])
        self.stats = self.sb(ctx, "stats", [P, NB, 6])
        self.meanvar = self.sb(ctx, "meanvar", [P, NB, 2])
        self.varpe = self.sb(ctx, "varpe", [P, NB])
        self.rstd = self.sb(ctx, "rstd", [P, NB])
        self.mhalf = self.sb(ctx, "mhalf", [P, 1])
        self.ps = ctx.enter_context(nc.psum_tensor("ps", [P, 8, 512], F32))
        self.var_ready = self.sem("var_ready")
        self.rstd_ready = self.sem("rstd_ready")
        self.xn_ready = self.sem("xn_ready")
        self.xt_ready = self.sem("xt_ready")
        self.dve_own = self.sem("dve_own")
        self.pool_own = self.sem("pool_own")
        self.loaded = {}
        self.dve_count = 0
        self.pool_count = 0

    def sb(self, ctx, name, shape, dt=F32):
        return ctx.enter_context(self.nc.sbuf_tensor(name, shape, dt))

    def sem(self, name):
        return self.ctx.enter_context(self.nc.semaphore(name))

    def load(self, eng, name, dst, src):
        if name not in self.loaded:
            self.loaded[name] = [self.sem(f"{name}_loaded"), 0]
        sem, _ = self.loaded[name]
        eng.dma_start(dst, src).then_inc(sem, 16)
        self.loaded[name][1] += 16

    def arrived(self, eng, name):
        eng.wait_ge(*self.loaded[name])

    def row_stats(self, dve, link, b):
        link(self.nc.vector.bn_stats(self.stats[:, b, :], self.x[:, b, :]))
        self.nc.vector.bn_aggr(self.meanvar[:, b, :], self.stats[:, b, :]).then_inc(self.var_ready, 1)

    def row_rstd(self, pool, link, layer, b):
        pool.wait_ge(self.var_ready, NB * layer + b + 1)
        link(self.nc.gpsimd.tensor_scalar(self.varpe[:, b:b + 1], self.meanvar[:, b, 1:2], EPS, None, ALU.add))
        self.nc.gpsimd.tensor_tensor(self.rstd[:, b:b + 1], self.varpe[:, b:b + 1], self.mhalf[:, :],
                                     ALU.pow).then_inc(self.rstd_ready, 1)

    def normed(self, dve, layer, b, out, row=None):
        dve.wait_ge(self.rstd_ready, NB * layer + b + 1)
        return self.nc.vector.tensor_scalar(out, self.x[:, b, :] if row is None else row, self.meanvar[:, b, 0:1],
                                            self.rstd[:, b:b + 1], ALU.subtract, ALU.mult)

    def transpose4(self, bank, src):
        for c in range(C):
            last = self.nc.tensor.transpose(self.ps[:, bank, c * P:(c + 1) * P], src[:, c * P:(c + 1) * P],
                                            self.ident[:, :])
        return last


def row_block(ap):
    return ap.rearrange("(c p) n -> p c n", p=P)


def cross_attention_over_heads(k, x_dram, ctxT_dram, w, out=None):
    nc = k.nc
    H, HD = 16, 32
    R = P // HD
    scale = 1.0 / float(np.sqrt(HD))
    with ExitStack() as ctx:
        bqk = k.sb(ctx, "a0_bqk", [P, 2, C])
        bv = k.sb(ctx, "a0_bv", [P, D])
        qT = k.sb(ctx, "a0_qT", [P, C, TOK])
        kT = k.sb(ctx, "a0_kT", [P, C, TOK])
        v = k.sb(ctx, "a0_v", [P, NB, D])
        rowmax = k.sb(ctx, "a0_rowmax", [P, NB, P])
        allmax = k.sb(ctx, "a0_allmax", [P, P])
        total = k.sb(ctx, "a0_total", [P, P])
        inv = k.sb(ctx, "a0_inv", [P, P])
        with ExitStack() as early:
            c_parts = k.sb(early, "a0_ctx", [P, 2, C, TOK], F32R)
            x_parts = k.sb(early, "a0_xT", [P, 2, C, TOK], F32R)
            w_parts = k.sb(early, "a0_w", [P, 2, 2, C, D], F32R)
            whole = k.sb(early, "a0_whole", [P, 2, C, D])
        apart = k.sb(ctx, "a0_apart", [P, 2, C, R, P])
        E = k.sb(ctx, "a0_E", [P, NB, C, R, P])
        S = {n: k.sem("a0_" + n) for n in (
            "xt_copied", "kq_ready", "kq_copied", "v_ready",
            "v_copied", "scores_ready", "scores_copied", "shifted", "exp_ready", "sum_ready", "probs_ready",
            "out_ready", "added", "zeroed", "apart_pool", "apart_dve",
            "w_high", "wk_low", "w_low", "ctx_high", "ctx_low", "xt_low")}
        WK, WV, WQ = 0, 1, 2
        PE_ROWS = 4
        block = ctx.enter_context(nc.Block())
        ps = k.ps

        def part_heads(eng, engine, sem, heads, b):
            eng.wait_ge(S["kq_copied"], 12 + 4 * (b // 4))
            after_first(eng, S["scores_ready"], b - 1)
            for r in heads:
                rows = slice(HD * r, HD * (r + 1))
                engine.tensor_copy(apart[rows, b % 2, :, r, :], qT[rows, :, b * P:(b + 1) * P]).then_inc(sem, 1)

        def sum_pair(eng, engine, sem, slot, b):
            eng.wait_ge(S["exp_ready"], b + 2)
            e0, e1 = (E[:, row, :, :, :].rearrange("p c r q -> p (c r q)") for row in (b, b + 1))
            engine.tensor_tensor(apart[:, slot, :, :, :].rearrange("p c r q -> p (c r q)"), e0, e1, ALU.add)\
              .then_inc(sem, 1)

        def w_low(eng, engine, sem, i):
            eng.wait_ge(S["w_high"], i + 1)
            low_part(engine, w_parts[:, LO, i % 2, :, :], whole[:, i % 2, :, :], w_parts[:, HI, i % 2, :, :])\
              .then_inc(sem, 1)

        @block.sync
        def _(sp):
            k.load(sp, "a0_w0", whole[:, 0, :, :], w["Wk"])
            k.load(sp, "ctxT0", k.ctxT[:, :, 0:512], ctxT_dram[0])
            k.load(sp, "a0_k", k.ident[:, :], k.dram["ident"])
            k.load(sp, "a0_k", bqk[:, :, :], w["bqk"])
            k.load(sp, "ctxT1", k.ctxT[:, :, 512:TOK], ctxT_dram[1])
            k.load(sp, "a0_w1", whole[:, 1, :, :], w["Wv"])
            k.load(sp, "a0_v", bv[:, :], w["bv"].partition_broadcast(P))
            for b in range(NB):
                k.load(sp, f"x{b}", k.x[:, b, :], x_dram[b])
            sp.wait_ge(S["wk_low"], 1)
            k.load(sp, "a0_w2", whole[:, 0, :, :], w["Wq"])

        @block.gpsimd
        def _(pool):
            link = Link(pool, k.pool_own)
            link(nc.gpsimd.memset(k.mhalf[:, :], -0.5))
            w_low(pool, nc.gpsimd, S["w_low"], WV)
            for b in range(NB):
                k.row_rstd(pool, link, 0, b)
            w_low(pool, nc.gpsimd, S["w_low"], WQ)
            pool.wait_ge(S["v_ready"], NB)
            nc.gpsimd.memset(apart[:, :, :, :, :].rearrange("p s c r q -> p (s c r q)"), 0.0)\
              .then_inc(S["zeroed"], 1)
            pool.wait_ge(S["zeroed"], 1)
            for b in range(NB):
                part_heads(pool, nc.gpsimd, S["apart_pool"], range(1), b)
            sum_pair(pool, nc.gpsimd, S["apart_pool"], 0, PE_ROWS)
            for b in range(NB):
                k.row_rstd(pool, link, 1, b)
            k.pool_count = link.n

        @block.tensor
        def _(pe):
            def project(u, bank, weight, acts, o, half):
                if u >= 2:
                    pe.wait_ge(S["kq_copied"], u - 1)
                for c in range(C):
                    last = split_product(nc, ps[:, bank, :],
                                         parts(w_parts, weight % 2, c, slice(o * P, (o + 1) * P)),
                                         parts(acts, c, slice(half * 512, (half + 1) * 512)), c == 0, c == C - 1)
                last.then_inc(S["kq_ready"], 1)

            def turn_rows(b):
                pe.wait_ge(k.xn_ready, b + 1)
                if b >= 2:
                    pe.wait_ge(S["xt_low"], b - 1)
                k.transpose4(4 + b % 2, k.xn[:, b % 2, :]).then_inc(k.xt_ready, 1)

            pe.wait_ge(S["wk_low"], 1)
            u = 0
            for half in range(2):
                pe.wait_ge(S["ctx_low"], half + 1)
                for o in range(C):
                    project(u, u % 2, WK, c_parts, o, half)
                    if u >= 1:
                        turn_rows(u - 1)
                    u += 1
            k.arrived(pe, "a0_k")
            turn_rows(NB - 1)
            pe.wait_ge(S["w_low"], WV)
            for b in range(NB):
                if b >= 2:
                    pe.wait_ge(S["v_copied"], b - 1)
                for c in range(C):
                    last = split_product(nc, ps[:, 2 + b % 2, :], parts(c_parts, c, slice(b * P, (b + 1) * P)),
                                         parts(w_parts, WV % 2, c), c == 0, c == C - 1)
                last.then_inc(S["v_ready"], 1)
            pe.wait_ge(S["w_low"], WQ)
            for half in range(2):
                pe.wait_ge(S["xt_low"], 4 * half + 4)
                for o in range(C):
                    project(u, u % 2, WQ, x_parts, o, half)
                    u += 1
            pe.wait_ge(S["kq_copied"], 16)
            pe.wait_ge(S["v_copied"], NB)
            for b in range(NB):
                if b >= 2:
                    pe.wait_ge(S["scores_copied"], b - 1)
                pe.wait_ge(S["apart_pool"], b + 1)
                pe.wait_ge(S["apart_dve"], (R - 1) * (b + 1))
                for c in range(C):
                    last = nc.tensor.matmul(ps[:, 4 * (b % 2) + c, :], kT[:, c, b * P:(b + 1) * P],
                                            apart[:, b % 2, c, :, :].rearrange("p r q -> p (r q)"),
                                            start=True, stop=True)
                last.then_inc(S["scores_ready"], 1)
            pe.wait_ge(S["scores_copied"], NB)
            def add_heads(heads, first=False, last=False):
                for c in range(C):
                    done = nc.tensor.matmul(ps[:, 0, :], k.ident[:, :], heads[:, c, :, :].rearrange("p r q -> p (r q)"),
                                            start=first and c == 0, stop=last and c == C - 1)
                return done

            for b in range(PE_ROWS):
                pe.wait_ge(S["exp_ready"], b + 1)
                add_heads(E[:, b, :, :, :], first=b == 0)
            pe.wait_ge(S["apart_pool"], NB + 1)
            add_heads(apart[:, 0, :, :, :])
            pe.wait_ge(S["apart_dve"], (R - 1) * NB + 1)
            add_heads(apart[:, 1, :, :, :], last=True).then_inc(S["sum_ready"], 1)
            for b in range(NB):
                pe.wait_ge(S["probs_ready"], b + 1)
                if b >= 2:
                    pe.wait_ge(S["added"], b - 1)
                o = ps[:, 2 + b % 2, :].rearrange("p (d h) -> p h d", h=H)
                for c in range(C):
                    for r in range(R):
                        h = R * c + r
                        last = nc.tensor.matmul(o[:, h, :], E[:, b, c, r, :], v[:, b, h * HD:(h + 1) * HD],
                                                start=True, stop=True)
                last.then_inc(S["out_ready"], 1)

        @block.scalar
        def _(act):
            def copy_kq(u, dst, which, o, half):
                act.wait_ge(S["kq_ready"], u + 1)
                nc.scalar.activation(dst[:, o, half * 512:(half + 1) * 512], ps[:, u % 2, :], ACT.Identity,
                                     bias=bqk[:, which, o:o + 1]).then_inc(S["kq_copied"], 1)

            def w_high(i):
                k.arrived(act, f"a0_w{i}")
                if i == WQ:
                    act.wait_ge(S["kq_ready"], 8)
                nc.scalar.copy(w_parts[:, HI, i % 2, :, :], whole[:, i % 2, :, :]).then_inc(S["w_high"], 1)

            def ctx_high(half):
                tok = slice(half * 512, (half + 1) * 512)
                k.arrived(act, f"ctxT{half}")
                nc.scalar.copy(c_parts[:, HI, :, tok], k.ctxT[:, :, tok]).then_inc(S["ctx_high"], 1)

            w_high(WK)
            ctx_high(0)
            ctx_high(1)
            w_high(WV)
            k.arrived(act, "a0_k")
            def copy_x(b):
                act.wait_ge(k.xt_ready, b + 1)
                nc.scalar.copy(x_parts[:, HI, :, b * P:(b + 1) * P],
                               ps[:, 4 + b % 2, :].rearrange("p (c t) -> p c t", c=C)).then_inc(S["xt_copied"], 1)

            for u in range(8):
                copy_kq(u, kT, 1, u % C, u // C)
                if u >= 1:
                    copy_x(u - 1)
            copy_x(NB - 1)
            w_high(WQ)
            for u in range(8):
                copy_kq(8 + u, qT, 0, u % C, u // C)
            for b in range(NB):
                act.wait_ge(S["scores_ready"], b + 1)
                nc.scalar.copy(E[:, b, :, :, :].rearrange("p c r q -> p (c r q)"),
                               ps[:, 4 * (b % 2):4 * (b % 2) + 4, :].rearrange("p c n -> p (c n)"))\
                  .then_inc(S["scores_copied"], 1)
            for b in range(NB):
                act.wait_ge(S["shifted"], b + 1)
                e = E[:, b, :, :, :].rearrange("p c r q -> p (c r q)")
                nc.scalar.activation(e, e, ACT.Exp, scale=scale).then_inc(S["exp_ready"], 1)

        @block.vector
        def _(dve):
            link = Link(dve, k.dve_own)

            def x_low(b):
                tok = slice(b * P, (b + 1) * P)
                dve.wait_ge(S["xt_copied"], b + 1)
                low_part(nc.vector, x_parts[:, LO, :, tok], ps[:, 4 + b % 2, :].rearrange("p (c t) -> p c t", c=C),
                         x_parts[:, HI, :, tok]).then_inc(S["xt_low"], 1)

            w_low(dve, nc.vector, S["wk_low"], WK)
            for half in range(2):
                tok = slice(half * 512, (half + 1) * 512)
                dve.wait_ge(S["ctx_high"], half + 1)
                low_part(nc.vector, c_parts[:, LO, :, tok], k.ctxT[:, :, tok], c_parts[:, HI, :, tok])\
                  .then_inc(S["ctx_low"], 1)
            for b in range(NB):
                k.arrived(dve, f"x{b}")
                k.row_stats(dve, link, b)
                if b >= 1:
                    if b >= 3:
                        dve.wait_ge(k.xt_ready, b - 2)
                    k.normed(dve, 0, b - 1, k.xn[:, (b - 1) % 2, :]).then_inc(k.xn_ready, 1)
                    if b >= 2:
                        x_low(b - 2)
            dve.wait_ge(k.xt_ready, NB - 2)
            k.normed(dve, 0, NB - 1, k.xn[:, (NB - 1) % 2, :]).then_inc(k.xn_ready, 1)
            x_low(NB - 2)
            x_low(NB - 1)
            k.arrived(dve, "a0_v")
            for b in range(NB):
                dve.wait_ge(S["v_ready"], b + 1)
                nc.vector.tensor_tensor(v[:, b, :], ps[:, 2 + b % 2, :], bv[:, :], ALU.add).then_inc(S["v_copied"], 1)
            dve.wait_ge(S["zeroed"], 1)
            for b in range(2):
                part_heads(dve, nc.vector, S["apart_dve"], range(1, R), b)
            for b in range(NB):
                if b + 2 < NB:
                    part_heads(dve, nc.vector, S["apart_dve"], range(1, R), b + 2)
                dve.wait_ge(S["scores_copied"], b + 1)
                nc.vector.tensor_reduce(rowmax[:, b, :], E[:, b, :, :, :].rearrange("p c r q -> p q (c r)"),
                                        AX.X, ALU.max).then_inc(k.dve_own, 1)
                link.n += 1
            dve.wait_ge(k.dve_own, link.n)
            link(nc.vector.tensor_reduce(allmax[:, :], rowmax[:, :, :].rearrange("p b q -> p q b"), AX.X, ALU.max))
            heads = [P, R * C, P]
            for b in range(NB):
                e = E[:, b, :, :, :].rearrange("p c r q -> p (c r) q")
                nc.vector.tensor_tensor(e, e, allmax[:, :].unsqueeze(1).to_broadcast(heads), ALU.subtract)\
                  .then_inc(S["shifted"], 1)
            sum_pair(dve, nc.vector, S["apart_dve"], 1, NB - 2)
            dve.wait_ge(S["sum_ready"], 1)
            link(nc.vector.tensor_reduce(total[:, :], ps[:, 0, :].rearrange("p (r q) -> p q r", r=R), AX.X, ALU.add))
            link(nc.vector.reciprocal(inv[:, :], total[:, :]))

            def divide(b):
                e = E[:, b, :, :, :].rearrange("p c r q -> p (c r) q")
                nc.vector.tensor_tensor(e, e, inv[:, :].unsqueeze(1).to_broadcast(heads), ALU.mult)\
                  .then_inc(S["probs_ready"], 1)

            divide(0)
            for b in range(NB):
                if b + 1 < NB:
                    divide(b + 1)
                dve.wait_ge(S["out_ready"], b + 1)
                nc.vector.tensor_tensor(k.x[:, b, :], k.x[:, b, :], ps[:, 2 + b % 2, :], ALU.add)\
                  .then_inc(S["added"], 1)
                dve.wait_ge(S["added"], b + 1)
                k.row_stats(dve, link, b)
            k.dve_count = link.n


def ranked_lora(k, w):
    nc, ps = k.nc, k.ps
    RANKS = (8, 16, 32, 64)
    NR, MAXR = len(RANKS), RANKS[-1]
    with ExitStack() as ctx:
        wt = k.sb(ctx, "f0_w", [P, C, D])
        ag = k.sb(ctx, "f0_ag", [P, C, MAXR + NR])
        bt = k.sb(ctx, "f0_bt", [MAXR, D])
        bias = k.sb(ctx, "f0_bias", [P, D])
        gate_b = k.sb(ctx, "f0_gate_b", [P, NR])
        xT = k.sb(ctx, "f0_xT", [P, NB, C, P])
        low = k.sb(ctx, "f0_low", [P, NB, MAXR + NR])
        gated = k.sb(ctx, "f0_gated", [P, NB, MAXR])
        scores = k.sb(ctx, "f0_scores", [P, NB, NR])
        before = k.sb(ctx, "f0_before", [P, NB, NR])
        after = k.sb(ctx, "f0_after", [P, NB, NR])
        keep = k.sb(ctx, "f0_keep", [P, NB, NR])
        gatedT = k.sb(ctx, "f0_gatedT", [MAXR, 2, P])
        S = {n: k.sem("f0_" + n) for n in (
            "xt_copied", "low_ready", "low_copied", "biased", "gated", "gt_ready",
            "gt_copied", "out_ready", "added")}
        block = ctx.enter_context(nc.Block())

        @block.sync
        def _(sp):
            k.load(sp, "f0_low", ag[:, :, :], w["AG"])
            k.load(sp, "f0_low", gate_b[:, :], w["gate_b"].partition_broadcast(P))
            k.load(sp, "f0_w", wt[:, :, :], w["W"])
            k.load(sp, "f0_out", bt[:, :], w["B"])
            k.load(sp, "f0_out", bias[:, :], w["b"].partition_broadcast(P))

        @block.gpsimd
        def _(pool):
            link = Link(pool, k.pool_own, k.pool_count)
            k.arrived(pool, "f0_out")
            for b in range(NB):
                pool.wait_ge(k.xn_ready, NB + b + 1)
                nc.gpsimd.tensor_tensor(k.x[:, b, :], k.x[:, b, :], bias[:, :], ALU.add).then_inc(S["biased"], 1)
            for b in range(NB):
                k.row_rstd(pool, link, 2, b)
            k.pool_count = link.n

        @block.tensor
        def _(pe):
            def low_rank(b):
                pe.wait_ge(S["xt_copied"], b + 1)
                if b >= 2:
                    pe.wait_ge(S["low_copied"], b - 1)
                for c in range(C):
                    last = nc.tensor.matmul(ps[:, b % 2, 0:MAXR + NR], xT[:, b, c, :], ag[:, c, :],
                                            start=c == 0, stop=c == C - 1)
                last.then_inc(S["low_ready"], 1)

            for b in range(NB):
                pe.wait_ge(k.xn_ready, NB + b + 1)
                if b >= 2:
                    pe.wait_ge(S["xt_copied"], b - 1)
                k.transpose4(6 + b % 2, k.xn[:, b % 2, :]).then_inc(k.xt_ready, 1)
                if b == 0:
                    k.arrived(pe, "f0_low")
                else:
                    low_rank(b - 1)
            low_rank(NB - 1)
            k.arrived(pe, "f0_w")
            for i in range(NB + 2):
                if i < NB:
                    if i >= 4:
                        pe.wait_ge(S["added"], i - 3)
                    for c in range(C):
                        nc.tensor.matmul(ps[:, 2 + i % 4, :], xT[:, i, c, :], wt[:, c, :], start=c == 0, stop=False)
                if 1 <= i <= NB:
                    b = i - 1
                    if b == 0:
                        pe.wait_ge(S["gated"], NR)
                    if b >= 2:
                        pe.wait_ge(S["gt_copied"], b - 1)
                    nc.tensor.transpose(ps[0:MAXR, 6 + b % 2, 0:P], gated[:, b, :], k.ident[:, :])\
                      .then_inc(S["gt_ready"], 1)
                if i >= 2:
                    b = i - 2
                    if b == 0:
                        k.arrived(pe, "f0_out")
                    pe.wait_ge(S["gt_copied"], b + 1)
                    nc.tensor.matmul(ps[:, 2 + b % 4, :], gatedT[:, b % 2, :], bt[:, :], start=False, stop=True)\
                      .then_inc(S["out_ready"], 1)

        @block.scalar
        def _(act):
            for b in range(NB):
                act.wait_ge(k.xt_ready, NB + b + 1)
                nc.scalar.copy(xT[:, b, :, :].rearrange("p c t -> p (c t)"), ps[:, 6 + b % 2, :])\
                  .then_inc(S["xt_copied"], 1)
                if b >= 1:
                    act.wait_ge(S["low_ready"], b)
                    nc.scalar.copy(low[:, b - 1, :], ps[:, (b - 1) % 2, 0:MAXR + NR]).then_inc(S["low_copied"], 1)
            act.wait_ge(S["low_ready"], NB)
            nc.scalar.copy(low[:, NB - 1, :], ps[:, (NB - 1) % 2, 0:MAXR + NR]).then_inc(S["low_copied"], 1)
            for b in range(NB):
                act.wait_ge(S["gt_ready"], b + 1)
                if b >= 2:
                    act.wait_ge(S["out_ready"], b - 1)
                nc.scalar.copy(gatedT[:, b % 2, :], ps[0:MAXR, 6 + b % 2, 0:P]).then_inc(S["gt_copied"], 1)

        @block.vector
        def _(dve):
            link = Link(dve, k.dve_own, k.dve_count)
            for b in range(NB):
                if b >= 2:
                    dve.wait_ge(k.xt_ready, NB + b - 1)
                k.normed(dve, 1, b, k.xn[:, b % 2, :]).then_inc(k.xn_ready, 1)
            k.arrived(dve, "f0_low")
            dve.wait_ge(S["low_copied"], NB)
            link(nc.vector.tensor_tensor(scores[:, :, :], low[:, :, MAXR:MAXR + NR],
                                         gate_b[:, :].unsqueeze(1).to_broadcast([P, NB, NR]), ALU.add))
            link(nc.vector.tensor_copy(before[:, :, 1:2], scores[:, :, 0:1]))
            link(nc.vector.tensor_copy(after[:, :, NR - 1:NR], scores[:, :, NR - 1:NR]))
            for t in range(2, NR):
                link(nc.vector.tensor_tensor(before[:, :, t:t + 1], before[:, :, t - 1:t], scores[:, :, t - 1:t],
                                             ALU.max))
            for t in range(NR - 2, 0, -1):
                link(nc.vector.tensor_tensor(after[:, :, t:t + 1], after[:, :, t + 1:t + 2], scores[:, :, t:t + 1],
                                             ALU.max))
            link(nc.vector.tensor_tensor(keep[:, :, 1:NR], before[:, :, 1:NR], after[:, :, 1:NR], ALU.is_lt))
            nc.vector.tensor_copy(gated[:, :, 0:RANKS[0]], low[:, :, 0:RANKS[0]]).then_inc(S["gated"], 1)
            for t in range(1, NR):
                lo, hi = RANKS[t - 1], RANKS[t]
                nc.vector.tensor_tensor(gated[:, :, lo:hi], low[:, :, lo:hi],
                                        keep[:, :, t:t + 1].to_broadcast([P, NB, hi - lo]), ALU.mult)\
                  .then_inc(S["gated"], 1)
            for b in range(NB):
                dve.wait_ge(S["out_ready"], b + 1)
                dve.wait_ge(S["biased"], b + 1)
                nc.vector.tensor_tensor(k.x[:, b, :], k.x[:, b, :], ps[:, 2 + b % 4, :], ALU.add)\
                  .then_inc(S["added"], 1)
                dve.wait_ge(S["added"], b + 1)
                k.row_stats(dve, link, b)
            k.dve_count = link.n


def grouped_attention(k, dram):
    nc, ps = k.nc, k.ps
    G, R, HD = 8, 4, P
    HALF = TOK // 2
    scale = 1.0 / float(np.sqrt(HD))
    MAXPOS = dram["a1_rope"].shape[1] * P
    QK_BANK, V_BANK, S_BANK, PT_BANK, OT_BANK, Y_BANK = 0, 2, 3, 4, 5, 6
    with ExitStack() as ctx:
        cos = k.sb(ctx, "a1_cos", [P, TOK])
        sin = k.sb(ctx, "a1_sin", [P, TOK])
        mask = k.sb(ctx, "a1_mask", [P, NB, P], I32)
        hidden = k.sb(ctx, "a1_hidden", [P, NB, P], I32)
        fill = k.sb(ctx, "a1_fill", [P, P])
        gate = k.sb(ctx, "a1_gate", [P, 1])
        wq = k.sb(ctx, "a1_wq", [P, 2, R, C, HD], F32R)
        wk = k.sb(ctx, "a1_wk", [P, C, HD])
        wv = k.sb(ctx, "a1_wv", [P, G, C, HD])
        one = k.sb(ctx, "a1_one", [P, 1])
        piece = k.sb(ctx, "a1_piece", [P, 2, D])
        xT = k.sb(ctx, "a1_xT", [P, 2, C, TOK], F32R)
        qT = k.sb(ctx, "a1_qT", [P, R, TOK])
        kT = k.sb(ctx, "a1_kT", [P, TOK])
        v = k.sb(ctx, "a1_v", [P, NB, HD])
        turned = k.sb(ctx, "a1_turned", [P, 2, 2, HALF])
        negmax = k.sb(ctx, "a1_negmax", [P, 2, R])
        bias = k.sb(ctx, "a1_bias", [P, 2, R])
        total = k.sb(ctx, "a1_total", [P, 2, R])
        inv = k.sb(ctx, "a1_inv", [P, 2, R])
        prob = k.sb(ctx, "a1_prob", [P, 2, R, P])
        probT = k.sb(ctx, "a1_probT", [P, 2, R * P])
        oT = k.sb(ctx, "a1_oT", [P, 2, 2, R * P], F32R)
        with ExitStack() as tables:
            pos_i = k.sb(tables, "a1_pos_i", [P, TOK], I32)
            pos = k.sb(tables, "a1_pos", [P, TOK])
            wrap = k.sb(tables, "a1_wrap", [P, TOK])
            onehot = k.sb(tables, "a1_onehot", [P, MAXPOS // P, TOK])
            iota = k.sb(tables, "a1_iota", [P, MAXPOS // P])
            rope = k.sb(tables, "a1_rope", [P, MAXPOS // P, 2 * P])
        wo = k.sb(ctx, "a1_wo", [P, 2, 2, R, D], F32R)
        S = {n: k.sem("a1_" + n) for n in (
            "onehot_ready", "table_ready", "table_copied", "xt_copied", "qk_ready",
            "turned", "rotated", "v_ready", "v_copied", "s_ready", "bias_ready", "exp_ready", "prob_ready",
            "pt_ready", "pt_copied", "ot_ready", "ot_copied", "y_ready", "y_added", "wk_loaded",
            "split", "low_ready")}
        piece_loaded = [k.sem(f"a1_piece{n}_loaded") for n in range(2)]
        block = ctx.enter_context(nc.Block())

        def rotation(half, h):
            return 5 * half + 1 + h

        def before(g, b):
            if b > 0:
                return g, b - 1
            return None if isinstance(g, int) and g == 0 else (g - 1, NB - 1)

        @block.sync
        def _(sp):
            k.load(sp, "a1_tables", pos_i[:, :], dram["pos"].partition_broadcast(P))
            k.load(sp, "a1_tables", iota[:, :], dram["a1_iota"])
            k.load(sp, "a1_tables", rope[:, :, :], dram["a1_rope"])
            k.load(sp, "a1_mask", mask[:, :, :], dram["mask"])

            def load_wk(g):
                sp.dma_start(wk[:, :, :], dram["a1_wk"][g]).then_inc(S["wk_loaded"], 16)

            def load_piece(n, h, src):
                after_first(sp, S["split"], 2 * (n - 1))
                sp.dma_start(piece[:, h % 2, :], src).then_inc(piece_loaded[h % 2], 16)

            def load_wq(g, h):
                load_piece(2 * R * g + h, h, dram["a1_wq"][g, h].rearrange("p c n -> p (c n)"))

            def load_wo(g, h):
                load_piece(2 * R * g + R + h, h, dram["a1_wo"][g][:, h, :])

            for h in range(2):
                load_wq(0, h)
            load_wk(0)
            k.load(sp, "a1_wv", wv[:, :, :, :], dram["a1_wv"])
            for h in range(2, R):
                load_wq(0, h)

            def loads_in(g):
                for h in range(R):
                    load_wo(g, h)
                for h in range(2):
                    load_wq(g + 1, h)
                sp.wait_ge(S["qk_ready"], 10 * g + rotation(1, -1) + 1)
                load_wk(g + 1)
                for h in range(2, R):
                    load_wq(g + 1, h)

            loads_in(0)
            with sp.Fori(1, G - 1) as g:
                loads_in(g)
            for h in range(R):
                load_wo(G - 1, h)

        @block.gpsimd
        def _(pool):
            link = Link(pool, k.pool_own, k.pool_count)

            def rotate(g, half, h):
                r = 10 * g + rotation(half, h)
                slot = rotation(half, h) % 2
                pool.wait_ge(S["turned"], r + 1)
                after_first(pool, S["s_ready"], 8 * g - 8 + 4 * half + 4)
                dst = kT[:, half * HALF:(half + 1) * HALF] if h < 0 else qT[:, h, half * HALF:(half + 1) * HALF]
                nc.gpsimd.tensor_tensor(dst, turned[:, slot, 0, :], turned[:, slot, 1, :], ALU.add)\
                  .then_inc(S["rotated"], 1)

            def split(n, h, count, out):
                pool.wait_ge(piece_loaded[h % 2], 16 * count)
                nc.gpsimd.tensor_tensor(out[HI], piece[:, h % 2, :], one[:, :].to_broadcast([P, D]), ALU.mult).then_inc(S["split"], 1)
                pool.wait_ge(S["split"], 2 * n + 1)
                low_part(nc.gpsimd, out[LO], piece[:, h % 2, :], out[HI]).then_inc(S["split"], 1)

            def split_wq(g, h):
                split(2 * R * g + h, h, R * g + h // 2 + 1,
                      [wq[:, part, h, :, :].rearrange("p c n -> p (c n)") for part in (HI, LO)])

            def split_wo(g, slot, h):
                split(2 * R * g + R + h, h, R * g + R // 2 + h // 2 + 1, parts(wo, slot, h))

            def group(g, last=False):
                rotate(g, 0, -1)
                for h in range(R):
                    rotate(g, 0, h)
                    if h == 0:
                        after_first(pool, S["y_ready"], 8 * (g - 1))
                    split_wo(g, g % 2, h)
                rotate(g, 1, -1)
                for h in range(R):
                    rotate(g, 1, h)
                    if not last:
                        split_wq(g + 1, h)

            link(nc.gpsimd.memset(one[:, :], 1.0))
            for h in range(R):
                split_wq(0, h)
            pool.wait_ge(S["table_ready"], 4)
            group(0)
            group(1)
            with pool.Fori(2, G - 1) as g:
                group(g)
            group(G - 1, last=True)
            for b in range(NB):
                k.row_rstd(pool, link, 3, b)
            k.pool_count = link.n

        @block.tensor
        def _(pe):
            def unit(g, half, h):
                heads = [-1, 0] if h == 0 else [h]
                for j in heads:
                    r = 10 * g + rotation(half, j)
                    bank = QK_BANK + rotation(half, j) % 2
                    if half == 0 and j < 0:
                        pe.wait_ge(S["wk_loaded"], 16 * (g + 1))
                    elif half == 0:
                        pe.wait_ge(S["split"], 2 * (2 * R * g + j + 1))
                    after_first(pe, S["turned"], r - 1)
                    for c in range(C):
                        tok = slice(half * HALF, (half + 1) * HALF)
                        if j < 0:
                            last = nc.tensor.matmul(ps[:, bank, :], wk[:, c, :], k.ctxT[:, c, tok],
                                                    start=c == 0, stop=c == C - 1)
                        else:
                            last = split_product(nc, ps[:, bank, :], parts(wq, j, c), parts(xT, c, tok),
                                                 c == 0, c == C - 1)
                    last.then_inc(S["qk_ready"], 1)
                b = 4 * half + h
                after_first(pe, S["v_copied"], 8 * g + b)
                for c in range(C):
                    last = nc.tensor.matmul(ps[:, V_BANK, 0:HD], k.ctxT[:, c, b * P:(b + 1) * P], wv[:, g, c, :],
                                            start=c == 0, stop=c == C - 1)
                last.then_inc(S["v_ready"], 1)

            def output(g, b, heads):
                t = 8 * g + b
                if heads[0] == 0:
                    output_waits(g, b)
                for h in heads:
                    last = split_product(nc, ps[:, Y_BANK + b % 2, :],
                                         [oT[:, b % 2, part, h * P:(h + 1) * P] for part in (HI, LO)],
                                         parts(wo, g % 2, h), h == 0, h == R - 1)
                if heads[-1] == R - 1:
                    last.then_inc(S["y_ready"], 1)

            def output_waits(g, b):
                t = 8 * g + b
                if b == 0:
                    pe.wait_ge(S["split"], 4 * R * (g + 1))
                pe.wait_ge(S["low_ready"], NB + t + 1)
                after_first(pe, S["y_added"], t - 1)

            def step(g, b, project):
                t = 8 * g + b
                if b % 4 == 0:
                    pe.wait_ge(S["rotated"], 10 * g + 5 * (b // 4 + 1))
                after_first(pe, S["exp_ready"], R * t)
                for h in range(R):
                    last = nc.tensor.matmul(ps[:, S_BANK, h * P:(h + 1) * P], qT[:, h, b * P:(b + 1) * P],
                                            kT[:, b * P:(b + 1) * P], start=True, stop=True)
                last.then_inc(S["s_ready"], 1)
                if b < 4:
                    unit(g, 1, b)
                elif project:
                    unit(g + 1, 0, b - 4)
                if before(g, b):
                    output(*before(g, b), (0, 1))
                pe.wait_ge(S["prob_ready"], t + 1)
                after_first(pe, S["pt_copied"], t)
                k.transpose4(PT_BANK, prob[:, b % 2, :, :].rearrange("p h k -> p (h k)")).then_inc(S["pt_ready"], 1)
                if before(g, b):
                    output(*before(g, b), (2, 3))
                pe.wait_ge(S["pt_copied"], t + 1)
                pe.wait_ge(S["v_copied"], t + 1)
                if before(g, b):
                    pe.wait_ge(S["low_ready"], NB + t)
                nc.tensor.matmul(ps[:, OT_BANK, :], v[:, b, :], probT[:, b % 2, :], start=True, stop=True)\
                  .then_inc(S["ot_ready"], 1)

            k.arrived(pe, "a1_tables")
            pe.wait_ge(S["onehot_ready"], MAXPOS // P)
            for part in range(2):
                for half in range(2):
                    for c in range(MAXPOS // P):
                        last = nc.tensor.matmul(ps[:, 2 * part + half, :], rope[:, c, part * P:(part + 1) * P],
                                                onehot[:, c, half * HALF:(half + 1) * HALF],
                                                start=c == 0, stop=c == MAXPOS // P - 1)
                    last.then_inc(S["table_ready"], 1)
            for b in range(NB):
                pe.wait_ge(k.xn_ready, NB * 2 + b + 1)
                after_first(pe, S["low_ready"], b - 1)
                k.transpose4(4 + b % 2, k.xn[:, b % 2, :]).then_inc(k.xt_ready, 1)
            pe.wait_ge(S["table_copied"], 4)
            k.arrived(pe, "a1_wv")
            pe.wait_ge(S["low_ready"], NB)
            for h in range(R):
                unit(0, 0, h)

            def group(g, last=False):
                for b in range(NB):
                    step(g, b, not last)

            group(0)
            with pe.Fori(1, G - 1) as g:
                group(g)
            group(G - 1, last=True)
            output(G - 1, NB - 1, range(R))

        @block.scalar
        def _(act):
            def copy_v(g, b):
                act.wait_ge(S["v_ready"], 8 * g + b + 1)
                after_first(act, S["ot_ready"], 8 * g - 8 + b + 1)
                nc.scalar.copy(v[:, b, :], ps[:, V_BANK, 0:HD]).then_inc(S["v_copied"], 1)

            def step(g, b, project):
                t = 8 * g + b
                slot = b % 2
                act.wait_ge(S["bias_ready"], t + 1)
                after_first(act, S["pt_ready"], t - 1)
                for h in range(R):
                    nc.scalar.activation(prob[:, slot, h, :], ps[:, S_BANK, h * P:(h + 1) * P], ACT.Exp,
                                         bias=bias[:, slot, h:h + 1], scale=scale,
                                         accum_out=total[:, slot, h:h + 1]).then_inc(S["exp_ready"], 1)
                if b < 4:
                    copy_v(g, b + 4)
                elif project:
                    copy_v(g + 1, b - 4)
                act.wait_ge(S["pt_ready"], t + 1)
                after_first(act, S["ot_ready"], t - 1)
                nc.scalar.copy(probT[:, slot, :], ps[:, PT_BANK, :]).then_inc(S["pt_copied"], 1)
                act.wait_ge(S["ot_ready"], t + 1)
                after_first(act, S["y_ready"], t - 1)
                nc.scalar.copy(oT[:, slot, HI, :], ps[:, OT_BANK, :]).then_inc(S["ot_copied"], 1)

            for part, table in enumerate((cos, sin)):
                for half in range(2):
                    n = 2 * part + half
                    act.wait_ge(S["table_ready"], n + 1)
                    nc.scalar.copy(table[:, half * HALF:(half + 1) * HALF], ps[:, n, :])\
                      .then_inc(S["table_copied"], 1)
            for b in range(NB):
                act.wait_ge(k.xt_ready, NB * 2 + b + 1)
                nc.scalar.copy(xT[:, HI, :, b * P:(b + 1) * P],
                               ps[:, 4 + b % 2, :].rearrange("p (c t) -> p c t", c=C)).then_inc(S["xt_copied"], 1)
            for b in range(4):
                copy_v(0, b)

            def group(g, last=False):
                for b in range(NB):
                    step(g, b, not last)

            group(0)
            with act.Fori(1, G - 1) as g:
                group(g)
            group(G - 1, last=True)

        @block.vector
        def _(dve):
            link = Link(dve, k.dve_own, k.dve_count)
            hot, top = HD // 2, MAXPOS - 1

            def x_low(b):
                tok = slice(b * P, (b + 1) * P)
                dve.wait_ge(S["xt_copied"], b + 1)
                low_part(nc.vector, xT[:, LO, :, tok], ps[:, 4 + b % 2, :].rearrange("p (c t) -> p c t", c=C),
                         xT[:, HI, :, tok]).then_inc(S["low_ready"], 1)

            def o_low(g, b):
                t = 8 * g + b
                dve.wait_ge(S["ot_copied"], t + 1)
                low_part(nc.vector, oT[:, b % 2, LO, :], ps[:, OT_BANK, :], oT[:, b % 2, HI, :])\
                  .then_inc(S["low_ready"], 1)

            k.arrived(dve, "a1_tables")
            link(nc.vector.tensor_copy(pos[:, :], pos_i[:, :]))
            link(nc.vector.tensor_scalar(wrap[:, :], pos[:, :], 0.0, float(MAXPOS), ALU.is_lt, ALU.mult))
            link(nc.vector.tensor_tensor(pos[:, :], pos[:, :], wrap[:, :], ALU.add))
            link(nc.vector.tensor_scalar(pos[:, :], pos[:, :], 0.0, float(top), ALU.max, ALU.min))
            k.arrived(dve, "a1_tables")
            for c in range(MAXPOS // P):
                nc.vector.tensor_scalar(onehot[:, c, :], pos[:, :], iota[:, c:c + 1], None, ALU.is_equal)\
                  .then_inc(S["onehot_ready"], 1)
            for b in range(NB):
                after_first(dve, k.xt_ready, NB * 2 + b - 1)
                k.normed(dve, 2, b, k.xn[:, b % 2, :]).then_inc(k.xn_ready, 1)
                if b >= 1:
                    x_low(b - 1)
            x_low(NB - 1)
            k.arrived(dve, "a1_mask")
            link(nc.vector.memset(fill[:, :], -1e9 / scale))
            link(nc.vector.tensor_scalar(hidden[:, :, :], mask[:, :, :], 0.0, None, ALU.is_equal))
            dve.wait_ge(S["table_copied"], 4)

            own0 = link.n
            OWN = 3

            def turn(g, half, h):
                r = 10 * g + rotation(half, h)
                slot = rotation(half, h) % 2
                bank = ps[:, QK_BANK + slot, :]
                tok = slice(half * HALF, (half + 1) * HALF)
                dve.wait_ge(S["qk_ready"], r + 1)
                after_first(dve, S["rotated"], r - 1)
                nc.vector.tensor_tensor(turned[:, slot, 0, :], bank, cos[:, tok], ALU.mult)
                nc.vector.tensor_tensor(turned[0:hot, slot, 1, :], bank[hot:P, :], sin[hot:P, tok], ALU.mult)
                nc.vector.tensor_tensor(turned[hot:P, slot, 1, :], bank[0:hot, :], sin[0:hot, tok], ALU.mult)\
                  .then_inc(S["turned"], 1)

            def add(g, b, last):
                t = 8 * g + b
                dve.wait_ge(S["y_ready"], t + 1)
                after_first(dve, S["y_added"], t - 7)
                nc.vector.tensor_tensor(k.x[:, b, :], k.x[:, b, :], ps[:, Y_BANK + b % 2, :], ALU.add)\
                  .then_inc(S["y_added"], 1)
                if last:
                    dve.wait_ge(S["y_added"], t + 1)
                    k.row_stats(dve, last, b)

            def step(g, b, project, last):
                t = 8 * g + b
                own = own0 + OWN * t
                slot = b % 2
                scores = ps[:, S_BANK, :].rearrange("p (h k) -> p h k", h=R)
                dve.wait_ge(S["s_ready"], t + 1)
                nc.vector.memset(gate[:, :], 0.0)
                nc.vector.copy_predicated(scores, hidden[:, b, :].unsqueeze(1).to_broadcast([P, R, P]),
                                          fill[:, :].unsqueeze(1).to_broadcast([P, R, P])).then_inc(k.dve_own, 1)
                dve.wait_ge(k.dve_own, own + 1)
                nc.vector.tensor_reduce(negmax[:, slot, :], scores, AX.X, ALU.max, negate=True)\
                  .then_inc(k.dve_own, 1)
                dve.wait_ge(k.dve_own, own + 2)
                after_first(dve, S["exp_ready"], R * (t - 1))
                nc.vector.tensor_scalar(bias[:, slot, :], negmax[:, slot, :], scale, None, ALU.mult)\
                  .then_inc(S["bias_ready"], 1)
                next_g, half, h = (g, 1, b) if b < 4 else (g + 1, 0, b - 4)
                if h == 0 and (project or b < 4):
                    turn(next_g, half, -1)
                if before(g, b):
                    o_low(*before(g, b))
                dve.wait_ge(S["exp_ready"], R * (t + 1))
                nc.vector.reciprocal(inv[:, slot, :], total[:, slot, :]).then_inc(k.dve_own, 1)
                dve.wait_ge(k.dve_own, own + 3)
                nc.vector.tensor_tensor(prob[:, slot, :, :], prob[:, slot, :, :],
                                        inv[:, slot, :].unsqueeze(2).to_broadcast([P, R, P]), ALU.mult)\
                  .then_inc(S["prob_ready"], 1)
                if project or b < 4:
                    turn(next_g, half, h)
                if before(g, b):
                    add(*before(g, b), last if b else None)

            for h in range(-1, R):
                turn(0, 0, h)

            def group(g, last=None):
                for b in range(NB):
                    step(g, b, last is None, last)

            group(0)
            with dve.Fori(1, G - 1) as g:
                group(g)
            stats = Link(dve, k.sem("a1_stats"))
            group(G - 1, last=stats)
            o_low(G - 1, NB - 1)
            add(G - 1, NB - 1, stats)
            k.dve_count = own0 + OWN * NB * G


def mixture_of_experts(k, dram):
    nc, ps = k.nc, k.ps
    NE = 3
    NG = 4
    SLOTS = 3
    HALF = TOK // 2
    VISION = int(P * 0.3)
    FUNCS = (ACT.Tanh, ACT.Gelu, ACT.Silu)
    GATE, NORMS, PICKED = slice(0, NB * NG), slice(64, 64 + 2 * NB), slice(128, 128 + NB * 2 * NE)
    PRE_BANK, OUT_BANK, OUT_BANKS, GATE_BANK, T_BANK = 0, 2, 3, 5, 6
    with ExitStack() as ctx:
        whole = k.sb(ctx, "f1_whole", [P, SLOTS, C, D])
        w = k.sb(ctx, "f1_w", [P, 2, SLOTS, C, D], F32R)
        b1 = k.sb(ctx, "f1_b1", [P, NE, C])
        b2 = k.sb(ctx, "f1_b2", [P, NE, D])
        gw_whole = k.sb(ctx, "f1_gw_whole", [P, C, NG])
        gw = k.sb(ctx, "f1_gw", [P, 2, C, NG], F32R)
        gw_ratio = k.sb(ctx, "f1_gw_ratio", [P, NE])
        gb = k.sb(ctx, "f1_gb", [P, NE])
        ones = k.sb(ctx, "f1_ones", [P, P])
        row0 = k.sb(ctx, "f1_row0", [P, P])
        share = k.sb(ctx, "f1_share", [P, 2])
        xT = k.sb(ctx, "f1_xT", [P, 2, C, TOK], F32R)
        act_whole = k.sb(ctx, "f1_act_whole", [P, C, HALF])
        act_T = k.sb(ctx, "f1_act", [P, 2, 2, C, HALF], F32R)
        norms = k.sb(ctx, "f1_norms", [P, NB])
        both = k.sb(ctx, "f1_both", [P, NB, 2])
        prob = k.sb(ctx, "f1_prob", [P, NB, NE])
        tmp = k.sb(ctx, "f1_tmp", [P, NB, NE])
        ratio = k.sb(ctx, "f1_ratio", [P, NB])
        one = k.sb(ctx, "f1_one", [P, 12, NB])
        first = k.sb(ctx, "f1_first", [P, NB, NE])
        lowest = k.sb(ctx, "f1_lowest", [P, NB, NE])
        picks = k.sb(ctx, "f1_picks", [P, NB, 2, NE])
        weight = k.sb(ctx, "f1_weight", [P, NB, NE])
        S = {n: k.sem("f1_" + n) for n in (
            "norm_ready", "xt_copied", "gate_ready", "asked", "answered",
            "pre_ready", "act_ready", "act_high", "act_low", "out_ready", "added", "split", "xt_low", "gw_ready")}
        whole_loaded = [k.sem(f"f1_whole{n}_loaded") for n in range(SLOTS)]
        MEANS, EXP, PICKS = 1, 2, 3
        block = ctx.enter_context(nc.Block())

        @block.sync
        def _(sp):
            def load_matrix(i):
                after_first(sp, S["split"], 2 * (i - SLOTS + 1))
                sp.dma_start(whole[:, i % SLOTS, :, :], dram[f"f1_w{i % 2 + 1}"][i // 2])\
                  .then_inc(whole_loaded[i % SLOTS], 16)

            k.load(sp, "f1_gw", gw_whole[:, :, :], dram["f1_gw"])
            load_matrix(0)
            for name, dst in (("ones", ones[:, :]), ("share", share[:, :]), ("b1", b1[:, :, :]),
                              ("row0", row0[:, :])):
                k.load(sp, "f1_small", dst, dram["f1_" + name])
            k.load(sp, "f1_small", gw_ratio[:, :], dram["f1_gw_ratio"].partition_broadcast(P))
            k.load(sp, "f1_small", gb[:, :], dram["f1_gb"].partition_broadcast(P))
            k.load(sp, "f1_b2", b2[:, :, :], dram["f1_b2"].partition_broadcast(P))
            for i in range(1, 2 * NE):
                load_matrix(i)

        @block.gpsimd
        def _(pool):
            link = Link(pool, k.pool_own, k.pool_count)
            k.arrived(pool, "f1_gw")
            link(nc.gpsimd.tensor_copy(gw[:, HI, :, :], gw_whole[:, :, :]))
            low_part(nc.gpsimd, gw[:, LO, :, :], gw_whole[:, :, :], gw[:, HI, :, :]).then_inc(S["gw_ready"], 1)
            for i in range(2 * NE):
                slot = i % SLOTS
                pool.wait_ge(S["split"], 2 * i + 1)
                low_part(nc.gpsimd, w[:, LO, slot, :, :], whole[:, slot, :, :], w[:, HI, slot, :, :])\
                  .then_inc(S["split"], 1)
            for b in range(NB):
                k.row_rstd(pool, link, 4, b)
            k.pool_count = link.n

        @block.tensor
        def _(pe):
            def gate(b):
                pe.wait_ge(S["xt_low"], b + 1)
                for c in range(C):
                    last = split_product(nc, ps[:, GATE_BANK, GATE][:, NG * b:NG * (b + 1)],
                                         parts(xT, c, slice(b * P, (b + 1) * P)), parts(gw, c),
                                         c == 0, c == C - 1)
                last.then_inc(S["gate_ready"], 1)

            def first_product(n, chunks=range(C)):
                e, half = n // 2, n % 2
                pe.wait_ge(S["split"], 2 * (2 * e + 1))
                for f in chunks:
                    u = C * n + f
                    after_first(pe, S["act_ready"], u - 1)
                    for c in range(C):
                        last = split_product(nc, ps[:, PRE_BANK + u % 2, :],
                                             parts(w, 2 * e % SLOTS, c, slice(f * P, (f + 1) * P)),
                                             parts(xT, c, slice(half * HALF, (half + 1) * HALF)),
                                             c == 0, c == C - 1)
                    last.then_inc(S["pre_ready"], 1)

            def second_product(n):
                e, half = n // 2, n % 2
                pe.wait_ge(S["split"], 2 * (2 * e + 2))
                pe.wait_ge(S["act_low"], C * (n + 1))
                for j in range(4):
                    o = 4 * n + j
                    after_first(pe, S["added"], o - OUT_BANKS + 1)
                    for f in range(C):
                        last = split_product(nc, ps[:, OUT_BANK + o % OUT_BANKS, :],
                                             parts(act_T, n % 2, f, slice(j * P, (j + 1) * P)),
                                             parts(w, (2 * e + 1) % SLOTS, f), f == 0, f == C - 1)
                    last.then_inc(S["out_ready"], 1)

            for b in range(NB):
                pe.wait_ge(k.xn_ready, NB * 3 + b + 1)
                after_first(pe, S["xt_low"], b - 1)
                k.transpose4(T_BANK + b % 2, k.xn[:, b % 2, :]).then_inc(k.xt_ready, 1)
                if b == 0:
                    pe.wait_ge(S["gw_ready"], 1)
                else:
                    gate(b - 1)
                if b >= 4:
                    first_product(0, [b - 4])
            gate(NB - 1)
            k.arrived(pe, "f1_small")
            pe.wait_ge(S["asked"], MEANS)
            nc.tensor.matmul(ps[:, GATE_BANK, NORMS], ones[:, :], both[:, :, :].rearrange("p b n -> p (b n)"),
                             start=True, stop=True).then_inc(S["answered"], 1)
            for n in range(1, 2 * NE + 1):
                if n < 2 * NE:
                    first_product(n)
                if n == 1:
                    k.arrived(pe, "f1_small")
                    pe.wait_ge(S["asked"], PICKS)
                    nc.tensor.matmul(ps[:, GATE_BANK, PICKED], row0[:, :],
                                     picks[:, :, :, :].rearrange("p b i e -> p (b i e)"), start=True, stop=True)\
                      .then_inc(S["answered"], 1)
                second_product(n - 1)

        @block.scalar
        def _(act):
            def high_part(i):
                slot = i % SLOTS
                act.wait_ge(whole_loaded[slot], 16 * (i // SLOTS + 1))
                if i >= SLOTS:
                    used = S["out_ready"] if (i - SLOTS) % 2 else S["pre_ready"]
                    act.wait_ge(used, 2 * C * ((i - SLOTS) // 2 + 1))
                after_first(act, S["split"], 2 * i)
                nc.scalar.copy(w[:, HI, slot, :, :], whole[:, slot, :, :]).then_inc(S["split"], 1)

            def activations(n, f):
                e, u = n // 2, C * n + f
                act.wait_ge(S["pre_ready"], u + 1)
                after_first(act, S["act_low"], u - C + 1)
                nc.scalar.activation(act_whole[:, f, :], ps[:, PRE_BANK + u % 2, :], FUNCS[e],
                                     bias=b1[:, e, f:f + 1]).then_inc(S["act_ready"], 1)
                if f == 0:
                    after_first(act, S["out_ready"], 4 * (n - 1))
                act.wait_ge(S["act_ready"], u + 1)
                nc.scalar.copy(act_T[:, HI, n % 2, f, :], act_whole[:, f, :]).then_inc(S["act_high"], 1)

            for b in range(NB):
                if b >= 3 and b % 2:
                    high_part((b - 3) // 2)
                act.wait_ge(k.xn_ready, NB * 3 + b + 1)
                after_first(act, S["norm_ready"], b - 1)
                nc.scalar.activation(ps[:, OUT_BANK + b % 2, :], k.xn[:, b % 2, :], ACT.Abs, accum_out=norms[:, b:b + 1])\
                  .then_inc(S["norm_ready"], 1)
                act.wait_ge(k.xt_ready, NB * 3 + b + 1)
                nc.scalar.copy(xT[:, HI, :, b * P:(b + 1) * P],
                               ps[:, T_BANK + b % 2, :].rearrange("p (c t) -> p c t", c=C)).then_inc(S["xt_copied"], 1)
                if b == 4:
                    k.arrived(act, "f1_small")
                if b >= 4:
                    activations(0, b - 4)
            for n in range(1, 2 * NE):
                if n >= 2 and n - 2 + SLOTS < 2 * NE:
                    high_part(n - 2 + SLOTS)
                for f in range(C):
                    activations(n, f)
                    if n == 1 and f == 1:
                        act.wait_ge(S["asked"], EXP)
                        nc.scalar.activation(prob[:, :, :], prob[:, :, :], ACT.Exp).then_inc(S["answered"], 1)

        @block.vector
        def _(dve):
            link = Link(dve, k.dve_own, k.dve_count)
            tt, ts = nc.vector.tensor_tensor, nc.vector.tensor_scalar

            def x_low(b):
                tok = slice(b * P, (b + 1) * P)
                dve.wait_ge(S["xt_copied"], b + 1)
                low_part(nc.vector, xT[:, LO, :, tok], ps[:, T_BANK + b % 2, :].rearrange("p (c t) -> p c t", c=C),
                         xT[:, HI, :, tok]).then_inc(S["xt_low"], 1)

            def act_lows(n, chunks=range(C)):
                for f in chunks:
                    dve.wait_ge(S["act_high"], C * n + f + 1)
                    low_part(nc.vector, act_T[:, LO, n % 2, f, :], act_whole[:, f, :], act_T[:, HI, n % 2, f, :])\
                      .then_inc(S["act_low"], 1)

            for b in range(NB):
                after_first(dve, k.xt_ready, NB * 3 + b - 1)
                after_first(dve, S["norm_ready"], b - 1)
                k.normed(dve, 3, b, k.xn[:, b % 2, :]).then_inc(k.xn_ready, 1)
                if b >= 1:
                    x_low(b - 1)
                if b >= 5:
                    act_lows(0, [b - 5])
            x_low(NB - 1)
            act_lows(0, [C - 1])
            k.arrived(dve, "f1_small")
            dve.wait_ge(S["norm_ready"], NB)
            link(ts(both[:, :, 0], norms[:, :], share[:, 0:1], None, ALU.mult))
            ts(both[:, :, 1], norms[:, :], share[:, 1:2], None, ALU.mult).then_inc(S["asked"], 1)
            dve.wait_ge(S["gate_ready"], NB)
            dve.wait_ge(S["answered"], MEANS)
            means = ps[:, GATE_BANK, NORMS].rearrange("p (b n) -> p b n", n=2)
            link(ts(ratio[:, :], means[:, :, 1], 1e-8, None, ALU.add))
            link(nc.vector.reciprocal(one[:, 0, :], ratio[:, :]))
            link(tt(ratio[:, :], means[:, :, 0], one[:, 0, :], ALU.mult))
            each = [P, NB, NE]
            link(tt(tmp[:, :, :], ratio[:, :].unsqueeze(2).to_broadcast(each),
                    gw_ratio[:, :].unsqueeze(1).to_broadcast(each), ALU.mult))
            link(tt(tmp[:, :, :], ps[:, GATE_BANK, GATE].rearrange("p (b e) -> p b e", e=NG)[:, :, 0:NE], tmp[:, :, :], ALU.add))
            link(tt(tmp[:, :, :], tmp[:, :, :], gb[:, :].unsqueeze(1).to_broadcast(each), ALU.add))
            link(nc.vector.tensor_reduce(one[:, 1, :], tmp[:, :, :], AX.X, ALU.max))
            tt(prob[:, :, :], tmp[:, :, :], one[:, 1, :].unsqueeze(2).to_broadcast(each), ALU.subtract)\
              .then_inc(S["asked"], 1)
            dve.wait_ge(S["answered"], EXP)
            link(nc.vector.tensor_reduce(one[:, 2, :], prob[:, :, :], AX.X, ALU.add))
            link(nc.vector.reciprocal(one[:, 3, :], one[:, 2, :]))
            link(tt(prob[:, :, :], prob[:, :, :], one[:, 3, :].unsqueeze(2).to_broadcast(each), ALU.mult))
            p0, p1, p2 = (prob[:, :, e] for e in range(NE))
            top, second, least, larger, lesser, other, either = (one[:, n, :] for n in range(4, 11))
            link(tt(larger, p0, p1, ALU.max))
            link(tt(lesser, p0, p1, ALU.min))
            link(tt(top, larger, p2, ALU.max))
            link(tt(least, lesser, p2, ALU.min))
            link(tt(other, larger, p2, ALU.min))
            link(tt(second, lesser, other, ALU.max))
            link(tt(first[:, :, :], prob[:, :, :], top.unsqueeze(2).to_broadcast(each), ALU.is_ge))
            link(tt(lowest[:, :, :], prob[:, :, :], least.unsqueeze(2).to_broadcast(each), ALU.is_le))
            link(tt(either, first[:, :, 0], first[:, :, 1], ALU.max))
            link(tt(first[:, :, 2], first[:, :, 2], either, ALU.is_gt))
            link(tt(first[:, :, 1], first[:, :, 1], first[:, :, 0], ALU.is_gt))
            link(tt(either, lowest[:, :, 2], lowest[:, :, 1], ALU.max))
            link(tt(lowest[:, :, 0], lowest[:, :, 0], either, ALU.is_gt))
            link(tt(lowest[:, :, 1], lowest[:, :, 1], lowest[:, :, 2], ALU.is_gt))
            link(nc.vector.tensor_copy(picks[:, :, 0, :], first[:, :, :]))
            link(tt(tmp[:, :, :], first[:, :, :], lowest[:, :, :], ALU.add))
            ts(picks[:, :, 1, :], tmp[:, :, :], -1.0, 1.0, ALU.mult, ALU.add).then_inc(S["asked"], 1)
            link(tt(one[:, 0, :], top, second, ALU.add))
            link(ts(one[:, 1, :], one[:, 0, :], 1e-8, None, ALU.add))
            link(nc.vector.reciprocal(one[:, 2, :], one[:, 1, :]))
            link(tt(top, top, one[:, 2, :], ALU.mult))
            link(tt(second, second, one[:, 2, :], ALU.mult))
            dve.wait_ge(S["asked"], PICKS)
            dve.wait_ge(S["answered"], PICKS)
            picked = ps[:, GATE_BANK, PICKED].rearrange("p (b i e) -> p b i e", b=NB, i=2)
            link(tt(weight[:, :, :], picked[:, :, 0, :], top.unsqueeze(2).to_broadcast(each), ALU.mult))
            link(tt(tmp[:, :, :], picked[:, :, 1, :], second.unsqueeze(2).to_broadcast(each), ALU.mult))
            link(tt(weight[:, :, :], weight[:, :, :], tmp[:, :, :], ALU.add))

            def add(n):
                e, half = n // 2, n % 2
                k.arrived(dve, "f1_b2")
                for j in range(4):
                    b = 4 * half + j
                    link(nc.vector.scalar_tensor_tensor(k.x[:, b, :], b2[:, e, :], weight[:, b, e:e + 1],
                                                        k.x[:, b, :], ALU.mult, ALU.add))
                    dve.wait_ge(S["out_ready"], 4 * n + j + 1)
                    nc.vector.scalar_tensor_tensor(k.x[:, b, :], ps[:, OUT_BANK + (4 * n + j) % OUT_BANKS, :],
                                                   weight[:, b, e:e + 1], k.x[:, b, :], ALU.mult, ALU.add)\
                      .then_inc(S["added"], 1)
                    dve.wait_ge(S["added"], 4 * n + j + 1)
                    if e == NE - 1:
                        k.row_stats(dve, link, b)

            for n in range(2 * NE):
                if n + 1 < 2 * NE:
                    act_lows(n + 1)
                add(n)
            k.dve_count = link.n


def autocorrelation(k, dram):
    nc, ps = k.nc, k.ps
    CTX_BANK, Q_BANK, C_BANK, WT_BANK, W_BANK, OUT_BANK = 0, 2, 3, 4, 5, 7
    K1, K2, VC, VS = range(4)
    TOP = 9
    with ExitStack() as ctx:
        table = k.sb(ctx, "a2_table", [P, 12, P])
        T_Q, T_K2, T_VC, T_VS, T_C1, T_C2, T_WC, T_WS, T_OC, T_OSN, T_OS, T_LAST = (
            table[:, n, :] for n in range(12))
        value = k.sb(ctx, "a2_ctx", [P, NB, D])
        freq = k.sb(ctx, "a2_freq", [P, 2, 4, D])
        prod = k.sb(ctx, "a2_prod", [P, 2, D])
        corr = k.sb(ctx, "a2_corr", [P, 2, C, P])
        less8 = k.sb(ctx, "a2_less8", [P, C, P])
        less9 = k.sb(ctx, "a2_less9", [P, C, P])
        top8 = k.sb(ctx, "a2_top8", [P, C, 8])
        ninth = k.sb(ctx, "a2_ninth", [P, C, 8])
        negmax = k.sb(ctx, "a2_negmax", [P, 2, C])
        expo = k.sb(ctx, "a2_exp", [P, C, P])
        picked = k.sb(ctx, "a2_picked", [P, C, P])
        total = k.sb(ctx, "a2_total", [P, C])
        inv = k.sb(ctx, "a2_inv", [P, C])
        weight = k.sb(ctx, "a2_weight", [P, C, P])
        weightT = k.sb(ctx, "a2_weightT", [P, D])
        shift = k.sb(ctx, "a2_shift", [P, 4, D])
        S = {n: k.sem("a2_" + n) for n in (
            "freq_ready", "freq_copied", "q_ready", "prod_ready", "corr_ready", "corr_copied",
            "max_ready", "exp_ready", "weight_ready", "wt_ready", "wt_copied", "w_ready", "shift_ready",
            "out_ready", "added")}
        block = ctx.enter_context(nc.Block())

        @block.sync
        def _(sp):
            k.load(sp, "a2_table", table[:, :, :], dram["a2_table"])
            for b in range(NB):
                k.load(sp, f"a2_ctx{b // 4}", value[:, b, :], dram["ctx"][b])

        @block.gpsimd
        def _(pool):
            link = Link(pool, k.pool_own, k.pool_count)
            for b in range(NB):
                k.row_rstd(pool, link, 5, b)
            k.pool_count = link.n

        @block.tensor
        def _(pe):
            mm = nc.tensor.matmul

            def context(b):
                k.arrived(pe, f"a2_ctx{b // 4}")
                for n, t in enumerate((T_Q, T_K2, T_VC, T_VS)):
                    u = 4 * b + n
                    after_first(pe, S["freq_copied"], u - 1)
                    mm(ps[:, CTX_BANK + u % 2, :], t, value[:, b, :], start=True, stop=True)\
                        .then_inc(S["freq_ready"], 1)

            def query(b):
                pe.wait_ge(k.xn_ready, NB * 4 + b + 1)
                after_first(pe, S["prod_ready"], b)
                mm(ps[:, Q_BANK, :], T_Q, k.xn[:, b % 2, :], start=True, stop=True).then_inc(S["q_ready"], 1)

            def correlate(b):
                pe.wait_ge(S["prod_ready"], b + 1)
                after_first(pe, S["corr_copied"], b)
                for c in range(C):
                    o = ps[:, C_BANK, c * P:(c + 1) * P]
                    mm(o, prod[:, 0, c * P:(c + 1) * P], T_C1, start=True, stop=False)
                    last = mm(o, prod[:, 1, c * P:(c + 1) * P], T_C2, start=False, stop=True)
                last.then_inc(S["corr_ready"], 1)

            def weights(b):
                pe.wait_ge(S["weight_ready"], b + 1)
                after_first(pe, S["wt_copied"], b)
                k.transpose4(WT_BANK, weight[:, :, :].rearrange("p c t -> p (c t)")).then_inc(S["wt_ready"], 1)

            def weights_transform(b):
                pe.wait_ge(S["wt_copied"], b + 1)
                after_first(pe, S["shift_ready"], b)
                mm(ps[:, W_BANK, :], T_WC, weightT[:, :], start=True, stop=True)
                mm(ps[:, W_BANK + 1, :], T_WS, weightT[:, :], start=True, stop=True).then_inc(S["w_ready"], 1)

            def output(b):
                after_first(pe, S["added"], b)
                mm(ps[:, OUT_BANK, :], T_LAST, value[:, b, :], start=True, stop=False)
                pe.wait_ge(S["shift_ready"], b + 1)
                for n, t in enumerate((T_OC, T_OC, T_OSN, T_OS)):
                    last = mm(ps[:, OUT_BANK, :], t, shift[:, n, :], start=False, stop=n == 3)
                last.then_inc(S["out_ready"], 1)

            k.arrived(pe, "a2_table")
            for i in range(NB + 1):
                if i < NB:
                    context(i)
                    query(i)
                if i >= 1:
                    weights(i - 1)
                if i < NB:
                    correlate(i)
                if i >= 1:
                    weights_transform(i - 1)
                    output(i - 1)

        @block.scalar
        def _(act):
            def context(b):
                for n in range(4):
                    u = 4 * b + n
                    act.wait_ge(S["freq_ready"], u + 1)
                    after_first(act, S["prod_ready"], b - 1)
                    after_first(act, S["shift_ready"], b - 1)
                    nc.scalar.copy(freq[:, b % 2, n, :], ps[:, CTX_BANK + u % 2, :]).then_inc(S["freq_copied"], 1)

            for i in range(NB + 1):
                if i < NB:
                    context(i)
                if i >= 1:
                    act.wait_ge(S["wt_ready"], i)
                    after_first(act, S["w_ready"], i - 1)
                    nc.scalar.copy(weightT[:, :], ps[:, WT_BANK, :]).then_inc(S["wt_copied"], 1)
                if i < NB:
                    act.wait_ge(S["corr_ready"], i + 1)
                    after_first(act, S["weight_ready"], i - 1)
                    nc.scalar.copy(corr[:, i % 2, :, :].rearrange("p c t -> p (c t)"), ps[:, C_BANK, :])\
                      .then_inc(S["corr_copied"], 1)
                    act.wait_ge(S["max_ready"], i + 1)
                    act.wait_ge(S["corr_copied"], i + 1)
                    after_first(act, S["weight_ready"], i)
                    for c in range(C):
                        nc.scalar.activation(expo[:, c, :], corr[:, i % 2, c, :], ACT.Exp,
                                             bias=negmax[:, i % 2, c:c + 1]).then_inc(S["exp_ready"], 1)

        @block.vector
        def _(dve):
            link = Link(dve, k.dve_own, k.dve_count)
            tt = nc.vector.tensor_tensor

            def normalise(b):
                after_first(dve, S["q_ready"], b - 1)
                k.normed(dve, 4, b, k.xn[:, b % 2, :]).then_inc(k.xn_ready, 1)

            def multiply(b):
                dve.wait_ge(S["q_ready"], b + 1)
                dve.wait_ge(S["freq_copied"], 4 * b + 2)
                after_first(dve, S["corr_ready"], b)
                tt(prod[:, 0, :], ps[:, Q_BANK, :], freq[:, b % 2, K1, :], ALU.mult)
                tt(prod[:, 1, :], ps[:, Q_BANK, :], freq[:, b % 2, K2, :], ALU.mult).then_inc(S["prod_ready"], 1)

            def multiply_shift(b):
                dve.wait_ge(S["w_ready"], b + 1)
                dve.wait_ge(S["freq_copied"], 4 * b + 4)
                after_first(dve, S["out_ready"], b)
                wc, ws = ps[:, W_BANK, :], ps[:, W_BANK + 1, :]
                vc, vs = freq[:, b % 2, VC, :], freq[:, b % 2, VS, :]
                tt(shift[:, 0, :], wc, vc, ALU.mult)
                tt(shift[:, 1, :], ws, vs, ALU.mult)
                tt(shift[:, 2, :], ws, vc, ALU.mult)
                tt(shift[:, 3, :], wc, vs, ALU.mult).then_inc(S["shift_ready"], 1)

            def pick(b):
                dve.wait_ge(S["corr_copied"], b + 1)
                for c in range(C):
                    nc.vector.max(top8[:, c, :], corr[:, b % 2, c, :]).then_inc(k.dve_own, 1)
                link.n += C
                dve.wait_ge(k.dve_own, link.n)
                after_first(dve, S["exp_ready"], C * (b - 1))
                nc.vector.tensor_scalar(negmax[:, b % 2, :], top8[:, :, 0], -1.0, None, ALU.mult)\
                  .then_inc(S["max_ready"], 1)
                for c in range(C):
                    nc.vector.match_replace(less8[:, c, :], top8[:, c, :], corr[:, b % 2, c, :], LOWEST)\
                      .then_inc(k.dve_own, 1)
                link.n += C
                dve.wait_ge(k.dve_own, link.n)
                link(nc.vector.tensor_reduce(ninth[:, :, 0], less8[:, :, :], AX.X, ALU.max))
                for c in range(C):
                    nc.vector.match_replace(less9[:, c, :], ninth[:, c, :], less8[:, c, :], LOWEST)\
                      .then_inc(k.dve_own, 1)
                link.n += C
                dve.wait_ge(k.dve_own, link.n)
                dve.wait_ge(S["exp_ready"], C * (b + 1))
                link(nc.vector.scalar_tensor_tensor(picked[:, :, :], less9[:, :, :], LOWEST, expo[:, :, :],
                                                    ALU.is_equal, ALU.mult))
                link(nc.vector.tensor_reduce(total[:, :], picked[:, :, :], AX.X, ALU.add))
                link(nc.vector.reciprocal(inv[:, :], total[:, :]))
                after_first(dve, S["wt_ready"], b)
                tt(weight[:, :, :], picked[:, :, :], inv[:, :].unsqueeze(2).to_broadcast([P, C, P]), ALU.mult)\
                    .then_inc(S["weight_ready"], 1)
                dve.wait_ge(S["weight_ready"], b + 1)

            def add(b):
                dve.wait_ge(S["out_ready"], b + 1)
                tt(k.x[:, b, :], k.x[:, b, :], ps[:, OUT_BANK, :], ALU.add).then_inc(S["added"], 1)
                dve.wait_ge(S["added"], b + 1)
                k.row_stats(dve, link, b)

            link(nc.vector.memset(ninth[:, :, :], LOWEST))
            normalise(0)
            normalise(1)
            for i in range(NB + 1):
                if i < NB:
                    multiply(i)
                    if i + 2 < NB:
                        normalise(i + 2)
                if i >= 1:
                    multiply_shift(i - 1)
                if i < NB:
                    pick(i)
                if i >= 1:
                    add(i - 1)
            k.dve_count = link.n


def scaled_linear(k, dram):
    nc, ps = k.nc, k.ps
    OUT_BANK, OUT_BANKS, T_BANK = 0, 4, 6
    with ExitStack() as ctx:
        wt = k.sb(ctx, "f2_w", [P, C, D])
        scale = k.sb(ctx, "f2_scale", [P, C, C])
        bias = k.sb(ctx, "f2_bias", [P, D])
        xT = k.sb(ctx, "f2_xT", [P, 2, C, P])
        S = {n: k.sem("f2_" + n) for n in (
            "w_ready", "biased", "xt_copied", "out_ready", "added")}
        block = ctx.enter_context(nc.Block())

        @block.sync
        def _(sp):
            k.load(sp, "f2_w", scale[:, :, :].rearrange("p i o -> p (i o)"),
                   dram["f2_scale"].partition_broadcast(P))
            k.load(sp, "f2_w", wt[:, :, :], dram["f2_w"])
            k.load(sp, "f2_bias", bias[:, :], dram["f2_bias"].partition_broadcast(P))

        @block.gpsimd
        def _(pool):
            link = Link(pool, k.pool_own, k.pool_count)
            k.arrived(pool, "f2_bias")
            for b in range(NB):
                pool.wait_ge(k.xn_ready, NB * 5 + b + 1)
                nc.gpsimd.tensor_tensor(k.x[:, b, :], k.x[:, b, :], bias[:, :], ALU.add).then_inc(S["biased"], 1)
                if b >= 2:
                    k.row_rstd(pool, link, 6, b - 2)
            k.row_rstd(pool, link, 6, NB - 2)
            k.row_rstd(pool, link, 6, NB - 1)
            k.pool_count = link.n

        @block.tensor
        def _(pe):
            for i in range(NB + 1):
                if i < NB:
                    pe.wait_ge(k.xn_ready, NB * 5 + i + 1)
                    after_first(pe, S["xt_copied"], i - 1)
                    k.transpose4(T_BANK + i % 2, k.xn[:, i % 2, :]).then_inc(k.xt_ready, 1)
                if i >= 1:
                    b = i - 1
                    if b == 0:
                        pe.wait_ge(S["w_ready"], C)
                    pe.wait_ge(S["xt_copied"], b + 1)
                    after_first(pe, S["added"], b - OUT_BANKS + 1)
                    for c in range(C):
                        last = nc.tensor.matmul(ps[:, OUT_BANK + b % OUT_BANKS, :], xT[:, b % 2, c, :], wt[:, c, :],
                                                start=c == 0, stop=c == C - 1)
                    last.then_inc(S["out_ready"], 1)

        @block.scalar
        def _(act):
            for b in range(NB):
                act.wait_ge(k.xt_ready, NB * 4 + b + 1)
                after_first(act, S["out_ready"], b - 1)
                nc.scalar.copy(xT[:, b % 2, :, :].rearrange("p c t -> p (c t)"), ps[:, T_BANK + b % 2, :])\
                  .then_inc(S["xt_copied"], 1)

        @block.vector
        def _(dve):
            link = Link(dve, k.dve_own, k.dve_count)

            def normalise(b):
                after_first(dve, k.xt_ready, NB * 4 + b - 1)
                k.normed(dve, 5, b, k.xn[:, b % 2, :]).then_inc(k.xn_ready, 1)

            normalise(0)
            k.arrived(dve, "f2_w")
            k.arrived(dve, "f2_w")
            for c in range(C):
                w = wt[:, c, :].rearrange("p (o n) -> p o n", o=C)
                nc.vector.tensor_tensor(w, w, scale[:, c, :].unsqueeze(2).to_broadcast([P, C, P]), ALU.mult)\
                  .then_inc(S["w_ready"], 1)
            normalise(1)
            for b in range(NB):
                if b + 2 < NB:
                    normalise(b + 2)
                dve.wait_ge(S["out_ready"], b + 1)
                dve.wait_ge(S["biased"], b + 1)
                nc.vector.tensor_tensor(k.x[:, b, :], k.x[:, b, :], ps[:, OUT_BANK + b % OUT_BANKS, :], ALU.add)\
                  .then_inc(S["added"], 1)
                dve.wait_ge(S["added"], b + 1)
                k.row_stats(dve, link, b)
            k.dve_count = link.n


def token_attention(k, dram):
    nc, ps = k.nc, k.ps
    H, NK = 16, 32
    HJ = P // NK
    J = H // HJ
    T = D // P
    scale = 1.0 / float((P // H) ** 0.5)
    PROJ = NK + P
    Q_BANK, S_BANK, T_BANK, PV_BANK, OUT_BANK = 0, 1, 3, 5, 6
    with ExitStack() as ctx:
        w = k.sb(ctx, "a3_w", [P, 4, P])
        proj = k.sb(ctx, "a3_proj", [P, C, PROJ])
        bcol = k.sb(ctx, "a3_bcol", [P, 2])
        brow = k.sb(ctx, "a3_brow", [1, 2, P])
        ones = k.sb(ctx, "a3_ones", [P, 1])
        of_head = k.sb(ctx, "a3_of_head", [P, H])
        of_pair = k.sb(ctx, "a3_of_pair", [P, J, P])
        sums = k.sb(ctx, "a3_sums", [1, PROJ])
        sums_k = k.sb(ctx, "a3_sums_k", [1, NB, NK])
        ck = k.sb(ctx, "a3_ck", [P, NB, NK])
        cv = k.sb(ctx, "a3_cv", [P, NB, P])
        keys = k.sb(ctx, "a3_keys", [P, NB, NK])
        values = k.sb(ctx, "a3_values", [P, NB, P])
        spread_k = k.sb(ctx, "a3_spread_k", [P, 2, H, NK])
        spread_v = k.sb(ctx, "a3_spread_v", [P, 2, J, P])
        q = k.sb(ctx, "a3_q", [P, 2, D])
        top = k.sb(ctx, "a3_top", [P, 2, H])
        prob = k.sb(ctx, "a3_prob", [P, 3, H, NK])
        total = k.sb(ctx, "a3_total", [P, 2, H])
        inv = k.sb(ctx, "a3_inv", [P, 2, H])
        probT = k.sb(ctx, "a3_probT", [P, 2, J, D])
        o = k.sb(ctx, "a3_o", [P, 2, D])
        S = {n: k.sem("a3_" + n) for n in (
            "made", "made_copied", "k_spread", "v_spread", "q_ready", "q_copied", "s_ready", "shifted",
            "exp_ready", "inv_ready", "prob_ready", "pt_ready", "pt_copied", "o_ready", "o_copied", "out_ready",
            "added")}
        block = ctx.enter_context(nc.Block())
        TILES = NB * T
        SUMS, PROJECTED, KEYS, VALUES = 1, 2, NB + 2, NB + 3

        @block.sync
        def _(sp):
            for name, dst in (("proj", proj[:, :, :]), ("ones", ones[:, :]), ("w", w[:, :, :]), ("brow", brow[:, :, :]),
                              ("bcol", bcol[:, :]), ("of_head", of_head[:, :]), ("of_pair", of_pair[:, :, :])):
                k.load(sp, "a3_consts", dst, dram["a3_" + name])

        @block.gpsimd
        def _(pool):
            link = Link(pool, k.pool_own, k.pool_count)

            def spread(b):
                if b == 0:
                    pool.wait_ge(S["made_copied"], KEYS)
                    k.arrived(pool, "a3_consts")
                after_first(pool, S["s_ready"], T * (b - 1))
                nc.gpsimd.tensor_tensor(spread_k[:, b % 2, :, :], keys[:, b, :].unsqueeze(1).to_broadcast([P, H, NK]),
                                        of_head[:, :].unsqueeze(2).to_broadcast([P, H, NK]), ALU.mult)\
                  .then_inc(S["k_spread"], 1)
                if b == 0:
                    pool.wait_ge(S["made_copied"], VALUES + 1)
                    k.arrived(pool, "a3_consts")
                after_first(pool, S["o_ready"], b - 1)
                nc.gpsimd.tensor_tensor(spread_v[:, b % 2, :, :], values[:, b, :].unsqueeze(1).to_broadcast([P, J, P]),
                                        of_pair[:, :, :], ALU.mult).then_inc(S["v_spread"], 1)

            spread(0)
            for u in range(TILES):
                b, t = u // T, u % T
                pool.wait_ge(S["inv_ready"], u + 1)
                nc.gpsimd.tensor_tensor(prob[:, u % 3, :, :], prob[:, u % 3, :, :],
                                        inv[:, u % 2, :].unsqueeze(2).to_broadcast([P, H, NK]), ALU.mult)\
                    .then_inc(S["prob_ready"], 1)
                if t == 1 and b + 1 < NB:
                    spread(b + 1)
                if t == 2 and b >= 2:
                    k.row_rstd(pool, link, 7, b - 2)
            k.row_rstd(pool, link, 7, NB - 2)
            k.row_rstd(pool, link, 7, NB - 1)
            k.pool_count = link.n

        @block.tensor
        def _(pe):
            mm = nc.tensor.matmul
            k.arrived(pe, "a3_consts")
            k.arrived(pe, "a3_consts")
            for c in range(C):
                last = mm(ps[0:1, OUT_BANK, 0:PROJ], ones[:, :], proj[:, c, :], start=c == 0, stop=c == C - 1)
            last.then_inc(S["made"], 1)
            for b in range(NB):
                if b >= 2:
                    pe.wait_ge(S["made_copied"], PROJECTED + b - 2)
                for c in range(C):
                    last = mm(ps[:, T_BANK + b % 2, 0:PROJ], k.ctxT[:, c, b * P:(b + 1) * P], proj[:, c, :],
                              start=c == 0, stop=c == C - 1)
                last.then_inc(S["made"], 1)

            def query(b):
                if b == 0:
                    k.arrived(pe, "a3_consts")
                pe.wait_ge(k.xn_ready, NB * 6 + b + 1)
                after_first(pe, S["q_copied"], b)
                mm(ps[:, Q_BANK, :], w[:, 0, :], k.xn[:, b % 2, :], start=True, stop=True).then_inc(S["q_ready"], 1)

            query(0)
            pe.wait_ge(S["made_copied"], SUMS)
            k.arrived(pe, "a3_consts")
            pe.wait_ge(S["made_copied"], PROJECTED + NB - 1)
            mm(ps[:, PV_BANK, 0:NB * NK], w[:, 1, :], ck[:, :, :].rearrange("p b k -> p (b k)"), start=True, stop=False)
            mm(ps[:, PV_BANK, 0:NB * NK], brow[:, 0, :], sums_k[:, :, :].rearrange("p b k -> p (b k)"),
               start=False, stop=True).then_inc(S["made"], 1)
            for half in range(2):
                for b in range(4 * half, 4 * half + 4):
                    out = ps[:, OUT_BANK + half, (b % 4) * P:(b % 4 + 1) * P]
                    mm(out, cv[:, b, :], w[:, 2, :], start=True, stop=False)
                    last = mm(out, sums[:, NK:PROJ], brow[:, 1, :], start=False, stop=True)
                last.then_inc(S["made"], 1)
            pe.wait_ge(S["made_copied"], KEYS)
            pe.wait_ge(S["made_copied"], VALUES + 1)

            def scores(u):
                b, t = u // T, u % T
                if t == 0:
                    pe.wait_ge(S["q_copied"], b + 1)
                    pe.wait_ge(S["k_spread"], b + 1)
                after_first(pe, S["shifted"], u - 1)
                mm(ps[:, S_BANK + u % 2, :], q[:, b % 2, t * P:(t + 1) * P],
                   spread_k[:, b % 2, :, :].rearrange("p h k -> p (h k)"), start=True, stop=True)\
                    .then_inc(S["s_ready"], 1)

            def transposes(u):
                pe.wait_ge(S["prob_ready"], u + 1)
                after_first(pe, S["pt_copied"], u - 1)
                k.transpose4(T_BANK + u % 2, prob[:, u % 3, :, :].rearrange("p h k -> p (h k)"))\
                    .then_inc(S["pt_ready"], 1)

            def attend(b):
                pe.wait_ge(S["pt_copied"], T * (b + 1))
                pe.wait_ge(S["v_spread"], b + 1)
                after_first(pe, S["o_copied"], b)
                for j in range(J):
                    last = mm(ps[:, PV_BANK, :], spread_v[:, b % 2, j, :], probT[:, b % 2, j, :],
                              start=j == 0, stop=j == J - 1)
                last.then_inc(S["o_ready"], 1)

            def output(b):
                pe.wait_ge(S["o_copied"], b + 1)
                after_first(pe, S["added"], b - 1)
                mm(ps[:, OUT_BANK + b % 2, :], w[:, 3, :], o[:, b % 2, :], start=True, stop=True)\
                    .then_inc(S["out_ready"], 1)

            for u in range(TILES + 2 * T):
                b, t = u // T, u % T
                if u < TILES:
                    scores(u)
                if 2 <= u < TILES + 2:
                    transposes(u - 2)
                if t == 1 and b + 1 < NB:
                    query(b + 1)
                if t == 2 and 1 <= b <= NB:
                    attend(b - 1)
                if t == 3 and 1 <= b <= NB:
                    output(b - 1)

        @block.scalar
        def _(act):
            act.wait_ge(S["made"], SUMS)
            nc.scalar.copy(sums[:, :], ps[0:1, OUT_BANK, 0:PROJ])
            nc.scalar.copy(sums_k[:, :, :], ps[0:1, OUT_BANK, 0:NK].unsqueeze(1).to_broadcast([1, NB, NK]))\
              .then_inc(S["made_copied"], 1)
            for b in range(NB):
                act.wait_ge(S["made"], PROJECTED + b)
                nc.scalar.copy(ck[:, b, :], ps[:, T_BANK + b % 2, 0:NK])
                nc.scalar.copy(cv[:, b, :], ps[:, T_BANK + b % 2, NK:PROJ]).then_inc(S["made_copied"], 1)

            def query(b):
                act.wait_ge(S["q_ready"], b + 1)
                after_first(act, S["s_ready"], T * (b - 1))
                nc.scalar.activation(q[:, b % 2, :], ps[:, Q_BANK, :], ACT.Identity, bias=bcol[:, 0:1])\
                  .then_inc(S["q_copied"], 1)

            k.arrived(act, "a3_consts")
            query(0)
            act.wait_ge(S["made"], KEYS)
            nc.scalar.copy(keys[:, :, :].rearrange("p b k -> p (b k)"), ps[:, PV_BANK, 0:NB * NK])\
              .then_inc(S["made_copied"], 1)
            for half in range(2):
                act.wait_ge(S["made"], VALUES + half)
                nc.scalar.copy(values[:, 4 * half:4 * half + 4, :].rearrange("p b d -> p (b d)"),
                               ps[:, OUT_BANK + half, :]).then_inc(S["made_copied"], 1)
            for u in range(TILES + 2 * T):
                b, t = u // T, u % T
                if u < TILES:
                    act.wait_ge(S["shifted"], u + 1)
                    nc.scalar.activation(prob[:, u % 3, :, :], prob[:, u % 3, :, :], ACT.Exp, scale=scale)\
                      .then_inc(S["exp_ready"], 1)
                if 2 <= u < TILES + 2:
                    n = u - 2
                    act.wait_ge(S["pt_ready"], n + 1)
                    after_first(act, S["o_ready"], n // T - 1)
                    nc.scalar.copy(probT[:, (n // T) % 2, :, (n % T) * P:(n % T + 1) * P],
                                   ps[:, T_BANK + n % 2, :].rearrange("p (j n) -> p j n", j=J))\
                      .then_inc(S["pt_copied"], 1)
                if t == 1 and b + 1 < NB:
                    query(b + 1)
                if t == 2 and 1 <= b <= NB:
                    act.wait_ge(S["o_ready"], b)
                    after_first(act, S["out_ready"], b - 2)
                    nc.scalar.copy(o[:, (b - 1) % 2, :], ps[:, PV_BANK, :]).then_inc(S["o_copied"], 1)

        @block.vector
        def _(dve):
            link = Link(dve, k.dve_own, k.dve_count)

            def normalise(b):
                after_first(dve, S["q_ready"], b - 1)
                k.normed(dve, 6, b, k.xn[:, b % 2, :]).then_inc(k.xn_ready, 1)

            def shift(u):
                s = ps[:, S_BANK + u % 2, :].rearrange("p (h k) -> p h k", h=H)
                dve.wait_ge(S["s_ready"], u + 1)
                link(nc.vector.tensor_reduce(top[:, u % 2, :], s, AX.X, ALU.max))
                after_first(dve, S["pt_ready"], u - 2)
                nc.vector.tensor_tensor(prob[:, u % 3, :, :], s,
                                        top[:, u % 2, :].unsqueeze(2).to_broadcast([P, H, NK]), ALU.subtract)\
                  .then_inc(S["shifted"], 1)

            def invert(u):
                dve.wait_ge(S["exp_ready"], u + 1)
                link(nc.vector.tensor_reduce(total[:, u % 2, :], prob[:, u % 3, :, :], AX.X, ALU.add))
                after_first(dve, S["prob_ready"], u - 1)
                nc.vector.reciprocal(inv[:, u % 2, :], total[:, u % 2, :]).then_inc(S["inv_ready"], 1)

            normalise(0)
            normalise(1)
            for u in range(TILES + 2 * T + 1):
                b, t = u // T, u % T
                if u < TILES:
                    shift(u)
                if 1 <= u < TILES + 1:
                    invert(u - 1)
                if t == 2 and b + 2 < NB:
                    normalise(b + 2)
                if t == 0 and 2 <= b <= NB + 1:
                    b -= 2
                    dve.wait_ge(S["out_ready"], b + 1)
                    nc.vector.scalar_tensor_tensor(k.x[:, b, :], ps[:, OUT_BANK + b % 2, :], bcol[:, 1:2],
                                                   k.x[:, b, :], ALU.add, ALU.add).then_inc(S["added"], 1)
                    dve.wait_ge(S["added"], b + 1)
                    k.row_stats(dve, link, b)
            k.dve_count = link.n


def packed_linear(k, dram, out):
    nc, ps = k.nc, k.ps
    NIB, BITS = 8, 4
    WORDS = D // NIB
    OUT_BANK, OUT_BANKS, T_BANK = 0, 4, 6
    with ExitStack() as ctx:
        words = k.sb(ctx, "f3_words", [P, D], I32)
        zwords = k.sb(ctx, "f3_zwords", [P, WORDS], I32)
        scale = k.sb(ctx, "f3_scale", [P, D], F16)
        bias = k.sb(ctx, "f3_bias", [P, D], F16)
        q = k.sb(ctx, "f3_q", [P, C, D], I32)
        z = k.sb(ctx, "f3_z", [P, WORDS, NIB], I32)
        wt = k.sb(ctx, "f3_w", [P, C, D], F16)
        xT = k.sb(ctx, "f3_xT", [P, 2, C, P], F16)
        y = k.sb(ctx, "f3_y", [P, 2, D], F16)
        yb = k.sb(ctx, "f3_yb", [P, 2, D], F16)
        S = {n: k.sem("f3_" + n) for n in (
            "w_ready", "xt_copied", "out_ready", "out_copied",
            "added", "stored")}
        block = ctx.enter_context(nc.Block())

        @block.sync
        def _(sp):
            for name, dst in (("words", words[:, :]), ("zwords", zwords[:, :]), ("scale", scale[:, :])):
                k.load(sp, "f3_consts", dst, dram["f3_" + name])
            k.load(sp, "f3_consts", bias[:, :], dram["f3_bias"].partition_broadcast(P))
            for b in range(NB):
                sp.wait_ge(S["added"], b + 1)
                sp.dma_start(out[b], k.x[:, b, :]).then_inc(S["stored"], 16)
            sp.wait_ge(S["stored"], 16 * NB)

        @block.tensor
        def _(pe):
            for i in range(NB + 1):
                if i < NB:
                    pe.wait_ge(k.xn_ready, NB * 7 + i + 1)
                    after_first(pe, S["xt_copied"], i - 1)
                    k.transpose4(T_BANK + i % 2, k.xn[:, i % 2, :]).then_inc(k.xt_ready, 1)
                if i >= 1:
                    b = i - 1
                    if b == 0:
                        pe.wait_ge(S["w_ready"], C)
                    pe.wait_ge(S["xt_copied"], b + 1)
                    after_first(pe, S["out_copied"], b - OUT_BANKS + 1)
                    for j in range(C):
                        last = nc.tensor.matmul(ps[:, OUT_BANK + b % OUT_BANKS, :], xT[:, b % 2, j, :], wt[:, j, :],
                                                start=j == 0, stop=j == C - 1)
                    last.then_inc(S["out_ready"], 1)

        @block.scalar
        def _(act):
            for i in range(NB + 1):
                if i < NB:
                    act.wait_ge(k.xt_ready, NB * 5 + i + 1)
                    after_first(act, S["out_ready"], i - 1)
                    nc.scalar.copy(xT[:, i % 2, :, :].rearrange("p c t -> p (c t)"), ps[:, T_BANK + i % 2, :])\
                      .then_inc(S["xt_copied"], 1)
                if i >= 1:
                    b = i - 1
                    act.wait_ge(S["out_ready"], b + 1)
                    after_first(act, S["added"], b - 1)
                    nc.scalar.copy(y[:, b % 2, :], ps[:, OUT_BANK + b % OUT_BANKS, :]).then_inc(S["out_copied"], 1)

        @block.vector
        def _(dve):
            link = Link(dve, k.dve_own, k.dve_count)

            def normalise(b):
                after_first(dve, k.xt_ready, NB * 5 + b - 1)
                k.normed(dve, 7, b, k.xn[:, b % 2, :].rearrange("p (s r) -> p r s", s=NIB),
                         k.x[:, b, :].rearrange("p (r s) -> p r s", s=NIB)).then_inc(k.xn_ready, 1)

            def unpack(dst, src, s):
                nc.vector.tensor_scalar(dst, src, BITS * s, 15, ALU.logical_shift_right, ALU.bitwise_and)\
                  .then_inc(k.dve_own, 1)
                link.n += 1

            normalise(0)
            normalise(1)
            k.arrived(dve, "f3_consts")
            for j in range(C):
                for h in range(2):
                    rows = slice(h * WORDS, (h + 1) * WORDS)
                    unpack(q[rows, j, :], words[rows, :], 2 * j + h)
            k.arrived(dve, "f3_consts")
            for s in range(NIB):
                unpack(z[:, :, s], zwords[:, :], s)
            dve.wait_ge(k.dve_own, link.n)
            for j in range(C):
                nc.vector.tensor_tensor(wt[:, j, :], q[:, j, :], z[:, :, :].rearrange("p w s -> p (w s)"),
                                        ALU.subtract).then_inc(k.dve_own, 1)
            link.n += C
            k.arrived(dve, "f3_consts")
            for j in range(C):
                dve.wait_ge(k.dve_own, link.n - C + j + 1)
                nc.vector.tensor_tensor(wt[:, j, :], wt[:, j, :], scale[:, :], ALU.mult).then_inc(S["w_ready"], 1)
            k.arrived(dve, "f3_consts")
            for b in range(NB):
                if b + 2 < NB:
                    normalise(b + 2)
                dve.wait_ge(S["out_copied"], b + 1)
                after_first(dve, S["added"], b - 1)
                link(nc.vector.tensor_tensor(yb[:, b % 2, :], y[:, b % 2, :], bias[:, :], ALU.add))
                nc.vector.tensor_tensor(k.x[:, b, :], k.x[:, b, :], yb[:, b % 2, :], ALU.add)\
                  .then_inc(S["added"], 1)




def program(nc, dram, out):
    with ExitStack() as ctx:
        k = Core(nc, ctx, dram)
        cross_attention_over_heads(k, dram["x"], dram["ctxT"], {
            "Wq": dram["a0_wq"], "Wk": dram["a0_wk"], "Wv": dram["a0_wv"], "bqk": dram["a0_bqk"],
            "bv": dram["a0_bv"]})
        ranked_lora(k, {"AG": dram["f0_ag"], "gate_b": dram["f0_gate_b"], "W": dram["f0_w"], "B": dram["f0_bt"],
                        "b": dram["f0_b"]})
        grouped_attention(k, dram)
        mixture_of_experts(k, dram)
        autocorrelation(k, dram)
        scaled_linear(k, dram)
        token_attention(k, dram)
        packed_linear(k, dram, out)


def rows128(a):
    return np.ascontiguousarray(a.reshape(-1, P, a.shape[-1]).transpose(1, 0, 2))


def columns(a):
    return np.ascontiguousarray(a.reshape(-1, P).T)


def rope_table(positions, dim, theta):
    freq = (1.0 / np.float32(theta) ** (np.arange(0, dim, 2, dtype=np.float32) / np.float32(dim))).astype(np.float32)
    angle = np.arange(positions, dtype=np.float32)[:, None] * freq
    c, s = np.cos(angle), np.sin(angle)
    return rows128(np.concatenate([c, c, s, -s], axis=1).astype(np.float32))


def shares(vision):
    text = np.arange(P) >= vision
    return np.stack([text / ((P - vision) * D), ~text / (vision * D)], axis=1).astype(np.float32)


def transform_tables():
    t, f = np.arange(P)[:, None], np.arange(P // 2)[None, :]
    angle = 2 * np.pi * t * f / P
    cos, sin, flip = np.cos(angle), np.sin(angle), np.cos(np.pi * t)
    to_q = np.concatenate([cos, flip, sin[:, 1:]], axis=1)
    to_k2 = np.concatenate([sin, 0 * flip, -cos[:, 1:]], axis=1)
    from_1 = np.concatenate([0.5 * cos[:, :1], cos[:, 1:], 0.5 * flip, cos[:, 1:]], axis=1).T * (2 / P)
    from_2 = np.concatenate([0 * flip, -sin[:, 1:], 0 * flip, -sin[:, 1:]], axis=1).T * (2 / P)
    odd = 2 * np.pi * t * (np.arange(P)[None, :] + 0.5) / (2 * P)
    wc, ws = np.cos(odd), np.sin(odd)
    vc, vs = wc.copy(), ws.copy()
    vc[-1], vs[-1] = -wc[:-1].sum(axis=0), -ws[:-1].sum(axis=0)
    last = np.zeros((P, P))
    last[-1] = 1.0
    tables = [to_q, to_k2, vc, vs, from_1, from_2, wc, ws, wc.T / P, -ws.T / P, ws.T / P, last]
    return np.stack(tables, axis=1).astype(np.float32)


def layouts(i):
    ctx = i["ctx_4096"].reshape(TOK, D)
    ctxT = rows128(ctx.T)
    channel = np.arange(P)
    row0 = np.zeros((P, P), np.float32)
    row0[0] = 1.0
    return {
        "ident": np.eye(P, dtype=np.float32),
        "x": i["x"],
        "ctxT": np.stack([ctxT[:, :, :512], ctxT[:, :, 512:]]),
        "a0_wq": rows128(i["L0_xattn_Wq"].T), "a0_wk": rows128(i["L0_xattn_Wk"].T),
        "a0_wv": rows128(i["L0_xattn_Wv"].T),
        "a0_bqk": np.stack([columns(i["L0_xattn_bq"]), columns(i["L0_xattn_bk"])], axis=1),
        "a0_bv": i["L0_xattn_bv"],
        "f0_w": rows128(i["L0_ffn_W"].T), "f0_b": i["L0_ffn_b"],
        "f0_ag": rows128(np.concatenate([i["L0_ffn_A"], i["L0_ffn_gate_w"]]).T),
        "f0_gate_b": i["L0_ffn_gate_b"], "f0_bt": i["L0_ffn_B"].T,
        "pos": i["pos_BxS2"].reshape(TOK), "mask": i["mask_BxSxS2_ik0"].transpose(1, 0, 2),
        "a1_iota": columns(np.arange(512, dtype=np.float32)), "a1_rope": rope_table(512, P, 10000.0),
        "a1_wq": i["L1_xattn_Wq"].reshape(C, P, 8, 4, P).transpose(2, 3, 1, 0, 4),
        "a1_wk": i["L1_xattn_Wk"].reshape(C, P, 8, P).transpose(2, 1, 0, 3),
        "a1_wv": i["L1_xattn_Wv"].reshape(C, P, 8, P).transpose(1, 2, 0, 3),
        "f1_gw": rows128(np.pad(i["L1_ffn_gate_w"][:D], ((0, 0), (0, 1)))), "f1_gw_ratio": i["L1_ffn_gate_w"][D], "f1_gb": i["L1_ffn_gate_b"],
        "f1_ones": np.ones((P, P), np.float32), "f1_row0": row0, "f1_share": shares(int(P * 0.3)),
        "f1_b1": i["L1_ffn_b1"].reshape(3, C, P).transpose(2, 0, 1), "f1_b2": i["L1_ffn_b2"],
        "f1_w1": i["L1_ffn_w1"].reshape(3, C, P, D).transpose(0, 2, 1, 3),
        "f1_w2": i["L1_ffn_w2"].reshape(3, C, P, D).transpose(0, 2, 1, 3),
        "ctx": i["ctx_4096"], "a2_table": transform_tables(),
        "f2_w": rows128(i["L2_ffn_weight"].T), "f2_scale": i["L2_ffn_weight_scale_inv"].T.reshape(C * C),
        "f2_bias": i["L2_ffn_bias"],
        "a3_w": np.stack([i[f"L3_xattn_W{n}"].T for n in "qkvm"], axis=1),
        "a3_proj": rows128(np.concatenate([i["L3_xattn_proj_k"]] + [i["L3_xattn_proj_v"]] * 4, axis=1)),
        "a3_bcol": np.stack([i["L3_xattn_bq"], i["L3_xattn_bm"]], axis=1),
        "a3_brow": np.stack([i["L3_xattn_bk"], i["L3_xattn_bv"]])[None],
        "a3_ones": np.ones((P, 1), np.float32),
        "a3_of_head": (channel[:, None] % 16 == np.arange(16)).astype(np.float32),
        "a3_of_pair": (4 * np.arange(4)[None, :, None] + channel[:, None, None] // 32
                       == channel[None, None, :] % 16).astype(np.float32),
        "f3_words": np.tile(i["L3_ffn_qweight"], (2, 1)),
        "f3_zwords": np.tile(np.repeat(i["L3_ffn_qzeros"], 16, axis=0), (2, 1)),
        "f3_scale": np.tile(np.repeat(i["L3_ffn_scales"], 16, axis=0), (2, 1)), "f3_bias": i["L3_ffn_bias"],
        "a1_wo": i["L1_xattn_Wo"].reshape(8, 4, P, D).transpose(0, 2, 1, 3),
    }


def kernel(**inputs):
    import concourse.bacc as bacc
    from concourse.bass_utils import run_bass_kernel_spmd

    nc = bacc.Bacc("TRN2", target_bir_lowering=False, num_devices=1)
    arrays, dram = {}, {}
    for name, a in layouts({n: np.asarray(a) for n, a in inputs.items()}).items():
        a = np.ascontiguousarray(a)
        arrays[f"in_{name}"] = a
        dram[name] = nc.dram_tensor(f"in_{name}", a.shape, mybir.dt.from_np(a.dtype), kind="ExternalInput").ap()
    out = nc.dram_tensor("out_x", (NB, P, D), F32, kind="ExternalOutput").ap()
    program(nc, dram, out)
    r = run_bass_kernel_spmd(nc, [arrays], core_ids=[0])
    return r.results[0]["out_x"]
```

```python
import numpy as np

import concourse.bass as bass
from concourse import mybir
from contextlib import ExitStack

F32 = mybir.dt.float32
F16 = mybir.dt.float16
I32 = mybir.dt.int32
F32R = mybir.dt.float32r
ALU = mybir.AluOpType
ACT = mybir.ActivationFunctionType
AX = mybir.AxisListType

P = 128
NB = 8
D = 512
C = D // P
TOK = NB * P
EPS = 1e-5
LOWEST = -3.0e38


HI, LO = 0, 1


def after_first(eng, sem, value):
    if isinstance(value, int) and value <= 0:
        return
    eng.wait_ge(sem, value)


def split_product(nc, out, weights, moving, first=True, last=True):
    nc.tensor.matmul(out, weights[HI], moving[HI], start=first, stop=False)
    nc.tensor.matmul(out, weights[HI], moving[LO], start=False, stop=False)
    return nc.tensor.matmul(out, weights[LO], moving[HI], start=False, stop=last)


def parts(tile, *at):
    return [tile[(slice(None), part, *at)] for part in (HI, LO)]


def low_part(engine, out, whole, high):
    return engine.tensor_tensor(out, whole, high.bitcast(F32), ALU.subtract)


class Link:

    def __init__(self, eng, sem, n=0):
        self.eng, self.sem, self.n = eng, sem, n

    def __call__(self, ins):
        self.n += 1
        ins.then_inc(self.sem, 1)
        self.eng.wait_ge(self.sem, self.n)


class Core:

    def __init__(self, nc, ctx, dram):
        self.nc, self.ctx, self.dram = nc, ctx, dram
        self.x = self.sb(ctx, "x", [P, NB, D])
        self.ctxT = self.sb(ctx, "ctxT", [P, C, TOK])
        self.ident = self.sb(ctx, "ident", [P, P])
        self.xn = self.sb(ctx, "xn", [P, 2, D])
        self.stats = self.sb(ctx, "stats", [P, NB, 6])
        self.meanvar = self.sb(ctx, "meanvar", [P, NB, 2])
        self.varpe = self.sb(ctx, "varpe", [P, NB])
        self.rstd = self.sb(ctx, "rstd", [P, NB])
        self.mhalf = self.sb(ctx, "mhalf", [P, 1])
        self.ps = ctx.enter_context(nc.psum_tensor("ps", [P, 8, 512], F32))
        self.var_ready = self.sem("var_ready")
        self.rstd_ready = self.sem("rstd_ready")
        self.xn_ready = self.sem("xn_ready")
        self.xt_ready = self.sem("xt_ready")
        self.xt_copied = self.sem("xt_copied")
        self.dve_own = self.sem("dve_own")
        self.pool_own = self.sem("pool_own")
        self.loaded = {}
        self.dve_count = 0
        self.pool_count = 0

    def sb(self, ctx, name, shape, dt=F32):
        return ctx.enter_context(self.nc.sbuf_tensor(name, shape, dt))

    def sem(self, name):
        return self.ctx.enter_context(self.nc.semaphore(name))

    def load(self, eng, name, dst, src):
        if name not in self.loaded:
            self.loaded[name] = [self.sem(f"{name}_loaded"), 0]
        sem, _ = self.loaded[name]
        eng.dma_start(dst, src).then_inc(sem, 16)
        self.loaded[name][1] += 16

    def arrived(self, eng, name):
        eng.wait_ge(*self.loaded[name])

    def row_stats(self, dve, link, b):
        link(self.nc.vector.bn_stats(self.stats[:, b, :], self.x[:, b, :]))
        self.nc.vector.bn_aggr(self.meanvar[:, b, :], self.stats[:, b, :]).then_inc(self.var_ready, 1)

    def row_rstd(self, pool, link, layer, b):
        pool.wait_ge(self.var_ready, NB * layer + b + 1)
        link(self.nc.gpsimd.tensor_scalar(self.varpe[:, b:b + 1], self.meanvar[:, b, 1:2], EPS, None, ALU.add))
        self.nc.gpsimd.tensor_tensor(self.rstd[:, b:b + 1], self.varpe[:, b:b + 1], self.mhalf[:, :],
                                     ALU.pow).then_inc(self.rstd_ready, 1)

    def normed(self, dve, layer, b, out, row=None):
        dve.wait_ge(self.rstd_ready, NB * layer + b + 1)
        return self.nc.vector.tensor_scalar(out, self.x[:, b, :] if row is None else row, self.meanvar[:, b, 0:1],
                                            self.rstd[:, b:b + 1], ALU.subtract, ALU.mult)

    def transpose4(self, bank, src):
        for c in range(C):
            last = self.nc.tensor.transpose(self.ps[:, bank, c * P:(c + 1) * P], src[:, c * P:(c + 1) * P],
                                            self.ident[:, :])
        return last


def row_block(ap):
    return ap.rearrange("(c p) n -> p c n", p=P)


def cross_attention_over_heads(k, x_dram, ctxT_dram, w):
    nc = k.nc
    H, HD = 16, 32
    R = P // HD
    scale = 1.0 / float(np.sqrt(HD))
    with ExitStack() as ctx:
        bqk = k.sb(ctx, "a0_bqk", [P, 2, C])
        bv = k.sb(ctx, "a0_bv", [P, D])
        qT = k.sb(ctx, "a0_qT", [P, C, TOK])
        kT = k.sb(ctx, "a0_kT", [P, C, TOK])
        v = k.sb(ctx, "a0_v", [P, NB * D + P - HD])
        rowmax = k.sb(ctx, "a0_rowmax", [P, NB, P])
        allmax = k.sb(ctx, "a0_allmax", [P, P])
        total = k.sb(ctx, "a0_total", [P, P])
        inv = k.sb(ctx, "a0_inv", [P, P])
        with ExitStack() as early:
            c_parts = k.sb(early, "a0_ctx", [P, 2, C, TOK], F32R)
            x_parts = k.sb(early, "a0_xT", [P, 2, C, TOK], F32R)
            w_parts = k.sb(early, "a0_w", [P, 2, 2, C, D], F32R)
            whole = k.sb(early, "a0_whole", [P, 2, C, D])
        apart = k.sb(ctx, "a0_apart", [P, 2, C, R, P])
        E = k.sb(ctx, "a0_E", [P, NB, C, R, P])
        S = {n: k.sem("a0_" + n) for n in (
            "kq_ready", "kq_copied", "v_ready",
            "v_copied", "scores_ready", "scores_copied", "max_ready", "shifted_pool", "shifted", "exp_ready", "sum_ready", "probs_dve", "probs_pool", "inv_ready",
            "out_ready", "added", "zeroed", "apart_pool", "apart_dve",
            "w_high", "wk_low", "w_low", "ctx_high", "ctx_low", "xt_low")}
        WK, WV, WQ = 0, 1, 2
        PE_ROWS, POOL_PAIR, DVE_PAIR = (0, 1, 2, 3), (5, 6), (4, 7)
        EXP_ORDER = (0, 1, 5, 2, 3, 6, 4, 7)
        assert DVE_PAIR[1] == NB - 1
        POOL_ROWS = (2, 5)
        block = ctx.enter_context(nc.Block())
        ps = k.ps
        last_scores = ps[:, 4 * ((NB - 1) % 2):4 * ((NB - 1) % 2) + 4, :]

        def part_heads(eng, engine, sem, heads, b):
            eng.wait_ge(S["kq_copied"], 12 + 4 * (b // 4))
            after_first(eng, S["scores_ready"], b - 1)
            for r in heads:
                rows = slice(HD * r, HD * (r + 1))
                engine.tensor_copy(apart[rows, b % 2, :, r, :], qT[rows, :, b * P:(b + 1) * P]).then_inc(sem, 1)

        def divide(engine, sem, b):
            e = E[:, b, :, :, :].rearrange("p c r q -> p (c r) q")
            engine.tensor_tensor(e, e, inv[:, :].unsqueeze(1).to_broadcast([P, H, P]), ALU.mult).then_inc(sem, 1)

        def shift(engine, sem, b):
            e = E[:, b, :, :, :].rearrange("p c r q -> p (c r) q")
            scores = e if b < NB - 1 else last_scores.rearrange("p c (r q) -> p (c r) q", r=R)
            engine.tensor_tensor(e, scores, allmax[:, :].unsqueeze(1).to_broadcast([P, H, P]), ALU.subtract)\
              .then_inc(sem, 1)

        def sum_pair(eng, engine, sem, slot, pair):
            eng.wait_ge(S["exp_ready"], max(EXP_ORDER.index(b) for b in pair) + 1)
            e0, e1 = (E[:, b, :, :, :].rearrange("p c r q -> p (c r q)") for b in pair)
            engine.tensor_tensor(apart[:, slot, :, :, :].rearrange("p c r q -> p (c r q)"), e0, e1, ALU.add)\
              .then_inc(sem, 1)

        def w_low(eng, engine, sem, i):
            eng.wait_ge(S["w_high"], i + 1)
            low_part(engine, w_parts[:, LO, i % 2, :, :], whole[:, i % 2, :, :], w_parts[:, HI, i % 2, :, :])\
              .then_inc(sem, 1)

        @block.sync
        def _(sp):
            k.load(sp, "a0_w0", whole[:, 0, :, :], w["Wk"])
            k.load(sp, "ctxT0", k.ctxT[:, :, 0:512], ctxT_dram[0])
            k.load(sp, "a0_k", k.ident[:, :], k.dram["ident"])
            k.load(sp, "a0_k", bqk[:, :, :], w["bqk"])
            k.load(sp, "ctxT1", k.ctxT[:, :, 512:TOK], ctxT_dram[1])
            k.load(sp, "a0_w1", whole[:, 1, :, :], w["Wv"])
            k.load(sp, "a0_v", bv[:, :], w["bv"].partition_broadcast(P))
            for b in range(NB):
                k.load(sp, f"x{b // 2}", k.x[:, b, :], x_dram[b])
            sp.wait_ge(S["wk_low"], 1)
            k.load(sp, "a0_w2", whole[:, 0, :, :], w["Wq"])

        @block.gpsimd
        def _(pool):
            link = Link(pool, k.pool_own)
            link(nc.gpsimd.memset(k.mhalf[:, :], -0.5))
            link(nc.gpsimd.memset(v[:, NB * D:], 0.0))
            w_low(pool, nc.gpsimd, S["w_low"], WV)
            for b in range(NB):
                k.row_rstd(pool, link, 0, b)
            w_low(pool, nc.gpsimd, S["w_low"], WQ)
            pool.wait_ge(S["v_ready"], NB)
            nc.gpsimd.memset(apart[:, :, :, :, :].rearrange("p s c r q -> p (s c r q)"), 0.0)\
              .then_inc(S["zeroed"], 1)
            pool.wait_ge(S["zeroed"], 1)
            for b in range(NB):
                part_heads(pool, nc.gpsimd, S["apart_pool"], range(1), b)
            pool.wait_ge(S["max_ready"], NB - 1)
            for b in POOL_PAIR:
                shift(nc.gpsimd, S["shifted_pool"], b)
            sum_pair(pool, nc.gpsimd, S["apart_pool"], 0, POOL_PAIR)
            pool.wait_ge(S["inv_ready"], 1)
            for b in POOL_ROWS:
                divide(nc.gpsimd, S["probs_pool"], b)
            for b in range(NB):
                k.row_rstd(pool, link, 1, b)
            k.pool_count = link.n

        @block.tensor
        def _(pe):
            def project(u, bank, weight, acts, o, half):
                if u >= 2:
                    pe.wait_ge(S["kq_copied"], u - 1)
                for c in range(C):
                    last = split_product(nc, ps[:, bank, :],
                                         parts(w_parts, weight % 2, c, slice(o * P, (o + 1) * P)),
                                         parts(acts, c, slice(half * 512, (half + 1) * 512)), c == 0, c == C - 1)
                last.then_inc(S["kq_ready"], 1)

            def turn_rows(b):
                pe.wait_ge(k.xn_ready, b + 1)
                if b >= 2:
                    pe.wait_ge(S["xt_low"], b - 1)
                k.transpose4(4 + b % 2, k.xn[:, b % 2, :]).then_inc(k.xt_ready, 1)

            pe.wait_ge(S["wk_low"], 1)
            u = 0
            for half in range(2):
                pe.wait_ge(S["ctx_low"], half + 1)
                for o in range(C):
                    project(u, u % 2, WK, c_parts, o, half)
                    if u >= 1:
                        turn_rows(u - 1)
                    u += 1
            k.arrived(pe, "a0_k")
            turn_rows(NB - 1)
            pe.wait_ge(S["w_low"], WV)
            for b in range(NB):
                if b >= 2:
                    pe.wait_ge(S["v_copied"], b - 1)
                for c in range(C):
                    last = split_product(nc, ps[:, 2 + b % 2, :], parts(c_parts, c, slice(b * P, (b + 1) * P)),
                                         parts(w_parts, WV % 2, c), c == 0, c == C - 1)
                last.then_inc(S["v_ready"], 1)
            pe.wait_ge(S["w_low"], WQ)
            for half in range(2):
                pe.wait_ge(S["xt_low"], 4 * half + 4)
                for o in range(C):
                    project(u, u % 2, WQ, x_parts, o, half)
                    u += 1
            pe.wait_ge(S["kq_copied"], 16)
            pe.wait_ge(S["v_copied"], NB)
            for b in range(NB):
                if b >= 2:
                    pe.wait_ge(S["scores_copied"], b - 1)
                pe.wait_ge(S["apart_pool"], b + 1)
                pe.wait_ge(S["apart_dve"], (R - 1) * (b + 1))
                for c in range(C):
                    last = nc.tensor.matmul(ps[:, 4 * (b % 2) + c, :], kT[:, c, b * P:(b + 1) * P],
                                            apart[:, b % 2, c, :, :].rearrange("p r q -> p (r q)"),
                                            start=True, stop=True)
                last.then_inc(S["scores_ready"], 1)
            pe.wait_ge(S["scores_copied"], NB - 1)
            def add_heads(heads, first=False, last=False):
                for c in range(C):
                    done = nc.tensor.matmul(ps[:, 0, :], k.ident[:, :], heads[:, c, :, :].rearrange("p r q -> p (r q)"),
                                            start=first and c == 0, stop=last and c == C - 1)
                return done

            for b in PE_ROWS:
                pe.wait_ge(S["exp_ready"], EXP_ORDER.index(b) + 1)
                add_heads(E[:, b, :, :, :], first=b == 0)
            pe.wait_ge(S["apart_pool"], NB + 1)
            add_heads(apart[:, 0, :, :, :])
            pe.wait_ge(S["apart_dve"], (R - 1) * NB + 1)
            add_heads(apart[:, 1, :, :, :], last=True).then_inc(S["sum_ready"], 1)
            for b in range(NB):
                if b in POOL_ROWS:
                    pe.wait_ge(S["probs_pool"], POOL_ROWS.index(b) + 1)
                else:
                    pe.wait_ge(S["probs_dve"], b + 1 - sum(row < b for row in POOL_ROWS))
                if b >= 2:
                    pe.wait_ge(S["added"], b - 1)
                for c in range(C):
                    for r in range(R):
                        h = R * c + r
                        last = nc.tensor.matmul(ps[:, 4 * (b % 2) + c, r * P:(r + 1) * P], E[:, b, c, r, :],
                                                v[:, b * D + h * HD:b * D + h * HD + P], start=True, stop=True)
                last.then_inc(S["out_ready"], 1)

        @block.scalar
        def _(act):
            def copy_kq(u, dst, which, o, half):
                act.wait_ge(S["kq_ready"], u + 1)
                nc.scalar.activation(dst[:, o, half * 512:(half + 1) * 512], ps[:, u % 2, :], ACT.Identity,
                                     bias=bqk[:, which, o:o + 1]).then_inc(S["kq_copied"], 1)

            def w_high(i):
                k.arrived(act, f"a0_w{i}")
                if i == WQ:
                    act.wait_ge(S["kq_ready"], 8)
                nc.scalar.copy(w_parts[:, HI, i % 2, :, :], whole[:, i % 2, :, :]).then_inc(S["w_high"], 1)

            def ctx_high(half):
                tok = slice(half * 512, (half + 1) * 512)
                k.arrived(act, f"ctxT{half}")
                nc.scalar.copy(c_parts[:, HI, :, tok], k.ctxT[:, :, tok]).then_inc(S["ctx_high"], 1)

            w_high(WK)
            ctx_high(0)
            ctx_high(1)
            w_high(WV)
            k.arrived(act, "a0_k")
            def copy_x(b):
                act.wait_ge(k.xt_ready, b + 1)
                nc.scalar.copy(x_parts[:, HI, :, b * P:(b + 1) * P],
                               ps[:, 4 + b % 2, :].rearrange("p (c t) -> p c t", c=C)).then_inc(k.xt_copied, 1)

            for u in range(8):
                copy_kq(u, kT, 1, u % C, u // C)
                if u >= 1:
                    copy_x(u - 1)
            copy_x(NB - 1)
            w_high(WQ)
            for u in range(8):
                copy_kq(8 + u, qT, 0, u % C, u // C)
            for b in range(NB - 1):
                act.wait_ge(S["scores_ready"], b + 1)
                nc.scalar.copy(E[:, b, :, :, :].rearrange("p c r q -> p (c r q)"),
                               ps[:, 4 * (b % 2):4 * (b % 2) + 4, :].rearrange("p c n -> p (c n)"))\
                  .then_inc(S["scores_copied"], 1)
            for b in EXP_ORDER:
                if b in POOL_PAIR:
                    act.wait_ge(S["shifted_pool"], POOL_PAIR.index(b) + 1)
                else:
                    act.wait_ge(S["shifted"], (*PE_ROWS, *DVE_PAIR).index(b) + 1)
                e = E[:, b, :, :, :].rearrange("p c r q -> p (c r q)")
                nc.scalar.activation(e, e, ACT.Exp, scale=scale).then_inc(S["exp_ready"], 1)

        @block.vector
        def _(dve):
            link = Link(dve, k.dve_own)

            def x_low(b):
                tok = slice(b * P, (b + 1) * P)
                dve.wait_ge(k.xt_copied, b + 1)
                low_part(nc.vector, x_parts[:, LO, :, tok], ps[:, 4 + b % 2, :].rearrange("p (c t) -> p c t", c=C),
                         x_parts[:, HI, :, tok]).then_inc(S["xt_low"], 1)

            w_low(dve, nc.vector, S["wk_low"], WK)
            for half in range(2):
                tok = slice(half * 512, (half + 1) * 512)
                dve.wait_ge(S["ctx_high"], half + 1)
                low_part(nc.vector, c_parts[:, LO, :, tok], k.ctxT[:, :, tok], c_parts[:, HI, :, tok])\
                  .then_inc(S["ctx_low"], 1)
            for b in range(NB):
                k.arrived(dve, f"x{b // 2}")
                k.row_stats(dve, link, b)
                if b >= 1:
                    if b >= 3:
                        dve.wait_ge(k.xt_ready, b - 2)
                    k.normed(dve, 0, b - 1, k.xn[:, (b - 1) % 2, :]).then_inc(k.xn_ready, 1)
                    if b >= 2:
                        x_low(b - 2)
            dve.wait_ge(k.xt_ready, NB - 2)
            k.normed(dve, 0, NB - 1, k.xn[:, (NB - 1) % 2, :]).then_inc(k.xn_ready, 1)
            x_low(NB - 2)
            x_low(NB - 1)
            k.arrived(dve, "a0_v")
            for b in range(NB):
                dve.wait_ge(S["v_ready"], b + 1)
                nc.vector.tensor_tensor(v[:, b * D:(b + 1) * D], ps[:, 2 + b % 2, :], bv[:, :], ALU.add).then_inc(S["v_copied"], 1)
            dve.wait_ge(S["zeroed"], 1)
            for b in range(2):
                part_heads(dve, nc.vector, S["apart_dve"], range(1, R), b)
            for b in range(NB):
                if b + 2 < NB:
                    part_heads(dve, nc.vector, S["apart_dve"], range(1, R), b + 2)
                dve.wait_ge(*((S["scores_copied"], b + 1) if b < NB - 1 else (S["scores_ready"], NB)))
                scores = E[:, b, :, :, :] if b < NB - 1 else last_scores.rearrange("p c (r q) -> p c r q", r=R)
                link(nc.vector.tensor_reduce(rowmax[:, b, :] if b else allmax[:, :],
                                             scores.rearrange("p c r q -> p q (c r)"), AX.X, ALU.max))
                if b:
                    nc.vector.tensor_tensor(allmax[:, :], allmax[:, :], rowmax[:, b, :], ALU.max)\
                      .then_inc(S["max_ready"], 1)
                    dve.wait_ge(S["max_ready"], b)
            for b in (*PE_ROWS, *DVE_PAIR):
                shift(nc.vector, S["shifted"], b)
            sum_pair(dve, nc.vector, S["apart_dve"], 1, DVE_PAIR)
            dve.wait_ge(S["sum_ready"], 1)
            link(nc.vector.tensor_reduce(total[:, :], ps[:, 0, :].rearrange("p (r q) -> p q r", r=R), AX.X, ALU.add))
            nc.vector.reciprocal(inv[:, :], total[:, :]).then_inc(S["inv_ready"], 1)
            dve.wait_ge(S["inv_ready"], 1)
            for i in range(-1, NB + 1):
                if i + 1 < NB and i + 1 not in POOL_ROWS:
                    divide(nc.vector, S["probs_dve"], i + 1)
                if i >= 1:
                    b = i - 1
                    dve.wait_ge(S["out_ready"], b + 1)
                    x = k.x[:, b, :].rearrange("p (d c r) -> p c r d", c=C, r=R)
                    out = ps[:, 4 * (b % 2):4 * (b % 2) + 4, :].rearrange("p c (r n) -> p c r n", r=R)[:, :, :, 0:HD]
                    nc.vector.tensor_tensor(x, x, out, ALU.add).then_inc(S["added"], 1)
                    dve.wait_ge(S["added"], b + 1)
                    k.row_stats(dve, link, b)
            k.dve_count = link.n


def ranked_lora(k, w, dram, a):
    nc, ps = k.nc, k.ps
    RANKS = (8, 16, 32, 64)
    NR, MAXR = len(RANKS), RANKS[-1]
    MC = dram["a1_rope"].shape[1]
    HALF = TOK // 2
    with ExitStack() as ctx:
        wt = k.sb(ctx, "f0_w", [P, C, D])
        ag = k.sb(ctx, "f0_ag", [P, C, MAXR + NR])
        bt = k.sb(ctx, "f0_bt", [MAXR, D])
        bias = k.sb(ctx, "f0_bias", [P, D])
        gate_b = k.sb(ctx, "f0_gate_b", [P, NR])
        xT = k.sb(ctx, "f0_xT", [P, NB, C, P])
        low = k.sb(ctx, "f0_low", [P, NB, MAXR + NR])
        gated = k.sb(ctx, "f0_gated", [P, NB, MAXR])
        scores = k.sb(ctx, "f0_scores", [P, NB, NR])
        before = k.sb(ctx, "f0_before", [P, NB, NR])
        after = k.sb(ctx, "f0_after", [P, NB, NR])
        keep = k.sb(ctx, "f0_keep", [P, NB, NR])
        gatedT = k.sb(ctx, "f0_gatedT", [MAXR, 2, P])
        pos_i = k.sb(ctx, "a1_pos_i", [P, TOK], I32)
        pos = k.sb(ctx, "a1_pos", [P, TOK])
        wrap = k.sb(ctx, "a1_wrap", [P, TOK])
        iota = k.sb(ctx, "a1_iota", [P, MC])
        rope = k.sb(ctx, "a1_rope", [P, MC, 2 * P])
        rope_parts = k.sb(ctx, "a1_rope_parts", [P, 2, MC, 2 * P], F32R)
        onehot = k.sb(ctx, "a1_onehot", [P, MC, TOK], F32R)
        S = {n: k.sem("f0_" + n) for n in (
            "onehot_ready", "rope_high", "rope_low", "table_ready", "table_copied",
            "low_ready", "low_copied", "biased", "gated", "gt_ready",
            "gt_copied", "out_ready", "added")}
        block = ctx.enter_context(nc.Block())

        @block.sync
        def _(sp):
            k.load(sp, "f0_low", ag[:, :, :], w["AG"])
            k.load(sp, "f0_low", gate_b[:, :], w["gate_b"].partition_broadcast(P))
            k.load(sp, "f0_w", wt[:, :, :], w["W"])
            k.load(sp, "f0_out", bt[:, :], w["B"])
            k.load(sp, "f0_out", bias[:, :], w["b"].partition_broadcast(P))
            k.load(sp, "a1_tables", pos_i[:, :], dram["pos"].partition_broadcast(P))
            k.load(sp, "a1_tables", iota[:, :], dram["a1_iota"])
            k.load(sp, "a1_tables", rope[:, :, :], dram["a1_rope"])
            load_grouped_attention(k, sp, dram, a)

        @block.gpsimd
        def _(pool):
            link = Link(pool, k.pool_own, k.pool_count)
            k.arrived(pool, "f0_out")
            for b in range(NB):
                pool.wait_ge(k.xn_ready, NB + b + 1)
                nc.gpsimd.tensor_tensor(k.x[:, b, :], k.x[:, b, :], bias[:, :], ALU.add).then_inc(S["biased"], 1)
            pool.wait_ge(S["rope_high"], 1)
            low_part(nc.gpsimd, rope_parts[:, LO, :, :], rope[:, :, :], rope_parts[:, HI, :, :])\
              .then_inc(S["rope_low"], 1)
            for b in range(NB):
                k.row_rstd(pool, link, 2, b)
            k.pool_count = link.n

        @block.tensor
        def _(pe):
            def low_rank(b):
                pe.wait_ge(k.xt_copied, NB + b + 1)
                if b >= 2:
                    pe.wait_ge(S["low_copied"], b - 1)
                for c in range(C):
                    last = nc.tensor.matmul(ps[:, b % 2, 0:MAXR + NR], xT[:, b, c, :], ag[:, c, :],
                                            start=c == 0, stop=c == C - 1)
                last.then_inc(S["low_ready"], 1)

            for b in range(NB):
                pe.wait_ge(k.xn_ready, NB + b + 1)
                if b >= 2:
                    pe.wait_ge(k.xt_copied, NB + b - 1)
                k.transpose4(6 + b % 2, k.xn[:, b % 2, :]).then_inc(k.xt_ready, 1)
                if b == 0:
                    k.arrived(pe, "f0_low")
                else:
                    low_rank(b - 1)
            low_rank(NB - 1)
            k.arrived(pe, "f0_w")
            for i in range(NB + 2):
                if i < NB:
                    if i >= 4:
                        pe.wait_ge(S["added"], i - 3)
                    for c in range(C):
                        nc.tensor.matmul(ps[:, 2 + i % 4, :], xT[:, i, c, :], wt[:, c, :], start=c == 0, stop=False)
                if 1 <= i <= NB:
                    b = i - 1
                    if b == 0:
                        pe.wait_ge(S["gated"], NR)
                    if b >= 2:
                        pe.wait_ge(S["gt_copied"], b - 1)
                    nc.tensor.transpose(ps[0:MAXR, 6 + b % 2, 0:P], gated[:, b, :], k.ident[:, :])\
                      .then_inc(S["gt_ready"], 1)
                if i >= 2:
                    b = i - 2
                    if b == 0:
                        k.arrived(pe, "f0_out")
                    pe.wait_ge(S["gt_copied"], b + 1)
                    nc.tensor.matmul(ps[:, 2 + b % 4, :], gatedT[:, b % 2, :], bt[:, :], start=False, stop=True)\
                      .then_inc(S["out_ready"], 1)

            pe.wait_ge(S["rope_low"], 1)
            pe.wait_ge(S["onehot_ready"], MC)
            pe.wait_ge(S["low_copied"], NB)
            for n in range(4):
                tab, half = n // 2, n % 2
                after_first(pe, S["table_copied"], n - 1)
                for c in range(MC):
                    for part in (HI, LO):
                        last = nc.tensor.matmul(ps[:, n % 2, :], rope_parts[:, part, c, tab * P:(tab + 1) * P],
                                                onehot[:, c, half * HALF:(half + 1) * HALF],
                                                start=c == 0 and part == HI, stop=c == MC - 1 and part == LO)
                last.then_inc(S["table_ready"], 1)

        @block.scalar
        def _(act):
            for b in range(NB):
                act.wait_ge(k.xt_ready, NB + b + 1)
                nc.scalar.copy(xT[:, b, :, :].rearrange("p c t -> p (c t)"), ps[:, 6 + b % 2, :])\
                  .then_inc(k.xt_copied, 1)
                if b >= 1:
                    act.wait_ge(S["low_ready"], b)
                    nc.scalar.copy(low[:, b - 1, :], ps[:, (b - 1) % 2, 0:MAXR + NR]).then_inc(S["low_copied"], 1)
            act.wait_ge(S["low_ready"], NB)
            nc.scalar.copy(low[:, NB - 1, :], ps[:, (NB - 1) % 2, 0:MAXR + NR]).then_inc(S["low_copied"], 1)
            k.arrived(act, "a1_tables")
            nc.scalar.copy(rope_parts[:, HI, :, :], rope[:, :, :]).then_inc(S["rope_high"], 1)
            for b in range(NB):
                act.wait_ge(S["gt_ready"], b + 1)
                if b >= 2:
                    act.wait_ge(S["out_ready"], b - 1)
                nc.scalar.copy(gatedT[:, b % 2, :], ps[0:MAXR, 6 + b % 2, 0:P]).then_inc(S["gt_copied"], 1)

            for n in range(4):
                act.wait_ge(S["table_ready"], n + 1)
                nc.scalar.copy(a["cos" if n < 2 else "sin"][:, n % 2 * HALF:(n % 2 + 1) * HALF], ps[:, n % 2, :])\
                  .then_inc(S["table_copied"], 1)

        @block.vector
        def _(dve):
            link = Link(dve, k.dve_own, k.dve_count)
            for b in range(NB):
                if b >= 2:
                    dve.wait_ge(k.xt_ready, NB + b - 1)
                k.normed(dve, 1, b, k.xn[:, b % 2, :]).then_inc(k.xn_ready, 1)
            k.arrived(dve, "f0_low")
            dve.wait_ge(S["low_copied"], NB)
            link(nc.vector.tensor_tensor(scores[:, :, :], low[:, :, MAXR:MAXR + NR],
                                         gate_b[:, :].unsqueeze(1).to_broadcast([P, NB, NR]), ALU.add))
            link(nc.vector.tensor_copy(before[:, :, 1:2], scores[:, :, 0:1]))
            link(nc.vector.tensor_copy(after[:, :, NR - 1:NR], scores[:, :, NR - 1:NR]))
            for t in range(2, NR):
                link(nc.vector.tensor_tensor(before[:, :, t:t + 1], before[:, :, t - 1:t], scores[:, :, t - 1:t],
                                             ALU.max))
            for t in range(NR - 2, 0, -1):
                link(nc.vector.tensor_tensor(after[:, :, t:t + 1], after[:, :, t + 1:t + 2], scores[:, :, t:t + 1],
                                             ALU.max))
            link(nc.vector.tensor_tensor(keep[:, :, 1:NR], before[:, :, 1:NR], after[:, :, 1:NR], ALU.is_lt))
            nc.vector.tensor_copy(gated[:, :, 0:RANKS[0]], low[:, :, 0:RANKS[0]]).then_inc(S["gated"], 1)
            for t in range(1, NR):
                lo, hi = RANKS[t - 1], RANKS[t]
                nc.vector.tensor_tensor(gated[:, :, lo:hi], low[:, :, lo:hi],
                                        keep[:, :, t:t + 1].to_broadcast([P, NB, hi - lo]), ALU.mult)\
                  .then_inc(S["gated"], 1)
            k.arrived(dve, "a1_tables")
            link(nc.vector.tensor_copy(pos[:, :], pos_i[:, :]))
            link(nc.vector.tensor_scalar(wrap[:, :], pos[:, :], 0.0, float(MC * P), ALU.is_lt, ALU.mult))
            link(nc.vector.tensor_tensor(pos[:, :], pos[:, :], wrap[:, :], ALU.add))
            link(nc.vector.tensor_scalar(pos[:, :], pos[:, :], 0.0, float(MC * P - 1), ALU.max, ALU.min))
            k.arrived(dve, "a1_tables")
            for c in range(MC):
                nc.vector.tensor_scalar(onehot[:, c, :], pos[:, :], iota[:, c:c + 1], None, ALU.is_equal)\
                  .then_inc(S["onehot_ready"], 1)
            for b in range(NB):
                dve.wait_ge(S["out_ready"], b + 1)
                dve.wait_ge(S["biased"], b + 1)
                nc.vector.tensor_tensor(k.x[:, b, :], k.x[:, b, :], ps[:, 2 + b % 4, :], ALU.add)\
                  .then_inc(S["added"], 1)
                dve.wait_ge(S["added"], b + 1)
                k.row_stats(dve, link, b)
            k.dve_count = link.n


def grouped_attention_inputs(k, ctx):
    G, HD = 8, P
    return {
        "cos": k.sb(ctx, "a1_cos", [P, TOK]), "sin": k.sb(ctx, "a1_sin", [P, TOK]),
        "mask": k.sb(ctx, "a1_mask", [P, NB, P], I32),
        "wk": k.sb(ctx, "a1_wk", [P, C, HD]), "wv": k.sb(ctx, "a1_wv", [P, G, C, HD]),
        "piece": k.sb(ctx, "a1_piece", [P, 2, D]),
        "wk_loaded": k.sem("a1_wk_loaded"), "piece_loaded": [k.sem(f"a1_piece{n}_loaded") for n in range(2)]}


def load_grouped_attention(k, sp, dram, a):
    for h in range(2):
        sp.dma_start(a["piece"][:, h, :], dram["a1_wq"][0, h].rearrange("p c n -> p (c n)"))\
          .then_inc(a["piece_loaded"][h], 16)
    sp.dma_start(a["wk"][:, :, :], dram["a1_wk"][0]).then_inc(a["wk_loaded"], 16)
    k.load(sp, "a1_wv", a["wv"][:, :, :, :], dram["a1_wv"])
    k.load(sp, "a1_mask", a["mask"][:, :, :], dram["mask"])


def grouped_attention(k, dram, a):
    nc, ps = k.nc, k.ps
    G, R, HD = 8, 4, P
    HALF = TOK // 2
    scale = 1.0 / float(np.sqrt(HD))
    cos, sin, mask, wk, wv, piece = (a[n] for n in ("cos", "sin", "mask", "wk", "wv", "piece"))
    wk_loaded, piece_loaded = a["wk_loaded"], a["piece_loaded"]
    QK_BANK, V_BANK, S_BANK, PT_BANK, OT_BANK, Y_BANK = 0, 2, 3, 4, 5, 6
    with ExitStack() as ctx:
        hidden = k.sb(ctx, "a1_hidden", [P, NB, P], I32)
        fill = k.sb(ctx, "a1_fill", [P, P])
        gate = k.sb(ctx, "a1_gate", [P, 1])
        wq = k.sb(ctx, "a1_wq", [P, 2, R, C, HD], F32R)
        one = k.sb(ctx, "a1_one", [P, 1])
        xT = k.sb(ctx, "a1_xT", [P, 2, C, TOK], F32R)
        qT = k.sb(ctx, "a1_qT", [P, R, TOK])
        kT = k.sb(ctx, "a1_kT", [P, TOK])
        v = k.sb(ctx, "a1_v", [P, NB, HD])
        turned = k.sb(ctx, "a1_turned", [P, 2, 2, HALF])
        negmax = k.sb(ctx, "a1_negmax", [P, 2, R])
        bias = k.sb(ctx, "a1_bias", [P, 2, R])
        total = k.sb(ctx, "a1_total", [P, 2, R])
        inv = k.sb(ctx, "a1_inv", [P, 2, R])
        prob = k.sb(ctx, "a1_prob", [P, 2, R, P])
        probT = k.sb(ctx, "a1_probT", [P, 2, R * P])
        oT = k.sb(ctx, "a1_oT", [P, 2, 2, R * P], F32R)
        wo = k.sb(ctx, "a1_wo", [P, 2, 2, R, D], F32R)
        S = {n: k.sem("a1_" + n) for n in (
            "qk_ready",
            "turned", "rotated", "v_ready", "v_copied", "s_ready", "bias_ready", "exp_ready", "prob_ready",
            "pt_ready", "pt_copied", "ot_ready", "ot_copied", "y_ready", "y_added",
            "split", "low_ready")}
        block = ctx.enter_context(nc.Block())

        def rotation(half, h):
            return 5 * half + 1 + h

        def before(g, b):
            if b > 0:
                return g, b - 1
            return None if isinstance(g, int) and g == 0 else (g - 1, NB - 1)

        @block.sync
        def _(sp):
            def load_wk(g):
                sp.dma_start(wk[:, :, :], dram["a1_wk"][g]).then_inc(wk_loaded, 16)

            def load_piece(n, h, src):
                after_first(sp, S["split"], 2 * (n - 1))
                sp.dma_start(piece[:, h % 2, :], src).then_inc(piece_loaded[h % 2], 16)

            def load_wq(g, h):
                load_piece(2 * R * g + h, h, dram["a1_wq"][g, h].rearrange("p c n -> p (c n)"))

            def load_wo(g, h):
                load_piece(2 * R * g + R + h, h, dram["a1_wo"][g][:, h, :])

            for h in range(2, R):
                load_wq(0, h)

            def loads_in(g):
                for h in range(R):
                    load_wo(g, h)
                for h in range(2):
                    load_wq(g + 1, h)
                sp.wait_ge(S["qk_ready"], 10 * g + rotation(1, -1) + 1)
                load_wk(g + 1)
                for h in range(2, R):
                    load_wq(g + 1, h)

            loads_in(0)
            with sp.Fori(1, G - 1) as g:
                loads_in(g)
            for h in range(R):
                load_wo(G - 1, h)

        @block.gpsimd
        def _(pool):
            link = Link(pool, k.pool_own, k.pool_count)

            def rotate(g, half, h):
                r = 10 * g + rotation(half, h)
                slot = rotation(half, h) % 2
                pool.wait_ge(S["turned"], r + 1)
                after_first(pool, S["s_ready"], 8 * g - 8 + 4 * half + 4)
                dst = kT[:, half * HALF:(half + 1) * HALF] if h < 0 else qT[:, h, half * HALF:(half + 1) * HALF]
                nc.gpsimd.tensor_tensor(dst, turned[:, slot, 0, :], turned[:, slot, 1, :], ALU.add)\
                  .then_inc(S["rotated"], 1)

            def split(n, h, count, out):
                pool.wait_ge(piece_loaded[h % 2], 16 * count)
                nc.gpsimd.tensor_tensor(out[HI], piece[:, h % 2, :], one[:, :].to_broadcast([P, D]), ALU.mult).then_inc(S["split"], 1)
                pool.wait_ge(S["split"], 2 * n + 1)
                low_part(nc.gpsimd, out[LO], piece[:, h % 2, :], out[HI]).then_inc(S["split"], 1)

            def split_wq(g, h):
                split(2 * R * g + h, h, R * g + h // 2 + 1,
                      [wq[:, part, h, :, :].rearrange("p c n -> p (c n)") for part in (HI, LO)])

            def split_wo(g, slot, h):
                split(2 * R * g + R + h, h, R * g + R // 2 + h // 2 + 1, parts(wo, slot, h))

            def group(g, last=False):
                rotate(g, 0, -1)
                for h in range(R):
                    rotate(g, 0, h)
                    if h == 0:
                        after_first(pool, S["y_ready"], 8 * (g - 1))
                    split_wo(g, g % 2, h)
                rotate(g, 1, -1)
                for h in range(R):
                    rotate(g, 1, h)
                    if not last:
                        split_wq(g + 1, h)

            link(nc.gpsimd.memset(one[:, :], 1.0))
            for h in range(R):
                split_wq(0, h)
            group(0)
            group(1)
            with pool.Fori(2, G - 1) as g:
                group(g)
            group(G - 1, last=True)
            for b in range(NB):
                k.row_rstd(pool, link, 3, b)
            k.pool_count = link.n

        @block.tensor
        def _(pe):
            def unit(g, half, h):
                project(g, half, [-1, 0] if h == 0 else [h])
                values(g, 4 * half + h)

            def project(g, half, heads):
                for j in heads:
                    r = 10 * g + rotation(half, j)
                    bank = QK_BANK + rotation(half, j) % 2
                    if half == 0 and j < 0:
                        pe.wait_ge(wk_loaded, 16 * (g + 1))
                    elif half == 0:
                        pe.wait_ge(S["split"], 2 * (2 * R * g + j + 1))
                    after_first(pe, S["turned"], r - 1)
                    for c in range(C):
                        tok = slice(half * HALF, (half + 1) * HALF)
                        if j < 0:
                            last = nc.tensor.matmul(ps[:, bank, :], wk[:, c, :], k.ctxT[:, c, tok],
                                                    start=c == 0, stop=c == C - 1)
                        else:
                            last = split_product(nc, ps[:, bank, :], parts(wq, j, c), parts(xT, c, tok),
                                                 c == 0, c == C - 1)
                    last.then_inc(S["qk_ready"], 1)

            def values(g, b):
                after_first(pe, S["v_copied"], 8 * g + b)
                for c in range(C):
                    last = nc.tensor.matmul(ps[:, V_BANK, 0:HD], k.ctxT[:, c, b * P:(b + 1) * P], wv[:, g, c, :],
                                            start=c == 0, stop=c == C - 1)
                last.then_inc(S["v_ready"], 1)

            def output(g, b, heads):
                t = 8 * g + b
                if heads[0] == 0:
                    output_waits(g, b)
                for h in heads:
                    last = split_product(nc, ps[:, Y_BANK + b % 2, :],
                                         [oT[:, b % 2, part, h * P:(h + 1) * P] for part in (HI, LO)],
                                         parts(wo, g % 2, h), h == 0, h == R - 1)
                if heads[-1] == R - 1:
                    last.then_inc(S["y_ready"], 1)

            def output_waits(g, b):
                t = 8 * g + b
                if b == 0:
                    pe.wait_ge(S["split"], 4 * R * (g + 1))
                pe.wait_ge(S["low_ready"], NB + t + 1)
                after_first(pe, S["y_added"], t - 1)

            def step(g, b, project):
                t = 8 * g + b
                if b % 4 == 0:
                    pe.wait_ge(S["rotated"], 10 * g + 5 * (b // 4 + 1))
                after_first(pe, S["exp_ready"], R * t)
                for h in range(R):
                    last = nc.tensor.matmul(ps[:, S_BANK, h * P:(h + 1) * P], qT[:, h, b * P:(b + 1) * P],
                                            kT[:, b * P:(b + 1) * P], start=True, stop=True)
                last.then_inc(S["s_ready"], 1)
                if b < 4:
                    unit(g, 1, b)
                elif project:
                    unit(g + 1, 0, b - 4)
                if before(g, b):
                    output(*before(g, b), (0, 1))
                pe.wait_ge(S["prob_ready"], t + 1)
                after_first(pe, S["pt_copied"], t)
                k.transpose4(PT_BANK, prob[:, b % 2, :, :].rearrange("p h k -> p (h k)")).then_inc(S["pt_ready"], 1)
                if before(g, b):
                    output(*before(g, b), (2, 3))
                pe.wait_ge(S["pt_copied"], t + 1)
                pe.wait_ge(S["v_copied"], t + 1)
                if before(g, b):
                    pe.wait_ge(S["low_ready"], NB + t)
                nc.tensor.matmul(ps[:, OT_BANK, :], v[:, b, :], probT[:, b % 2, :], start=True, stop=True)\
                  .then_inc(S["ot_ready"], 1)

            k.arrived(pe, "a1_wv")
            project(0, 0, [-1])
            for b in range(NB):
                pe.wait_ge(k.xn_ready, NB * 2 + b + 1)
                after_first(pe, S["low_ready"], b - 1)
                k.transpose4(4 + b % 2, k.xn[:, b % 2, :]).then_inc(k.xt_ready, 1)
                if b == 4:
                    pe.wait_ge(S["low_ready"], 4)
                if b >= 4:
                    project(0, 0, [b - 4])
                    values(0, b - 4)
            pe.wait_ge(S["low_ready"], NB)

            def group(g, last=False):
                for b in range(NB):
                    step(g, b, not last)

            group(0)
            with pe.Fori(1, G - 1) as g:
                group(g)
            group(G - 1, last=True)
            output(G - 1, NB - 1, range(R))

        @block.scalar
        def _(act):
            def copy_v(g, b):
                act.wait_ge(S["v_ready"], 8 * g + b + 1)
                after_first(act, S["ot_ready"], 8 * g - 8 + b + 1)
                nc.scalar.copy(v[:, b, :], ps[:, V_BANK, 0:HD]).then_inc(S["v_copied"], 1)

            def step(g, b, project):
                t = 8 * g + b
                slot = b % 2
                act.wait_ge(S["bias_ready"], t + 1)
                after_first(act, S["pt_ready"], t - 1)
                for h in range(R):
                    nc.scalar.activation(prob[:, slot, h, :], ps[:, S_BANK, h * P:(h + 1) * P], ACT.Exp,
                                         bias=bias[:, slot, h:h + 1], scale=scale,
                                         accum_out=total[:, slot, h:h + 1]).then_inc(S["exp_ready"], 1)
                if b < 4:
                    copy_v(g, b + 4)
                elif project:
                    copy_v(g + 1, b - 4)
                act.wait_ge(S["pt_ready"], t + 1)
                after_first(act, S["ot_ready"], t - 1)
                nc.scalar.copy(probT[:, slot, :], ps[:, PT_BANK, :]).then_inc(S["pt_copied"], 1)
                act.wait_ge(S["ot_ready"], t + 1)
                after_first(act, S["y_ready"], t - 1)
                nc.scalar.copy(oT[:, slot, HI, :], ps[:, OT_BANK, :]).then_inc(S["ot_copied"], 1)

            for b in range(NB):
                act.wait_ge(k.xt_ready, NB * 2 + b + 1)
                nc.scalar.copy(xT[:, HI, :, b * P:(b + 1) * P],
                               ps[:, 4 + b % 2, :].rearrange("p (c t) -> p c t", c=C)).then_inc(k.xt_copied, 1)
                if b >= 4:
                    copy_v(0, b - 4)

            def group(g, last=False):
                for b in range(NB):
                    step(g, b, not last)

            group(0)
            with act.Fori(1, G - 1) as g:
                group(g)
            group(G - 1, last=True)

        @block.vector
        def _(dve):
            link = Link(dve, k.dve_own, k.dve_count)
            hot = HD // 2

            def x_low(b):
                tok = slice(b * P, (b + 1) * P)
                dve.wait_ge(k.xt_copied, NB * 2 + b + 1)
                low_part(nc.vector, xT[:, LO, :, tok], ps[:, 4 + b % 2, :].rearrange("p (c t) -> p c t", c=C),
                         xT[:, HI, :, tok]).then_inc(S["low_ready"], 1)

            def o_low(g, b):
                t = 8 * g + b
                dve.wait_ge(S["ot_copied"], t + 1)
                low_part(nc.vector, oT[:, b % 2, LO, :], ps[:, OT_BANK, :], oT[:, b % 2, HI, :])\
                  .then_inc(S["low_ready"], 1)

            own0 = link.n + 2
            OWN = 3

            def turn(g, half, h):
                r = 10 * g + rotation(half, h)
                slot = rotation(half, h) % 2
                bank = ps[:, QK_BANK + slot, :]
                tok = slice(half * HALF, (half + 1) * HALF)
                dve.wait_ge(S["qk_ready"], r + 1)
                after_first(dve, S["rotated"], r - 1)
                nc.vector.tensor_tensor(turned[:, slot, 0, :], bank, cos[:, tok], ALU.mult)
                nc.vector.tensor_tensor(turned[0:hot, slot, 1, :], bank[hot:P, :], sin[hot:P, tok], ALU.mult)
                nc.vector.tensor_tensor(turned[hot:P, slot, 1, :], bank[0:hot, :], sin[0:hot, tok], ALU.mult)\
                  .then_inc(S["turned"], 1)

            def add(g, b, last):
                t = 8 * g + b
                dve.wait_ge(S["y_ready"], t + 1)
                after_first(dve, S["y_added"], t - 7)
                nc.vector.tensor_tensor(k.x[:, b, :], k.x[:, b, :], ps[:, Y_BANK + b % 2, :], ALU.add)\
                  .then_inc(S["y_added"], 1)
                if last:
                    dve.wait_ge(S["y_added"], t + 1)
                    k.row_stats(dve, last, b)

            def step(g, b, project, last):
                t = 8 * g + b
                own = own0 + OWN * t
                slot = b % 2
                scores = ps[:, S_BANK, :].rearrange("p (h k) -> p h k", h=R)
                dve.wait_ge(S["s_ready"], t + 1)
                nc.vector.memset(gate[:, :], 0.0)
                nc.vector.copy_predicated(scores, hidden[:, b, :].unsqueeze(1).to_broadcast([P, R, P]),
                                          fill[:, :].unsqueeze(1).to_broadcast([P, R, P])).then_inc(k.dve_own, 1)
                dve.wait_ge(k.dve_own, own + 1)
                nc.vector.tensor_reduce(negmax[:, slot, :], scores, AX.X, ALU.max, negate=True)\
                  .then_inc(k.dve_own, 1)
                dve.wait_ge(k.dve_own, own + 2)
                after_first(dve, S["exp_ready"], R * (t - 1))
                nc.vector.tensor_scalar(bias[:, slot, :], negmax[:, slot, :], scale, None, ALU.mult)\
                  .then_inc(S["bias_ready"], 1)
                next_g, half, h = (g, 1, b) if b < 4 else (g + 1, 0, b - 4)
                if h == 0 and (project or b < 4):
                    turn(next_g, half, -1)
                if before(g, b):
                    o_low(*before(g, b))
                dve.wait_ge(S["exp_ready"], R * (t + 1))
                nc.vector.reciprocal(inv[:, slot, :], total[:, slot, :]).then_inc(k.dve_own, 1)
                dve.wait_ge(k.dve_own, own + 3)
                nc.vector.tensor_tensor(prob[:, slot, :, :], prob[:, slot, :, :],
                                        inv[:, slot, :].unsqueeze(2).to_broadcast([P, R, P]), ALU.mult)\
                  .then_inc(S["prob_ready"], 1)
                if project or b < 4:
                    turn(next_g, half, h)
                if before(g, b):
                    add(*before(g, b), last if b else None)

            for b in range(NB):
                after_first(dve, k.xt_ready, NB * 2 + b - 1)
                k.normed(dve, 2, b, k.xn[:, b % 2, :]).then_inc(k.xn_ready, 1)
                if b >= 1:
                    x_low(b - 1)
                if b >= 4:
                    turn(0, 0, b - 5)
            x_low(NB - 1)
            turn(0, 0, R - 1)
            k.arrived(dve, "a1_mask")
            link(nc.vector.memset(fill[:, :], -1e9 / scale))
            link(nc.vector.tensor_scalar(hidden[:, :, :], mask[:, :, :], 0.0, None, ALU.is_equal))

            def group(g, last=None):
                for b in range(NB):
                    step(g, b, last is None, last)

            group(0)
            with dve.Fori(1, G - 1) as g:
                group(g)
            stats = Link(dve, k.sem("a1_stats"))
            group(G - 1, last=stats)
            o_low(G - 1, NB - 1)
            add(G - 1, NB - 1, stats)
            k.dve_count = own0 + OWN * NB * G


def mixture_of_experts(k, dram, table, ahead):
    nc, ps = k.nc, k.ps
    NE = 3
    NG = 4
    SLOTS = 3
    HALF = TOK // 2
    VISION = int(P * 0.3)
    FUNCS = (ACT.Tanh, ACT.Gelu, ACT.Silu)
    GATE, NORMS, PICKED = slice(0, NB * NG), slice(64, 64 + 2 * NB), slice(128, 128 + NB * 2 * NE)
    PRE_BANK, OUT_BANK, OUT_BANKS, GATE_BANK, T_BANK = 0, 2, 3, 5, 6
    GT_BANK = OUT_BANK + 2
    with ExitStack() as ctx:
        whole = k.sb(ctx, "f1_whole", [P, SLOTS, C, D])
        w = k.sb(ctx, "f1_w", [P, 2, SLOTS, C, D], F32R)
        b1 = k.sb(ctx, "f1_b1", [P, NE, C])
        b2 = k.sb(ctx, "f1_b2", [P, NE, D])
        gw_whole = k.sb(ctx, "f1_gw_whole", [P, C, NG])
        gw = k.sb(ctx, "f1_gw", [P, 2, C, NG], F32R)
        gw_ratio = k.sb(ctx, "f1_gw_ratio", [P, NE])
        gb = k.sb(ctx, "f1_gb", [P, NE])
        gateT = k.sb(ctx, "f1_gateT", [NG, TOK])
        ones = k.sb(ctx, "f1_ones", [P, P])
        row0 = k.sb(ctx, "f1_row0", [P, P])
        share = k.sb(ctx, "f1_share", [P, 2])
        xT = k.sb(ctx, "f1_xT", [P, 2, C, TOK], F32R)
        act_whole = k.sb(ctx, "f1_act_whole", [P, C, HALF])
        act_T = k.sb(ctx, "f1_act", [P, 2, 2, C, HALF], F32R)
        norms = k.sb(ctx, "f1_norms", [P, NB])
        both = k.sb(ctx, "f1_both", [P, NB, 2])
        prob = k.sb(ctx, "f1_prob", [P, NB, NE])
        tmp = k.sb(ctx, "f1_tmp", [P, NB, NE])
        ratio = k.sb(ctx, "f1_ratio", [P, NB])
        one = k.sb(ctx, "f1_one", [P, 12, NB])
        first = k.sb(ctx, "f1_first", [P, NB, NE])
        lowest = k.sb(ctx, "f1_lowest", [P, NB, NE])
        picks = k.sb(ctx, "f1_picks", [P, NB, 2, NE])
        weight = k.sb(ctx, "f1_weight", [P, NB, NE])
        S = {n: k.sem("f1_" + n) for n in (
            "norm_ready", "gt_ready", "gt_copied", "gate_ready", "asked", "answered",
            "pre_ready", "act_ready", "act_high", "act_low", "out_ready", "added", "split", "xt_low", "gw_ready")}
        whole_loaded = [k.sem(f"f1_whole{n}_loaded") for n in range(SLOTS)]
        MEANS, EXP, PICKS = 1, 2, 3
        block = ctx.enter_context(nc.Block())

        @block.sync
        def _(sp):
            def load_matrix(i):
                after_first(sp, S["split"], 2 * (i - SLOTS + 1))
                sp.dma_start(whole[:, i % SLOTS, :, :], dram[f"f1_w{i % 2 + 1}"][i // 2])\
                  .then_inc(whole_loaded[i % SLOTS], 16)

            k.load(sp, "f1_gw", gw_whole[:, :, :], dram["f1_gw"])
            load_matrix(0)
            for name, dst in (("ones", ones[:, :]), ("share", share[:, :]), ("b1", b1[:, :, :]),
                              ("row0", row0[:, :])):
                k.load(sp, "f1_small", dst, dram["f1_" + name])
            k.load(sp, "f1_small", gw_ratio[:, :], dram["f1_gw_ratio"].partition_broadcast(P))
            k.load(sp, "f1_small", gb[:, :], dram["f1_gb"].partition_broadcast(P))
            k.load(sp, "f1_b2", b2[:, :, :], dram["f1_b2"].partition_broadcast(P))
            for i in range(1, 2 * NE):
                load_matrix(i)
            k.load(sp, "a2_table", table[:, :, :], dram["a2_table"])
            for b in range(AHEAD):
                k.load(sp, "a2_ahead", ahead[:, b, :], dram["ctx"][b])

        @block.gpsimd
        def _(pool):
            link = Link(pool, k.pool_own, k.pool_count)
            k.arrived(pool, "f1_gw")
            link(nc.gpsimd.tensor_copy(gw[:, HI, :, :], gw_whole[:, :, :]))
            low_part(nc.gpsimd, gw[:, LO, :, :], gw_whole[:, :, :], gw[:, HI, :, :]).then_inc(S["gw_ready"], 1)
            for i in range(1, 2 * NE):
                slot = i % SLOTS
                pool.wait_ge(S["split"], 2 * i + 1)
                low_part(nc.gpsimd, w[:, LO, slot, :, :], whole[:, slot, :, :], w[:, HI, slot, :, :])\
                  .then_inc(S["split"], 1)
            for b in range(NB):
                k.row_rstd(pool, link, 4, b)
            k.pool_count = link.n

        @block.tensor
        def _(pe):
            def gate(half):
                pe.wait_ge(S["gw_ready"], 1)
                after_first(pe, S["gt_copied"], half)
                for c in range(C):
                    last = split_product(nc, ps[0:NG, GT_BANK, :], parts(gw, c),
                                         parts(xT, c, slice(half * HALF, (half + 1) * HALF)), c == 0, c == C - 1)
                last.then_inc(S["gt_ready"], 1)

            def first_product(n, chunks=range(C)):
                e, half = n // 2, n % 2
                pe.wait_ge(S["split"], 2 * (2 * e + 1))
                for f in chunks:
                    u = C * n + f
                    after_first(pe, S["act_ready"], u - 1)
                    for c in range(C):
                        last = split_product(nc, ps[:, PRE_BANK + u % 2, :],
                                             parts(w, 2 * e % SLOTS, c, slice(f * P, (f + 1) * P)),
                                             parts(xT, c, slice(half * HALF, (half + 1) * HALF)),
                                             c == 0, c == C - 1)
                    last.then_inc(S["pre_ready"], 1)

            def second_product(n):
                e, half = n // 2, n % 2
                pe.wait_ge(S["split"], 2 * (2 * e + 2))
                pe.wait_ge(S["act_low"], C * (n + 1))
                for j in range(4):
                    o = 4 * n + j
                    after_first(pe, S["added"], o - OUT_BANKS + 1)
                    for f in range(C):
                        last = split_product(nc, ps[:, OUT_BANK + o % OUT_BANKS, :],
                                             parts(act_T, n % 2, f, slice(j * P, (j + 1) * P)),
                                             parts(w, (2 * e + 1) % SLOTS, f), f == 0, f == C - 1)
                    last.then_inc(S["out_ready"], 1)

            for b in range(NB):
                pe.wait_ge(k.xn_ready, NB * 3 + b + 1)
                after_first(pe, S["xt_low"], b - 1)
                k.transpose4(T_BANK + b % 2, k.xn[:, b % 2, :]).then_inc(k.xt_ready, 1)
                if b == 4:
                    pe.wait_ge(S["xt_low"], 4)
                if b >= 4:
                    first_product(0, [b - 4])
                if b == 4:
                    gate(0)
            pe.wait_ge(S["xt_low"], NB)
            gate(1)
            pe.wait_ge(S["gt_copied"], 2)
            for b in range(NB):
                last = nc.tensor.transpose(ps[:, GATE_BANK, GATE][:, NG * b:NG * (b + 1)],
                                           gateT[:, b * P:(b + 1) * P], k.ident[0:NG, 0:NG])
            last.then_inc(S["gate_ready"], 1)
            k.arrived(pe, "f1_small")
            pe.wait_ge(S["asked"], MEANS)
            nc.tensor.matmul(ps[:, GATE_BANK, NORMS], ones[:, :], both[:, :, :].rearrange("p b n -> p (b n)"),
                             start=True, stop=True).then_inc(S["answered"], 1)
            for n in range(1, 2 * NE + 1):
                if n < 2 * NE:
                    first_product(n)
                if n == 1:
                    k.arrived(pe, "f1_small")
                    pe.wait_ge(S["asked"], PICKS)
                    nc.tensor.matmul(ps[:, GATE_BANK, PICKED], row0[:, :],
                                     picks[:, :, :, :].rearrange("p b i e -> p (b i e)"), start=True, stop=True)\
                      .then_inc(S["answered"], 1)
                second_product(n - 1)

        @block.scalar
        def _(act):
            def high_part(i):
                slot = i % SLOTS
                act.wait_ge(whole_loaded[slot], 16 * (i // SLOTS + 1))
                if i >= SLOTS:
                    used = S["out_ready"] if (i - SLOTS) % 2 else S["pre_ready"]
                    act.wait_ge(used, 2 * C * ((i - SLOTS) // 2 + 1))
                after_first(act, S["split"], 2 * i)
                nc.scalar.copy(w[:, HI, slot, :, :], whole[:, slot, :, :]).then_inc(S["split"], 1)

            def activations(n, f):
                e, u = n // 2, C * n + f
                act.wait_ge(S["pre_ready"], u + 1)
                after_first(act, S["act_low"], u - C + 1)
                nc.scalar.activation(act_whole[:, f, :], ps[:, PRE_BANK + u % 2, :], FUNCS[e],
                                     bias=b1[:, e, f:f + 1]).then_inc(S["act_ready"], 1)
                if f == 0:
                    after_first(act, S["out_ready"], 4 * (n - 1))
                act.wait_ge(S["act_ready"], u + 1)
                nc.scalar.copy(act_T[:, HI, n % 2, f, :], act_whole[:, f, :]).then_inc(S["act_high"], 1)

            def copy_gate(half):
                act.wait_ge(S["gt_ready"], half + 1)
                nc.scalar.copy(gateT[:, half * HALF:(half + 1) * HALF], ps[0:NG, GT_BANK, :])\
                  .then_inc(S["gt_copied"], 1)

            for b in range(NB):
                if b in (1, 5, 7):
                    high_part(b // 2 - (b > 1))
                act.wait_ge(k.xt_ready, NB * 3 + b + 1)
                nc.scalar.copy(xT[:, HI, :, b * P:(b + 1) * P],
                               ps[:, T_BANK + b % 2, :].rearrange("p (c t) -> p c t", c=C)).then_inc(k.xt_copied, 1)
                act.wait_ge(k.xn_ready, NB * 3 + b + 1)
                after_first(act, S["norm_ready"], b - 1)
                nc.scalar.activation(ps[:, OUT_BANK + b % 2, :], k.xn[:, b % 2, :], ACT.Abs, accum_out=norms[:, b:b + 1])\
                  .then_inc(S["norm_ready"], 1)
                if b == 4:
                    k.arrived(act, "f1_small")
                if b >= 4:
                    activations(0, b - 4)
                if b == 4:
                    copy_gate(0)
            copy_gate(1)
            for n in range(1, 2 * NE):
                if n >= 2 and n - 2 + SLOTS < 2 * NE:
                    high_part(n - 2 + SLOTS)
                for f in range(C):
                    activations(n, f)
                    if n == 1 and f == 1:
                        act.wait_ge(S["asked"], EXP)
                        nc.scalar.activation(prob[:, :, :], prob[:, :, :], ACT.Exp).then_inc(S["answered"], 1)

        @block.vector
        def _(dve):
            link = Link(dve, k.dve_own, k.dve_count)
            tt, ts = nc.vector.tensor_tensor, nc.vector.tensor_scalar

            def x_low(b):
                tok = slice(b * P, (b + 1) * P)
                dve.wait_ge(k.xt_copied, NB * 3 + b + 1)
                low_part(nc.vector, xT[:, LO, :, tok], ps[:, T_BANK + b % 2, :].rearrange("p (c t) -> p c t", c=C),
                         xT[:, HI, :, tok]).then_inc(S["xt_low"], 1)

            def act_lows(n, chunks=range(C)):
                for f in chunks:
                    dve.wait_ge(S["act_high"], C * n + f + 1)
                    low_part(nc.vector, act_T[:, LO, n % 2, f, :], act_whole[:, f, :], act_T[:, HI, n % 2, f, :])\
                      .then_inc(S["act_low"], 1)

            for b in range(NB):
                after_first(dve, k.xt_ready, NB * 3 + b - 1)
                after_first(dve, S["norm_ready"], b - 1)
                k.normed(dve, 3, b, k.xn[:, b % 2, :]).then_inc(k.xn_ready, 1)
                if b >= 1:
                    x_low(b - 1)
                if b == 2:
                    dve.wait_ge(S["split"], 1)
                    low_part(nc.vector, w[:, LO, 0, :, :], whole[:, 0, :, :], w[:, HI, 0, :, :])\
                      .then_inc(S["split"], 1)
                if b >= 5:
                    act_lows(0, [b - 5])
            x_low(NB - 1)
            act_lows(0, [C - 1])
            k.arrived(dve, "f1_small")
            dve.wait_ge(S["norm_ready"], NB)
            link(ts(both[:, :, 0], norms[:, :], share[:, 0:1], None, ALU.mult))
            ts(both[:, :, 1], norms[:, :], share[:, 1:2], None, ALU.mult).then_inc(S["asked"], 1)
            dve.wait_ge(S["gate_ready"], 1)
            dve.wait_ge(S["answered"], MEANS)
            means = ps[:, GATE_BANK, NORMS].rearrange("p (b n) -> p b n", n=2)
            link(ts(ratio[:, :], means[:, :, 1], 1e-8, None, ALU.add))
            link(nc.vector.reciprocal(one[:, 0, :], ratio[:, :]))
            link(tt(ratio[:, :], means[:, :, 0], one[:, 0, :], ALU.mult))
            each = [P, NB, NE]
            link(tt(tmp[:, :, :], ratio[:, :].unsqueeze(2).to_broadcast(each),
                    gw_ratio[:, :].unsqueeze(1).to_broadcast(each), ALU.mult))
            link(tt(tmp[:, :, :], ps[:, GATE_BANK, GATE].rearrange("p (b e) -> p b e", e=NG)[:, :, 0:NE], tmp[:, :, :], ALU.add))
            link(tt(tmp[:, :, :], tmp[:, :, :], gb[:, :].unsqueeze(1).to_broadcast(each), ALU.add))
            link(nc.vector.tensor_reduce(one[:, 1, :], tmp[:, :, :], AX.X, ALU.max))
            tt(prob[:, :, :], tmp[:, :, :], one[:, 1, :].unsqueeze(2).to_broadcast(each), ALU.subtract)\
              .then_inc(S["asked"], 1)
            dve.wait_ge(S["answered"], EXP)
            link(nc.vector.tensor_reduce(one[:, 2, :], prob[:, :, :], AX.X, ALU.add))
            link(nc.vector.reciprocal(one[:, 3, :], one[:, 2, :]))
            link(tt(prob[:, :, :], prob[:, :, :], one[:, 3, :].unsqueeze(2).to_broadcast(each), ALU.mult))
            p0, p1, p2 = (prob[:, :, e] for e in range(NE))
            top, second, least, larger, lesser, other, either = (one[:, n, :] for n in range(4, 11))
            link(tt(larger, p0, p1, ALU.max))
            link(tt(lesser, p0, p1, ALU.min))
            link(tt(top, larger, p2, ALU.max))
            link(tt(least, lesser, p2, ALU.min))
            link(tt(other, larger, p2, ALU.min))
            link(tt(second, lesser, other, ALU.max))
            link(tt(first[:, :, :], prob[:, :, :], top.unsqueeze(2).to_broadcast(each), ALU.is_ge))
            link(tt(lowest[:, :, :], prob[:, :, :], least.unsqueeze(2).to_broadcast(each), ALU.is_le))
            link(tt(either, first[:, :, 0], first[:, :, 1], ALU.max))
            link(tt(first[:, :, 2], first[:, :, 2], either, ALU.is_gt))
            link(tt(first[:, :, 1], first[:, :, 1], first[:, :, 0], ALU.is_gt))
            link(tt(either, lowest[:, :, 2], lowest[:, :, 1], ALU.max))
            link(tt(lowest[:, :, 0], lowest[:, :, 0], either, ALU.is_gt))
            link(tt(lowest[:, :, 1], lowest[:, :, 1], lowest[:, :, 2], ALU.is_gt))
            link(nc.vector.tensor_copy(picks[:, :, 0, :], first[:, :, :]))
            link(tt(tmp[:, :, :], first[:, :, :], lowest[:, :, :], ALU.add))
            ts(picks[:, :, 1, :], tmp[:, :, :], -1.0, 1.0, ALU.mult, ALU.add).then_inc(S["asked"], 1)
            link(tt(one[:, 0, :], top, second, ALU.add))
            link(ts(one[:, 1, :], one[:, 0, :], 1e-8, None, ALU.add))
            link(nc.vector.reciprocal(one[:, 2, :], one[:, 1, :]))
            link(tt(top, top, one[:, 2, :], ALU.mult))
            link(tt(second, second, one[:, 2, :], ALU.mult))
            dve.wait_ge(S["asked"], PICKS)
            dve.wait_ge(S["answered"], PICKS)
            picked = ps[:, GATE_BANK, PICKED].rearrange("p (b i e) -> p b i e", b=NB, i=2)
            link(tt(weight[:, :, :], picked[:, :, 0, :], top.unsqueeze(2).to_broadcast(each), ALU.mult))
            link(tt(tmp[:, :, :], picked[:, :, 1, :], second.unsqueeze(2).to_broadcast(each), ALU.mult))
            link(tt(weight[:, :, :], weight[:, :, :], tmp[:, :, :], ALU.add))

            def add(n):
                e, half = n // 2, n % 2
                k.arrived(dve, "f1_b2")
                for j in range(4):
                    b = 4 * half + j
                    link(nc.vector.scalar_tensor_tensor(k.x[:, b, :], b2[:, e, :], weight[:, b, e:e + 1],
                                                        k.x[:, b, :], ALU.mult, ALU.add))
                    dve.wait_ge(S["out_ready"], 4 * n + j + 1)
                    nc.vector.scalar_tensor_tensor(k.x[:, b, :], ps[:, OUT_BANK + (4 * n + j) % OUT_BANKS, :],
                                                   weight[:, b, e:e + 1], k.x[:, b, :], ALU.mult, ALU.add)\
                      .then_inc(S["added"], 1)
                    dve.wait_ge(S["added"], 4 * n + j + 1)
                    if e == NE - 1:
                        k.row_stats(dve, link, b)

            for n in range(2 * NE):
                if n + 1 < 2 * NE:
                    act_lows(n + 1)
                add(n)
            k.dve_count = link.n


AHEAD = 2


def autocorrelation(k, dram, table, ahead, f2, a3, f3):
    nc, ps = k.nc, k.ps
    CTX_BANK, Q_BANK, C_BANK, WT_BANK, W_BANK, OUT_BANK = 0, 2, 3, 4, 5, 7
    K1, K2, VC, VS = range(4)
    TOP = 9
    with ExitStack() as ctx:
        T_Q, T_K2, T_VC, T_VS, T_C1, T_C2, T_WC, T_WS, T_OC, T_OS, T_LAST = (
            table[:, n, :] for n in range(11))
        late = k.sb(ctx, "a2_late", [P, NB - AHEAD, D])
        value = [ahead[:, b, :] for b in range(AHEAD)] + [late[:, b, :] for b in range(NB - AHEAD)]
        freq = k.sb(ctx, "a2_freq", [P, 2, 4, D])
        prod = k.sb(ctx, "a2_prod", [P, 2, D])
        corr = k.sb(ctx, "a2_corr", [P, 2, C, P])
        less8 = k.sb(ctx, "a2_less8", [P, C, P])
        less9 = k.sb(ctx, "a2_less9", [P, C, P])
        top8 = k.sb(ctx, "a2_top8", [P, C, 8])
        ninth = k.sb(ctx, "a2_ninth", [P, C, 8])
        negmax = k.sb(ctx, "a2_negmax", [P, 2, C])
        expo = k.sb(ctx, "a2_exp", [P, C, P])
        picked = k.sb(ctx, "a2_picked", [P, 2, C, P])
        total = k.sb(ctx, "a2_total", [P, C])
        inv = k.sb(ctx, "a2_inv", [P, 2, C])
        weight = k.sb(ctx, "a2_weight", [P, C, P])
        weightT = k.sb(ctx, "a2_weightT", [P, D])
        shift = k.sb(ctx, "a2_shift", [P, 4, D])
        sums = k.sb(ctx, "a2_sums", [P, 2, D])
        S = {n: k.sem("a2_" + n) for n in (
            "freq_ready", "freq_copied", "q_ready", "prod_ready", "corr_ready", "corr_copied",
            "max_ready", "exp_ready", "inv_ready", "weight_ready", "wt_ready", "wt_copied", "w_ready", "shift_ready", "sums_ready",
            "out_ready", "added")}
        block = ctx.enter_context(nc.Block())

        def done(b, kind):
            if kind:
                return 2 * min(2 * b + 3, 2 * NB)
            return 2 * max(2 * b, 1)

        @block.sync
        def _(sp):
            for b in range(AHEAD, NB):
                k.load(sp, "a2_ctx", value[b], dram["ctx"][b])
            load_scaled_linear(k, sp, dram, f2)
            load_token_attention(k, sp, dram, a3)
            load_packed_linear(k, sp, dram, f3)

        @block.gpsimd
        def _(pool):
            link = Link(pool, k.pool_own, k.pool_count)
            for b in range(NB):
                after_first(pool, S["out_ready"], b)
                for n, (one, other, op) in enumerate(((0, 1, ALU.add), (3, 2, ALU.subtract))):
                    pool.wait_ge(S["shift_ready"], 2 * b + n + 1)
                    nc.gpsimd.tensor_tensor(sums[:, n, :], shift[:, one, :], shift[:, other, :], op)\
                      .then_inc(S["sums_ready"], 1)
                if b >= 2:
                    k.row_rstd(pool, link, 5, b - 2)
                if b == 3:
                    k.arrived(pool, "f2_w")
                if 3 <= b < 3 + C:
                    scale_weights(nc.gpsimd, f2, b - 3)
            for b in range(NB - 2, NB):
                k.row_rstd(pool, link, 5, b)
            k.pool_count = link.n

        @block.tensor
        def _(pe):
            mm = nc.tensor.matmul

            def context(b, kind):
                k.arrived(pe, "a2_ahead" if b < AHEAD else "a2_ctx")
                for n, t in enumerate((T_VC, T_VS) if kind else (T_Q, T_K2)):
                    after_first(pe, S["freq_copied"], done(b, kind) - 3 + n)
                    mm(ps[:, CTX_BANK + n, :], t, value[b], start=True, stop=True)\
                        .then_inc(S["freq_ready"], 1)

            def query(b):
                pe.wait_ge(k.xn_ready, NB * 4 + b + 1)
                after_first(pe, S["prod_ready"], b)
                mm(ps[:, Q_BANK, :], T_Q, k.xn[:, b % 2, :], start=True, stop=True).then_inc(S["q_ready"], 1)

            def correlate(b):
                pe.wait_ge(S["prod_ready"], b + 1)
                after_first(pe, S["corr_copied"], b)
                for c in range(C):
                    o = ps[:, C_BANK, c * P:(c + 1) * P]
                    mm(o, prod[:, 0, c * P:(c + 1) * P], T_C1, start=True, stop=False)
                    last = mm(o, prod[:, 1, c * P:(c + 1) * P], T_C2, start=False, stop=True)
                last.then_inc(S["corr_ready"], 1)

            def weights(b):
                pe.wait_ge(S["weight_ready"], b + 1)
                pe.wait_ge(a3["made_copied"], b + 1)
                k.transpose4(WT_BANK, weight[:, :, :].rearrange("p c t -> p (c t)")).then_inc(S["wt_ready"], 1)

            def weights_transform(b):
                pe.wait_ge(S["wt_copied"], b + 1)
                after_first(pe, S["shift_ready"], 2 * b)
                mm(ps[:, W_BANK, :], T_WC, weightT[:, :], start=True, stop=True)
                mm(ps[:, W_BANK + 1, :], T_WS, weightT[:, :], start=True, stop=True).then_inc(S["w_ready"], 1)

            def output(b):
                after_first(pe, S["added"], b)
                mm(ps[:, OUT_BANK, :], T_LAST, value[b], start=True, stop=False)
                for n, t in enumerate((T_OC, T_OS)):
                    pe.wait_ge(S["sums_ready"], 2 * b + n + 1)
                    last = mm(ps[:, OUT_BANK, :], t, sums[:, n, :], start=False, stop=n == 1)
                last.then_inc(S["out_ready"], 1)

            k.arrived(pe, "a2_table")
            context(0, 0)
            query(0)
            for i in range(NB + 1):
                if i >= 1:
                    weights(i - 1)
                if i < NB:
                    correlate(i)
                if i >= 1:
                    weights_transform(i - 1)
                if i + 1 < NB:
                    context(i + 1, 0)
                    query(i + 1)
                if i < NB:
                    context(i, 1)
                project_context(k, pe, a3, i, WT_BANK)
                if i >= 1:
                    output(i - 1)

        @block.scalar
        def _(act):
            def context(b, kind):
                for n in range(2):
                    act.wait_ge(S["freq_ready"], done(b, kind) - 1 + n)
                    after_first(act, *((S["shift_ready"], 2 * (b - 1)) if kind else (S["prod_ready"], b - 1)))
                    nc.scalar.copy(freq[:, b % 2, 2 * kind + n, :], ps[:, CTX_BANK + n, :])\
                      .then_inc(S["freq_copied"], 1)

            def weigh(b):
                act.wait_ge(S["inv_ready"], b + 1)
                after_first(act, S["wt_ready"], b)
                for c in range(C):
                    last = nc.scalar.activation(weight[:, c, :], picked[:, b % 2, c, :], ACT.Copy,
                                                scale=inv[:, b % 2, c:c + 1])
                last.then_inc(S["weight_ready"], 1)

            context(0, 0)
            for i in range(NB + 1):
                if i >= 1:
                    weigh(i - 1)
                    act.wait_ge(S["wt_ready"], i)
                    after_first(act, S["w_ready"], i - 1)
                    nc.scalar.copy(weightT[:, :], ps[:, WT_BANK, :]).then_inc(S["wt_copied"], 1)
                if i < NB:
                    act.wait_ge(S["corr_ready"], i + 1)
                    after_first(act, S["inv_ready"], i - 1)
                    nc.scalar.copy(corr[:, i % 2, :, :].rearrange("p c t -> p (c t)"), ps[:, C_BANK, :])\
                      .then_inc(S["corr_copied"], 1)
                    act.wait_ge(S["max_ready"], i + 1)
                    act.wait_ge(S["corr_copied"], i + 1)
                    after_first(act, S["inv_ready"], i)
                    for c in range(C):
                        nc.scalar.activation(expo[:, c, :], corr[:, i % 2, c, :], ACT.Exp,
                                             bias=negmax[:, i % 2, c:c + 1]).then_inc(S["exp_ready"], 1)
                if i + 1 < NB:
                    context(i + 1, 0)
                if i < NB:
                    context(i, 1)
                copy_projected(k, act, a3, i, WT_BANK)

        @block.vector
        def _(dve):
            link = Link(dve, k.dve_own, k.dve_count)
            tt = nc.vector.tensor_tensor

            def normalise(b):
                after_first(dve, S["q_ready"], b - 1)
                k.normed(dve, 4, b, k.xn[:, b % 2, :]).then_inc(k.xn_ready, 1)

            def multiply(b):
                dve.wait_ge(S["q_ready"], b + 1)
                dve.wait_ge(S["freq_copied"], done(b, 0))
                after_first(dve, S["corr_ready"], b)
                tt(prod[:, 0, :], ps[:, Q_BANK, :], freq[:, b % 2, K1, :], ALU.mult)
                tt(prod[:, 1, :], ps[:, Q_BANK, :], freq[:, b % 2, K2, :], ALU.mult).then_inc(S["prod_ready"], 1)

            def multiply_shift(b):
                dve.wait_ge(S["w_ready"], b + 1)
                dve.wait_ge(S["freq_copied"], done(b, 1))
                after_first(dve, S["sums_ready"], 2 * b)
                wc, ws = ps[:, W_BANK, :], ps[:, W_BANK + 1, :]
                vc, vs = freq[:, b % 2, VC, :], freq[:, b % 2, VS, :]
                tt(shift[:, 0, :], wc, vc, ALU.mult)
                tt(shift[:, 1, :], ws, vs, ALU.mult).then_inc(S["shift_ready"], 1)
                tt(shift[:, 2, :], ws, vc, ALU.mult)
                tt(shift[:, 3, :], wc, vs, ALU.mult).then_inc(S["shift_ready"], 1)

            def pick(b):
                dve.wait_ge(S["corr_copied"], b + 1)
                for c in range(C):
                    nc.vector.max(top8[:, c, :], corr[:, b % 2, c, :]).then_inc(k.dve_own, 1)
                link.n += C
                dve.wait_ge(k.dve_own, link.n)
                after_first(dve, S["exp_ready"], C * (b - 1))
                nc.vector.tensor_scalar(negmax[:, b % 2, :], top8[:, :, 0], -1.0, None, ALU.mult)\
                  .then_inc(S["max_ready"], 1)
                for c in range(C):
                    nc.vector.match_replace(less8[:, c, :], top8[:, c, :], corr[:, b % 2, c, :], LOWEST)\
                      .then_inc(k.dve_own, 1)
                link.n += C
                dve.wait_ge(k.dve_own, link.n)
                link(nc.vector.tensor_reduce(ninth[:, :, 0], less8[:, :, :], AX.X, ALU.max))
                for c in range(C):
                    nc.vector.match_replace(less9[:, c, :], ninth[:, c, :], less8[:, c, :], LOWEST)\
                      .then_inc(k.dve_own, 1)
                link.n += C
                dve.wait_ge(k.dve_own, link.n)

            def weigh(b):
                dve.wait_ge(S["exp_ready"], C * (b + 1))
                after_first(dve, S["weight_ready"], b - 1)
                link(nc.vector.scalar_tensor_tensor(picked[:, b % 2, :, :], less9[:, :, :], LOWEST, expo[:, :, :],
                                                    ALU.is_equal, ALU.mult))
                link(nc.vector.tensor_reduce(total[:, :], picked[:, b % 2, :, :], AX.X, ALU.add))
                nc.vector.reciprocal(inv[:, b % 2, :], total[:, :]).then_inc(S["inv_ready"], 1)

            def add(b):
                dve.wait_ge(S["out_ready"], b + 1)
                tt(k.x[:, b, :], k.x[:, b, :], ps[:, OUT_BANK, :], ALU.add).then_inc(S["added"], 1)
                dve.wait_ge(S["added"], b + 1)
                k.row_stats(dve, link, b)

            link(nc.vector.memset(ninth[:, :, :], LOWEST))
            normalise(0)
            normalise(1)
            for i in range(NB + 2):
                if i < NB:
                    multiply(i)
                    if i + 2 < NB:
                        normalise(i + 2)
                if i >= 2:
                    add(i - 2)
                if i < NB:
                    pick(i)
                if 1 <= i <= NB:
                    multiply_shift(i - 1)
                if i < NB:
                    weigh(i)
            k.dve_count = link.n


def scaled_linear_inputs(k, ctx):
    return {"w": k.sb(ctx, "f2_w", [P, C, D]), "scale": k.sb(ctx, "f2_scale", [P, C, C]),
            "bias": k.sb(ctx, "f2_bias", [P, D]), "w_ready": k.sem("f2_w_ready")}


def load_scaled_linear(k, sp, dram, a):
    k.load(sp, "f2_w", a["scale"][:, :, :].rearrange("p i o -> p (i o)"), dram["f2_scale"].partition_broadcast(P))
    k.load(sp, "f2_w", a["w"][:, :, :], dram["f2_w"])
    k.load(sp, "f2_bias", a["bias"][:, :], dram["f2_bias"].partition_broadcast(P))


def scale_weights(engine, a, c):
    w = a["w"][:, c, :].rearrange("p (o n) -> p o n", o=C)
    engine.tensor_tensor(w, w, a["scale"][:, c, :].unsqueeze(2).to_broadcast([P, C, P]), ALU.mult)\
      .then_inc(a["w_ready"], 1)


def scaled_linear(k, dram, a, f3):
    nc, ps = k.nc, k.ps
    OUT_BANK, OUT_BANKS, T_BANK = 0, 4, 6
    with ExitStack() as ctx:
        wt, bias = a["w"], a["bias"]
        xT = k.sb(ctx, "f2_xT", [P, 2, C, P])
        S = {n: k.sem("f2_" + n) for n in (
            "biased", "out_ready", "added")}
        block = ctx.enter_context(nc.Block())

        @block.gpsimd
        def _(pool):
            link = Link(pool, k.pool_own, k.pool_count)
            k.arrived(pool, "f2_bias")
            for b in range(NB):
                pool.wait_ge(k.xn_ready, NB * 5 + b + 1)
                nc.gpsimd.tensor_tensor(k.x[:, b, :], k.x[:, b, :], bias[:, :], ALU.add).then_inc(S["biased"], 1)
                if b >= 2:
                    k.row_rstd(pool, link, 6, b - 2)
            k.row_rstd(pool, link, 6, NB - 2)
            k.row_rstd(pool, link, 6, NB - 1)
            k.pool_count = link.n

        @block.tensor
        def _(pe):
            for i in range(NB + 1):
                if i < NB:
                    pe.wait_ge(k.xn_ready, NB * 5 + i + 1)
                    after_first(pe, k.xt_copied, NB * 4 + i - 1)
                    k.transpose4(T_BANK + i % 2, k.xn[:, i % 2, :]).then_inc(k.xt_ready, 1)
                if i >= 1:
                    b = i - 1
                    if b == 0:
                        pe.wait_ge(a["w_ready"], C)
                    pe.wait_ge(k.xt_copied, NB * 4 + b + 1)
                    after_first(pe, S["added"], b - OUT_BANKS + 1)
                    for c in range(C):
                        last = nc.tensor.matmul(ps[:, OUT_BANK + b % OUT_BANKS, :], xT[:, b % 2, c, :], wt[:, c, :],
                                                start=c == 0, stop=c == C - 1)
                    last.then_inc(S["out_ready"], 1)

        @block.scalar
        def _(act):
            for b in range(NB):
                act.wait_ge(k.xt_ready, NB * 4 + b + 1)
                after_first(act, S["out_ready"], b - 1)
                nc.scalar.copy(xT[:, b % 2, :, :].rearrange("p c t -> p (c t)"), ps[:, T_BANK + b % 2, :])\
                  .then_inc(k.xt_copied, 1)

        @block.vector
        def _(dve):
            link = Link(dve, k.dve_own, k.dve_count)

            def normalise(b):
                after_first(dve, k.xt_ready, NB * 4 + b - 1)
                k.normed(dve, 5, b, k.xn[:, b % 2, :]).then_inc(k.xn_ready, 1)

            normalise(0)
            normalise(1)
            for b in range(NB):
                if b + 2 < NB:
                    normalise(b + 2)
                if b >= NB - C:
                    unpack_weights(k, dve, link, f3, b - (NB - C))
                dve.wait_ge(S["out_ready"], b + 1)
                dve.wait_ge(S["biased"], b + 1)
                nc.vector.tensor_tensor(k.x[:, b, :], k.x[:, b, :], ps[:, OUT_BANK + b % OUT_BANKS, :], ALU.add)\
                  .then_inc(S["added"], 1)
                dve.wait_ge(S["added"], b + 1)
                k.row_stats(dve, link, b)
            k.dve_count = link.n


def token_attention_inputs(k, ctx):
    H, NK = 16, 32
    J = H * NK // P
    return {
        "sums": k.sb(ctx, "a3_sums", [1, NK + P]), "sums_k": k.sb(ctx, "a3_sums_k", [1, NB, NK]),
        "ck": k.sb(ctx, "a3_ck", [P, NB, NK]), "cv": k.sb(ctx, "a3_cv", [P, NB, P]),
        "made": k.sem("a3_made"), "made_copied": k.sem("a3_made_copied"),
        "w": k.sb(ctx, "a3_w", [P, 4, P]),
        "proj": k.sb(ctx, "a3_proj", [P, C, NK + P]),
        "bcol": k.sb(ctx, "a3_bcol", [P, 2]),
        "brow": k.sb(ctx, "a3_brow", [1, 2, P]),
        "ones": k.sb(ctx, "a3_ones", [P, 1]),
        "of_head": k.sb(ctx, "a3_of_head", [P, H]),
        "of_pair": k.sb(ctx, "a3_of_pair", [P, J, P])}


def load_token_attention(k, sp, dram, a):
    for name in ("proj", "ones", "w", "brow", "bcol", "of_head", "of_pair"):
        dst = a[name]
        k.load(sp, "a3_consts", dst[tuple(slice(None) for _ in dst.shape)], dram["a3_" + name])


def project_context(k, pe, a, n, bank):
    pe.wait_ge(*((a["made_copied"], n) if n else k.loaded["a3_consts"]))
    PROJ = a["proj"].shape[2]
    for c in range(C):
        left = k.ctxT[:, c, (n - 1) * P:n * P] if n else a["ones"][:, :]
        last = k.nc.tensor.matmul(k.ps[0:P if n else 1, bank, 0:PROJ], left, a["proj"][:, c, :],
                                  start=c == 0, stop=c == C - 1)
    last.then_inc(a["made"], 1)


def copy_projected(k, act, a, n, bank):
    NK, PROJ = a["ck"].shape[2], a["proj"].shape[2]
    act.wait_ge(a["made"], n + 1)
    if n:
        k.nc.scalar.copy(a["ck"][:, n - 1, :], k.ps[:, bank, 0:NK])
        last = k.nc.scalar.copy(a["cv"][:, n - 1, :], k.ps[:, bank, NK:PROJ])
    else:
        k.nc.scalar.copy(a["sums"][:, :], k.ps[0:1, bank, 0:PROJ])
        last = k.nc.scalar.copy(a["sums_k"][:, :, :], k.ps[0:1, bank, 0:NK].unsqueeze(1).to_broadcast([1, NB, NK]))
    last.then_inc(a["made_copied"], 1)


def token_attention(k, dram, a):
    nc, ps = k.nc, k.ps
    H, NK = 16, 32
    HJ = P // NK
    J = H // HJ
    T = D // P
    scale = 1.0 / float((P // H) ** 0.5)
    PROJ = NK + P
    Q_BANK, S_BANK, T_BANK, PV_BANK, OUT_BANK = 0, 1, 3, 5, 6
    with ExitStack() as ctx:
        w, bcol, brow, of_head, of_pair, sums, sums_k, ck, cv = (
            a[n] for n in ("w", "bcol", "brow", "of_head", "of_pair", "sums", "sums_k", "ck", "cv"))
        keys = k.sb(ctx, "a3_keys", [P, NB, NK])
        values = k.sb(ctx, "a3_values", [P, NB, P])
        spread_k = k.sb(ctx, "a3_spread_k", [P, 2, H, NK])
        spread_v = k.sb(ctx, "a3_spread_v", [P, 2, J, P])
        q = k.sb(ctx, "a3_q", [P, 2, D])
        top = k.sb(ctx, "a3_top", [P, 2, H])
        prob = k.sb(ctx, "a3_prob", [P, 3, H, NK])
        total = k.sb(ctx, "a3_total", [P, 2, H])
        inv = k.sb(ctx, "a3_inv", [P, 2, H])
        probT = k.sb(ctx, "a3_probT", [P, 2, J, D])
        o = k.sb(ctx, "a3_o", [P, 2, D])
        S = {n: k.sem("a3_" + n) for n in (
            "k_spread", "v_spread", "q_ready", "q_copied", "s_ready", "shifted",
            "exp_ready", "inv_ready", "prob_ready", "pt_ready", "pt_copied", "o_ready", "o_copied", "out_ready",
            "added")}
        block = ctx.enter_context(nc.Block())
        TILES = NB * T
        PROJECTED, KEYS, VALUES = NB + 1, NB + 2, NB + 3

        @block.gpsimd
        def _(pool):
            link = Link(pool, k.pool_own, k.pool_count)

            def spread(b):
                if b == 0:
                    pool.wait_ge(a["made_copied"], KEYS)
                    k.arrived(pool, "a3_consts")
                after_first(pool, S["s_ready"], T * (b - 1))
                nc.gpsimd.tensor_tensor(spread_k[:, b % 2, :, :], keys[:, b, :].unsqueeze(1).to_broadcast([P, H, NK]),
                                        of_head[:, :].unsqueeze(2).to_broadcast([P, H, NK]), ALU.mult)\
                  .then_inc(S["k_spread"], 1)
                if b == 0:
                    pool.wait_ge(a["made_copied"], VALUES + 1)
                    k.arrived(pool, "a3_consts")
                after_first(pool, S["o_ready"], b - 1)
                nc.gpsimd.tensor_tensor(spread_v[:, b % 2, :, :], values[:, b, :].unsqueeze(1).to_broadcast([P, J, P]),
                                        of_pair[:, :, :], ALU.mult).then_inc(S["v_spread"], 1)

            spread(0)
            for u in range(TILES):
                b, t = u // T, u % T
                pool.wait_ge(S["inv_ready"], u + 1)
                nc.gpsimd.tensor_tensor(prob[:, u % 3, :, :], prob[:, u % 3, :, :],
                                        inv[:, u % 2, :].unsqueeze(2).to_broadcast([P, H, NK]), ALU.mult)\
                    .then_inc(S["prob_ready"], 1)
                if t == 1 and b + 1 < NB:
                    spread(b + 1)
                if t == 2 and b >= 2:
                    k.row_rstd(pool, link, 7, b - 2)
            k.row_rstd(pool, link, 7, NB - 2)
            k.row_rstd(pool, link, 7, NB - 1)
            k.pool_count = link.n

        @block.tensor
        def _(pe):
            mm = nc.tensor.matmul
            k.arrived(pe, "a3_consts")
            k.arrived(pe, "a3_consts")
            def query(b):
                if b == 0:
                    k.arrived(pe, "a3_consts")
                pe.wait_ge(k.xn_ready, NB * 6 + b + 1)
                after_first(pe, S["q_copied"], b)
                mm(ps[:, Q_BANK, :], w[:, 0, :], k.xn[:, b % 2, :], start=True, stop=True).then_inc(S["q_ready"], 1)

            query(0)
            k.arrived(pe, "a3_consts")
            pe.wait_ge(a["made_copied"], PROJECTED)
            mm(ps[:, PV_BANK, 0:NB * NK], w[:, 1, :], ck[:, :, :].rearrange("p b k -> p (b k)"), start=True, stop=False)
            mm(ps[:, PV_BANK, 0:NB * NK], brow[:, 0, :], sums_k[:, :, :].rearrange("p b k -> p (b k)"),
               start=False, stop=True).then_inc(a["made"], 1)
            for half in range(2):
                for b in range(4 * half, 4 * half + 4):
                    out = ps[:, OUT_BANK + half, (b % 4) * P:(b % 4 + 1) * P]
                    mm(out, cv[:, b, :], w[:, 2, :], start=True, stop=False)
                    last = mm(out, sums[:, NK:PROJ], brow[:, 1, :], start=False, stop=True)
                last.then_inc(a["made"], 1)

            pe.wait_ge(a["made_copied"], KEYS)
            pe.wait_ge(a["made_copied"], VALUES + 1)

            def scores(u):
                b, t = u // T, u % T
                if t == 0:
                    pe.wait_ge(S["q_copied"], b + 1)
                    pe.wait_ge(S["k_spread"], b + 1)
                after_first(pe, S["shifted"], u - 1)
                mm(ps[:, S_BANK + u % 2, :], q[:, b % 2, t * P:(t + 1) * P],
                   spread_k[:, b % 2, :, :].rearrange("p h k -> p (h k)"), start=True, stop=True)\
                    .then_inc(S["s_ready"], 1)

            def transposes(u):
                pe.wait_ge(S["prob_ready"], u + 1)
                after_first(pe, S["pt_copied"], u - 1)
                k.transpose4(T_BANK + u % 2, prob[:, u % 3, :, :].rearrange("p h k -> p (h k)"))\
                    .then_inc(S["pt_ready"], 1)

            def attend(b):
                pe.wait_ge(S["pt_copied"], T * (b + 1))
                pe.wait_ge(S["v_spread"], b + 1)
                after_first(pe, S["o_copied"], b)
                for j in range(J):
                    last = mm(ps[:, PV_BANK, :], spread_v[:, b % 2, j, :], probT[:, b % 2, j, :],
                              start=j == 0, stop=j == J - 1)
                last.then_inc(S["o_ready"], 1)

            def output(b):
                pe.wait_ge(S["o_copied"], b + 1)
                after_first(pe, S["added"], b - 1)
                mm(ps[:, OUT_BANK + b % 2, :], w[:, 3, :], o[:, b % 2, :], start=True, stop=True)\
                    .then_inc(S["out_ready"], 1)

            scores(0)
            for u in range(TILES + 2 * T):
                b, t = u // T, u % T
                if u + 1 < TILES:
                    scores(u + 1)
                if 2 <= u < TILES + 2:
                    transposes(u - 2)
                if t == 1 and b + 1 < NB:
                    query(b + 1)
                if t == 2 and 1 <= b <= NB:
                    attend(b - 1)
                if t == 3 and 1 <= b <= NB:
                    output(b - 1)

        @block.scalar
        def _(act):
            def query(b):
                act.wait_ge(S["q_ready"], b + 1)
                after_first(act, S["s_ready"], T * (b - 1))
                nc.scalar.activation(q[:, b % 2, :], ps[:, Q_BANK, :], ACT.Identity, bias=bcol[:, 0:1])\
                  .then_inc(S["q_copied"], 1)

            k.arrived(act, "a3_consts")
            query(0)
            act.wait_ge(a["made"], KEYS)
            nc.scalar.copy(keys[:, :, :].rearrange("p b k -> p (b k)"), ps[:, PV_BANK, 0:NB * NK])\
              .then_inc(a["made_copied"], 1)
            for half in range(2):
                act.wait_ge(a["made"], VALUES + half)
                nc.scalar.copy(values[:, 4 * half:4 * half + 4, :].rearrange("p b d -> p (b d)"),
                               ps[:, OUT_BANK + half, :]).then_inc(a["made_copied"], 1)
            for u in range(TILES + 2 * T):
                b, t = u // T, u % T
                if u < TILES:
                    act.wait_ge(S["shifted"], u + 1)
                    nc.scalar.activation(prob[:, u % 3, :, :], prob[:, u % 3, :, :], ACT.Exp, scale=scale)\
                      .then_inc(S["exp_ready"], 1)
                if 2 <= u < TILES + 2:
                    n = u - 2
                    act.wait_ge(S["pt_ready"], n + 1)
                    after_first(act, S["o_ready"], n // T - 1)
                    nc.scalar.copy(probT[:, (n // T) % 2, :, (n % T) * P:(n % T + 1) * P],
                                   ps[:, T_BANK + n % 2, :].rearrange("p (j n) -> p j n", j=J))\
                      .then_inc(S["pt_copied"], 1)
                if t == 1 and b + 1 < NB:
                    query(b + 1)
                if t == 2 and 1 <= b <= NB:
                    act.wait_ge(S["o_ready"], b)
                    after_first(act, S["out_ready"], b - 2)
                    nc.scalar.copy(o[:, (b - 1) % 2, :], ps[:, PV_BANK, :]).then_inc(S["o_copied"], 1)

        @block.vector
        def _(dve):
            link = Link(dve, k.dve_own, k.dve_count)

            def normalise(b):
                after_first(dve, S["q_ready"], b - 1)
                k.normed(dve, 6, b, k.xn[:, b % 2, :]).then_inc(k.xn_ready, 1)

            def shift(u):
                s = ps[:, S_BANK + u % 2, :].rearrange("p (h k) -> p h k", h=H)
                dve.wait_ge(S["s_ready"], u + 1)
                link(nc.vector.tensor_reduce(top[:, u % 2, :], s, AX.X, ALU.max))
                after_first(dve, S["pt_ready"], u - 2)
                nc.vector.tensor_tensor(prob[:, u % 3, :, :], s,
                                        top[:, u % 2, :].unsqueeze(2).to_broadcast([P, H, NK]), ALU.subtract)\
                  .then_inc(S["shifted"], 1)

            def invert(u):
                dve.wait_ge(S["exp_ready"], u + 1)
                link(nc.vector.tensor_reduce(total[:, u % 2, :], prob[:, u % 3, :, :], AX.X, ALU.add))
                after_first(dve, S["prob_ready"], u - 1)
                nc.vector.reciprocal(inv[:, u % 2, :], total[:, u % 2, :]).then_inc(S["inv_ready"], 1)

            normalise(0)
            normalise(1)
            for u in range(TILES + 2 * T + 1):
                b, t = u // T, u % T
                if u < TILES:
                    shift(u)
                if 1 <= u < TILES + 1:
                    invert(u - 1)
                if t == 2 and b + 2 < NB:
                    normalise(b + 2)
                if t == 0 and 2 <= b <= NB + 1:
                    b -= 2
                    dve.wait_ge(S["out_ready"], b + 1)
                    nc.vector.scalar_tensor_tensor(k.x[:, b, :], ps[:, OUT_BANK + b % 2, :], bcol[:, 1:2],
                                                   k.x[:, b, :], ALU.add, ALU.add).then_inc(S["added"], 1)
                    dve.wait_ge(S["added"], b + 1)
                    k.row_stats(dve, link, b)
            k.dve_count = link.n


def packed_linear_inputs(k, ctx):
    NIB = 8
    WORDS = D // NIB
    return {
        "words": k.sb(ctx, "f3_words", [P, D], I32), "zwords": k.sb(ctx, "f3_zwords", [P, WORDS], I32),
        "scale": k.sb(ctx, "f3_scale", [P, D], F16), "bias": k.sb(ctx, "f3_bias", [P, D], F16),
        "q": k.sb(ctx, "f3_q", [P, C, D], I32), "z": k.sb(ctx, "f3_z", [P, WORDS, NIB], I32),
        "w": k.sb(ctx, "f3_w", [P, C, D], F16), "w_ready": k.sem("f3_w_ready")}


def load_packed_linear(k, sp, dram, a):
    for name in ("words", "zwords", "scale"):
        k.load(sp, "f3_consts", a[name][:, :], dram["f3_" + name])
    k.load(sp, "f3_consts", a["bias"][:, :], dram["f3_bias"].partition_broadcast(P))


def unpack_weights(k, dve, link, a, j):
    nc, NIB, BITS = k.nc, 8, 4
    WORDS = D // NIB

    def unpack(dst, src, s):
        nc.vector.tensor_scalar(dst, src, BITS * s, 15, ALU.logical_shift_right, ALU.bitwise_and)\
          .then_inc(k.dve_own, 1)
        link.n += 1

    if j == 0:
        k.arrived(dve, "f3_consts")
        for s in range(NIB):
            unpack(a["z"][:, :, s], a["zwords"][:, :], s)
        k.arrived(dve, "f3_consts")
    for h in range(2):
        rows = slice(h * WORDS, (h + 1) * WORDS)
        unpack(a["q"][rows, j, :], a["words"][rows, :], 2 * j + h)
    dve.wait_ge(k.dve_own, link.n)
    w = a["w"][:, j, :]
    link(nc.vector.tensor_tensor(w, a["q"][:, j, :], a["z"][:, :, :].rearrange("p w s -> p (w s)"), ALU.subtract))
    nc.vector.tensor_tensor(w, w, a["scale"][:, :], ALU.mult).then_inc(a["w_ready"], 1)


def packed_linear(k, dram, a, out):
    nc, ps = k.nc, k.ps
    NIB = 8
    OUT_BANK, OUT_BANKS, T_BANK = 0, 4, 6
    with ExitStack() as ctx:
        wt, bias = a["w"], a["bias"]
        xT = k.sb(ctx, "f3_xT", [P, 2, C, P], F16)
        y = k.sb(ctx, "f3_y", [P, 2, D], F16)
        yb = k.sb(ctx, "f3_yb", [P, 2, D], F16)
        S = {n: k.sem("f3_" + n) for n in (
            "out_ready", "out_copied",
            "added", "stored")}
        block = ctx.enter_context(nc.Block())

        @block.sync
        def _(sp):
            for b in range(NB):
                sp.wait_ge(S["added"], b + 1)
                sp.dma_start(out[b], k.x[:, b, :]).then_inc(S["stored"], 16)
            sp.wait_ge(S["stored"], 16 * NB)

        @block.tensor
        def _(pe):
            for i in range(NB + 1):
                if i < NB:
                    pe.wait_ge(k.xn_ready, NB * 7 + i + 1)
                    after_first(pe, k.xt_copied, NB * 5 + i - 1)
                    k.transpose4(T_BANK + i % 2, k.xn[:, i % 2, :]).then_inc(k.xt_ready, 1)
                if i >= 1:
                    b = i - 1
                    if b == 0:
                        pe.wait_ge(a["w_ready"], C)
                    pe.wait_ge(k.xt_copied, NB * 5 + b + 1)
                    after_first(pe, S["out_copied"], b - OUT_BANKS + 1)
                    for j in range(C):
                        last = nc.tensor.matmul(ps[:, OUT_BANK + b % OUT_BANKS, :], xT[:, b % 2, j, :], wt[:, j, :],
                                                start=j == 0, stop=j == C - 1)
                    last.then_inc(S["out_ready"], 1)

        @block.scalar
        def _(act):
            for i in range(NB + 1):
                if i < NB:
                    act.wait_ge(k.xt_ready, NB * 5 + i + 1)
                    after_first(act, S["out_ready"], i - 1)
                    nc.scalar.copy(xT[:, i % 2, :, :].rearrange("p c t -> p (c t)"), ps[:, T_BANK + i % 2, :])\
                      .then_inc(k.xt_copied, 1)
                if i >= 1:
                    b = i - 1
                    act.wait_ge(S["out_ready"], b + 1)
                    after_first(act, S["added"], b - 1)
                    nc.scalar.copy(y[:, b % 2, :], ps[:, OUT_BANK + b % OUT_BANKS, :]).then_inc(S["out_copied"], 1)

        @block.vector
        def _(dve):
            link = Link(dve, k.dve_own, k.dve_count)

            def normalise(b):
                after_first(dve, k.xt_ready, NB * 5 + b - 1)
                k.normed(dve, 7, b, k.xn[:, b % 2, :].rearrange("p (s r) -> p r s", s=NIB),
                         k.x[:, b, :].rearrange("p (r s) -> p r s", s=NIB)).then_inc(k.xn_ready, 1)

            normalise(0)
            normalise(1)
            for b in range(NB):
                if b + 2 < NB:
                    normalise(b + 2)
                dve.wait_ge(S["out_copied"], b + 1)
                after_first(dve, S["added"], b - 1)
                link(nc.vector.tensor_tensor(yb[:, b % 2, :], y[:, b % 2, :], bias[:, :], ALU.add))
                nc.vector.tensor_tensor(k.x[:, b, :], k.x[:, b, :], yb[:, b % 2, :], ALU.add)\
                  .then_inc(S["added"], 1)




def program(nc, dram, out):
    with ExitStack() as ctx:
        k = Core(nc, ctx, dram)
        cross_attention_over_heads(k, dram["x"], dram["ctxT"], {
            "Wq": dram["a0_wq"], "Wk": dram["a0_wk"], "Wv": dram["a0_wv"], "bqk": dram["a0_bqk"],
            "bv": dram["a0_bv"]})
        inputs = ctx.enter_context(ExitStack())
        a1 = grouped_attention_inputs(k, inputs)
        ranked_lora(k, {"AG": dram["f0_ag"], "gate_b": dram["f0_gate_b"], "W": dram["f0_w"], "B": dram["f0_bt"],
                        "b": dram["f0_b"]}, dram, a1)
        grouped_attention(k, dram, a1)
        inputs.close()
        table = k.sb(inputs, "a2_table", [P, 11, P])
        ahead = k.sb(inputs, "a2_ahead", [P, AHEAD, D])
        mixture_of_experts(k, dram, table, ahead)
        f2, a3, f3 = (inputs_of(k, inputs) for inputs_of in (
            scaled_linear_inputs, token_attention_inputs, packed_linear_inputs))
        autocorrelation(k, dram, table, ahead, f2, a3, f3)
        scaled_linear(k, dram, f2, f3)
        token_attention(k, dram, a3)
        packed_linear(k, dram, f3, out)
        inputs.close()


def rows128(a):
    return np.ascontiguousarray(a.reshape(-1, P, a.shape[-1]).transpose(1, 0, 2))


def columns(a):
    return np.ascontiguousarray(a.reshape(-1, P).T)


def rope_table(positions, dim, theta):
    freq = (1.0 / np.float32(theta) ** (np.arange(0, dim, 2, dtype=np.float32) / np.float32(dim))).astype(np.float32)
    angle = np.arange(positions, dtype=np.float32)[:, None] * freq
    c, s = np.cos(angle), np.sin(angle)
    return rows128(np.concatenate([c, c, s, -s], axis=1).astype(np.float32))


def shares(vision):
    text = np.arange(P) >= vision
    return np.stack([text / ((P - vision) * D), ~text / (vision * D)], axis=1).astype(np.float32)


def transform_tables():
    t, f = np.arange(P)[:, None], np.arange(P // 2)[None, :]
    angle = 2 * np.pi * t * f / P
    cos, sin, flip = np.cos(angle), np.sin(angle), np.cos(np.pi * t)
    to_q = np.concatenate([cos, flip, sin[:, 1:]], axis=1)
    to_k2 = np.concatenate([sin, 0 * flip, -cos[:, 1:]], axis=1)
    from_1 = np.concatenate([0.5 * cos[:, :1], cos[:, 1:], 0.5 * flip, cos[:, 1:]], axis=1).T * (2 / P)
    from_2 = np.concatenate([0 * flip, -sin[:, 1:], 0 * flip, -sin[:, 1:]], axis=1).T * (2 / P)
    odd = 2 * np.pi * t * (np.arange(P)[None, :] + 0.5) / (2 * P)
    wc, ws = np.cos(odd), np.sin(odd)
    vc, vs = wc.copy(), ws.copy()
    vc[-1], vs[-1] = -wc[:-1].sum(axis=0), -ws[:-1].sum(axis=0)
    last = np.zeros((P, P))
    last[-1] = 1.0
    tables = [to_q, to_k2, vc, vs, from_1, from_2, wc, ws, wc.T / P, ws.T / P, last]
    return np.stack(tables, axis=1).astype(np.float32)


def layouts(i):
    ctx = i["ctx_4096"].reshape(TOK, D)
    ctxT = rows128(ctx.T)
    channel = np.arange(P)
    row0 = np.zeros((P, P), np.float32)
    row0[0] = 1.0
    return {
        "ident": np.eye(P, dtype=np.float32),
        "x": i["x"],
        "ctxT": np.stack([ctxT[:, :, :512], ctxT[:, :, 512:]]),
        "a0_wq": rows128(i["L0_xattn_Wq"].T), "a0_wk": rows128(i["L0_xattn_Wk"].T),
        "a0_wv": rows128(i["L0_xattn_Wv"].T),
        "a0_bqk": np.stack([columns(i["L0_xattn_bq"]), columns(i["L0_xattn_bk"])], axis=1),
        "a0_bv": i["L0_xattn_bv"],
        "f0_w": rows128(i["L0_ffn_W"].T), "f0_b": i["L0_ffn_b"],
        "f0_ag": rows128(np.concatenate([i["L0_ffn_A"], i["L0_ffn_gate_w"]]).T),
        "f0_gate_b": i["L0_ffn_gate_b"], "f0_bt": i["L0_ffn_B"].T,
        "pos": i["pos_BxS2"].reshape(TOK), "mask": i["mask_BxSxS2_ik0"].transpose(1, 0, 2),
        "a1_iota": columns(np.arange(512, dtype=np.float32)), "a1_rope": rope_table(512, P, 10000.0),
        "a1_wq": i["L1_xattn_Wq"].reshape(C, P, 8, 4, P).transpose(2, 3, 1, 0, 4),
        "a1_wk": i["L1_xattn_Wk"].reshape(C, P, 8, P).transpose(2, 1, 0, 3),
        "a1_wv": i["L1_xattn_Wv"].reshape(C, P, 8, P).transpose(1, 2, 0, 3),
        "f1_gw": rows128(np.pad(i["L1_ffn_gate_w"][:D], ((0, 0), (0, 1)))), "f1_gw_ratio": i["L1_ffn_gate_w"][D], "f1_gb": i["L1_ffn_gate_b"],
        "f1_ones": np.ones((P, P), np.float32), "f1_row0": row0, "f1_share": shares(int(P * 0.3)),
        "f1_b1": i["L1_ffn_b1"].reshape(3, C, P).transpose(2, 0, 1), "f1_b2": i["L1_ffn_b2"],
        "f1_w1": i["L1_ffn_w1"].reshape(3, C, P, D).transpose(0, 2, 1, 3),
        "f1_w2": i["L1_ffn_w2"].reshape(3, C, P, D).transpose(0, 2, 1, 3),
        "ctx": i["ctx_4096"], "a2_table": transform_tables(),
        "f2_w": rows128(i["L2_ffn_weight"].T), "f2_scale": i["L2_ffn_weight_scale_inv"].T.reshape(C * C),
        "f2_bias": i["L2_ffn_bias"],
        "a3_w": np.stack([i[f"L3_xattn_W{n}"].T for n in "qkvm"], axis=1),
        "a3_proj": rows128(np.concatenate([i["L3_xattn_proj_k"]] + [i["L3_xattn_proj_v"]] * 4, axis=1)),
        "a3_bcol": np.stack([i["L3_xattn_bq"], i["L3_xattn_bm"]], axis=1),
        "a3_brow": np.stack([i["L3_xattn_bk"], i["L3_xattn_bv"]])[None],
        "a3_ones": np.ones((P, 1), np.float32),
        "a3_of_head": (channel[:, None] % 16 == np.arange(16)).astype(np.float32),
        "a3_of_pair": (4 * np.arange(4)[None, :, None] + channel[:, None, None] // 32
                       == channel[None, None, :] % 16).astype(np.float32),
        "f3_words": np.tile(i["L3_ffn_qweight"], (2, 1)),
        "f3_zwords": np.tile(np.repeat(i["L3_ffn_qzeros"], 16, axis=0), (2, 1)),
        "f3_scale": np.tile(np.repeat(i["L3_ffn_scales"], 16, axis=0), (2, 1)), "f3_bias": i["L3_ffn_bias"],
        "a1_wo": i["L1_xattn_Wo"].reshape(8, 4, P, D).transpose(0, 2, 1, 3),
    }


def kernel(**inputs):
    import concourse.bacc as bacc
    from concourse.bass_utils import run_bass_kernel_spmd

    nc = bacc.Bacc("TRN2", target_bir_lowering=False, num_devices=1)
    arrays, dram = {}, {}
    for name, a in layouts({n: np.asarray(a) for n, a in inputs.items()}).items():
        a = np.ascontiguousarray(a)
        arrays[f"in_{name}"] = a
        dram[name] = nc.dram_tensor(f"in_{name}", a.shape, mybir.dt.from_np(a.dtype), kind="ExternalInput").ap()
    out = nc.dram_tensor("out_x", (NB, P, D), F32, kind="ExternalOutput").ap()
    program(nc, dram, out)
    r = run_bass_kernel_spmd(nc, [arrays], core_ids=[0])
    return r.results[0]["out_x"]
```
